# Optimizing a Trainium2 kernel written in Bass

```python
import numpy as np
import jax
import jax.numpy as jnp

def _softmax(x, axis=-1):
    return jax.nn.softmax(x, axis=axis)

def _gelu(x):
    return jax.nn.gelu(x, approximate=True)

def _silu(x):
    return jax.nn.silu(x)

def _sigmoid(x):
    return jax.nn.sigmoid(x)

def _layernorm(x, axis=-1, eps=1e-05):
    m = jnp.mean(x, axis=axis, keepdims=True)
    v = jnp.var(x, axis=axis, keepdims=True)
    return (x - m) / jnp.sqrt(v + eps)

def _scatter_add(tgt, idx, src, axis=0):
    return tgt.at[idx].add(src)

def _segment_sum(src, seg, n):
    return jax.ops.segment_sum(src, seg, n)
kernel_name = 'mk_gnn_resnorm_d2_gnn_r8_a79f28'

def setup_inputs(seed: int=0):
    np.random.seed(seed)
    _w = jnp.asarray

    def _rec_inputs():
        import jax
        import jax.numpy as jnp
        _gk = jax.random.key(seed)
        x = -0.000202 + 1 * jax.random.normal(jax.random.fold_in(_gk, 1), (12500, 64), jnp.float32)
        src = jax.random.randint(jax.random.fold_in(_gk, 2), (200000,), 0, 12500, jnp.int32)
        dst = jnp.minimum((12500 * jax.random.uniform(jax.random.fold_in(_gk, 3), (200000,)) ** 2.0).astype(jnp.int32), 99999)
        _o = jnp.argsort(dst, stable=True)
        src = src[_o]
        dst = dst[_o]
        edge_attr_16 = 0.000196303 + 1.00016 * jax.random.normal(jax.random.fold_in(_gk, 12), (200000, 16), jnp.float32)
        edge_attr_32 = -9.77346e-05 + 0.999888 * jax.random.normal(jax.random.fold_in(_gk, 13), (200000, 32), jnp.float32)
        return (x, src, dst, edge_attr_16, edge_attr_32)
    x, src, dst, edge_attr_16, edge_attr_32 = _rec_inputs()

    def _L0_gnn_setup():
        import jax, jax.numpy as jnp
        import numpy as np
        N, E = (12500, 200000)
        IN_DIM, OUT_DIM, EDGE_DIM, H = (64, 64, 16, 4)
        HD = OUT_DIM // H
        NEG_SLOPE = 0.2
        EPS_SOFTMAX = 1e-08
        EPS_LN = 1e-05
        key = jax.random.key(seed)
        ks = jax.random.split(key, 8)
        return {'x': jax.random.normal(ks[0], (N, IN_DIM), jnp.float32), 'edge_index': jax.random.randint(ks[1], (2, E), 0, N, jnp.int64 if jax.config.jax_enable_x64 else jnp.int32), 'edge_attr': jax.random.normal(ks[2], (E, EDGE_DIM), jnp.float32), 'W_node': jax.random.normal(ks[3], (IN_DIM, OUT_DIM), jnp.float32) / np.sqrt(IN_DIM), 'W_edge': jax.random.normal(ks[4], (EDGE_DIM, H), jnp.float32) / np.sqrt(EDGE_DIM), 'attn_src': jax.random.normal(ks[5], (H, HD), jnp.float32), 'attn_dst': jax.random.normal(ks[6], (H, HD), jnp.float32), 'ln_gamma': jnp.ones((OUT_DIM,), jnp.float32), 'ln_beta': jnp.zeros((OUT_DIM,), jnp.float32)}
    _L0_gnn_all = _L0_gnn_setup()
    _L0_gnn_in = {k: v for k, v in _L0_gnn_all.items() if k in ('W_node', 'W_edge', 'attn_src', 'attn_dst', 'ln_gamma', 'ln_beta')}
    del _L0_gnn_all

    def _L1_gnn_setup():
        import jax, jax.numpy as jnp
        import numpy as np
        N_NODES = 12500
        N_EDGES = 200000
        NODE_F = 64
        EDGE_F = 32
        OUT_F = 64
        HIDDEN = 2 * OUT_F
        IN_F = 2 * NODE_F + EDGE_F
        key = jax.random.key(seed)
        ks = jax.random.split(key, 8)
        nodes = jax.random.normal(ks[0], (N_NODES, NODE_F), dtype=jnp.float32)
        edges = jax.random.normal(ks[1], (N_EDGES, EDGE_F), dtype=jnp.float32)
        senders = jax.random.randint(ks[2], (N_EDGES,), 0, N_NODES, dtype=jnp.int32)
        receivers = jax.random.randint(ks[3], (N_EDGES,), 0, N_NODES, dtype=jnp.int32)
        W1 = jax.random.normal(ks[4], (IN_F, HIDDEN), dtype=jnp.float32) / np.sqrt(IN_F)
        b1 = jnp.zeros((HIDDEN,), dtype=jnp.float32)
        W2 = jax.random.normal(ks[5], (HIDDEN, OUT_F), dtype=jnp.float32) / np.sqrt(HIDDEN)
        b2 = jnp.zeros((OUT_F,), dtype=jnp.float32)
        Wn = jax.random.normal(ks[6], (NODE_F, OUT_F), dtype=jnp.float32) / np.sqrt(NODE_F)
        bn = jnp.zeros((OUT_F,), dtype=jnp.float32)
        return {'nodes': nodes, 'edges': edges, 'senders': senders, 'receivers': receivers, 'W1': W1, 'b1': b1, 'W2': W2, 'b2': b2, 'Wn': Wn, 'bn': bn}
    _L1_gnn_all = _L1_gnn_setup()
    _L1_gnn_in = {k: v for k, v in _L1_gnn_all.items() if k in ('W1', 'b1', 'W2', 'b2', 'Wn', 'bn')}
    del _L1_gnn_all
    return {'x': x, 'src': src, 'dst': dst, 'edge_attr_16': edge_attr_16, 'edge_attr_32': edge_attr_32, 'L0_gnn_W_node': _L0_gnn_in['W_node'], 'L0_gnn_W_edge': _L0_gnn_in['W_edge'], 'L0_gnn_attn_src': _L0_gnn_in['attn_src'], 'L0_gnn_attn_dst': _L0_gnn_in['attn_dst'], 'L0_gnn_ln_gamma': _L0_gnn_in['ln_gamma'], 'L0_gnn_ln_beta': _L0_gnn_in['ln_beta'], 'L1_gnn_W1': _L1_gnn_in['W1'], 'L1_gnn_b1': _L1_gnn_in['b1'], 'L1_gnn_W2': _L1_gnn_in['W2'], 'L1_gnn_b2': _L1_gnn_in['b2'], 'L1_gnn_Wn': _L1_gnn_in['Wn'], 'L1_gnn_bn': _L1_gnn_in['bn']}

def reference(x, src, dst, edge_attr_16, edge_attr_32, L0_gnn_W_node, L0_gnn_W_edge, L0_gnn_attn_src, L0_gnn_attn_dst, L0_gnn_ln_gamma, L0_gnn_ln_beta, L1_gnn_W1, L1_gnn_b1, L1_gnn_W2, L1_gnn_b2, L1_gnn_Wn, L1_gnn_bn):
    import jax
    import jax.numpy as jnp

    def _L0_gnn_ref(x, edge_index, edge_attr, W_node, W_edge, attn_src, attn_dst, ln_gamma, ln_beta):
        import jax, jax.numpy as jnp
        import numpy as np
        N, E = (12500, 200000)
        IN_DIM, OUT_DIM, EDGE_DIM, H = (64, 64, 16, 4)
        HD = OUT_DIM // H
        NEG_SLOPE = 0.2
        EPS_SOFTMAX = 1e-08
        EPS_LN = 1e-05
        n = x.shape[0]
        src, dst = (edge_index[0], edge_index[1])
        h = (x @ W_node).reshape(n, H, HD)
        a_src_node = jnp.einsum('nhd,hd->nh', h, attn_src)
        a_dst_node = jnp.einsum('nhd,hd->nh', h, attn_dst)
        e_score = edge_attr @ W_edge
        attn = a_src_node[src] + a_dst_node[dst] + e_score
        attn = jnp.where(attn >= 0, attn, NEG_SLOPE * attn)
        attn_max = jnp.zeros((n, H), attn.dtype).at[dst].max(attn)
        attn = jnp.exp(attn - attn_max[dst])
        attn_sum = jnp.zeros((n, H), attn.dtype).at[dst].add(attn)
        attn = attn / (attn_sum[dst] + EPS_SOFTMAX)
        msg = h[src] * attn[:, :, None]
        out = jnp.zeros((n, H, HD), h.dtype).at[dst].add(msg).reshape(n, OUT_DIM)
        y = out + h.reshape(n, OUT_DIM)
        mu = jnp.mean(y, axis=-1, keepdims=True)
        var = jnp.mean((y - mu) ** 2, axis=-1, keepdims=True)
        return (y - mu) * jax.lax.rsqrt(var + EPS_LN) * ln_gamma + ln_beta

    def _L1_gnn_ref(nodes, edges, senders, receivers, W1, b1, W2, b2, Wn, bn):
        import jax, jax.numpy as jnp
        import numpy as np
        N_NODES = 12500
        N_EDGES = 200000
        NODE_F = 64
        EDGE_F = 32
        OUT_F = 64
        HIDDEN = 2 * OUT_F
        IN_F = 2 * NODE_F + EDGE_F
        n_nodes = nodes.shape[0]
        sender_features = nodes[senders]
        receiver_features = nodes[receivers]
        concat = jnp.concatenate([sender_features, receiver_features, edges], axis=-1)
        h = jax.nn.relu(concat @ W1 + b1)
        messages = h @ W2 + b2
        aggregated = jax.ops.segment_sum(messages, receivers, num_segments=n_nodes)
        degree = jax.ops.segment_sum(jnp.ones((receivers.shape[0],), dtype=messages.dtype), receivers, num_segments=n_nodes)
        aggregated = aggregated / jnp.maximum(degree, 1.0)[:, None]
        new_nodes = aggregated + (nodes @ Wn + bn)
        return new_nodes
    edge_index = jnp.stack([src, dst])
    x = _layernorm(x + _L0_gnn_ref(x, edge_index, edge_attr_16, L0_gnn_W_node, L0_gnn_W_edge, L0_gnn_attn_src, L0_gnn_attn_dst, L0_gnn_ln_gamma, L0_gnn_ln_beta), axis=-1)
    x = _layernorm(x + _L1_gnn_ref(x, edge_attr_32, src, dst, L1_gnn_W1, L1_gnn_b1, L1_gnn_W2, L1_gnn_b2, L1_gnn_Wn, L1_gnn_bn), axis=-1)
    return x

_drawn_inputs = setup_inputs


def setup_inputs(seed=0):
    import zlib

    import numpy as np

    out = dict(_drawn_inputs(seed))
    spreads = {'L0_gnn_ln_gamma': (1.0, 0.2),
     'L0_gnn_ln_beta': (0.0, 0.1),
     'L1_gnn_b1': (0.0, 0.1),
     'L1_gnn_b2': (0.0, 0.1),
     'L1_gnn_bn': (0.0, 0.1)}
    factors = {}
    for name, (base, spread) in spreads.items():
        noise = np.random.default_rng([zlib.crc32(name.encode()), seed]).standard_normal(out[name].shape)
        drawn = base * np.exp(spread * noise) if base else spread * noise
        out[name] = jnp.asarray(drawn.astype(out[name].dtype))
    for name, factor in factors.items():
        out[name] = (out[name] * factor).astype(out[name].dtype)
    return out
```

```python
from contextlib import ExitStack

import concourse.bass as bass
from concourse import mybir

F32 = mybir.dt.float32
BF16 = mybir.dt.bfloat16
I32 = mybir.dt.int32
ALU = mybir.AluOpType
ACT = mybir.ActivationFunctionType
AX = mybir.AxisListType

P = 128
N, E = 12500, 200000
D, H, HD = 64, 4, 16
F16, F32E = 16, 32
HID = 128
RECV = HID + D
SLOPE, EPS_SOFTMAX, EPS_LN = 0.2, 1e-8, 1e-5

LANE = 1568
NE = P * LANE
NB = 100
NP = P * NB
NC = 10
NPC = NC // 2
NK = NB // NC
REAL_Q = N // NB

ROW = D + 2 * H
ZCOL, MCOL = D, D + H
C0 = 32
K0 = LANE // C0
RING0 = 4
G0E = P // F16
C1 = 8
K1 = LANE // C1
RING1 = 4
G1E = P // F32E
WEIGHT_DMAS_0, WEIGHT_DMAS_1 = 4 + 2 * H + P // F16, P // F32E + 12
ZERO_COLS = 2048
NOWHERE = 1 << 20


def build(nc, x, xT2, src, dst, e16g, e32g, W_node, W_nodeT, W_edge, attn_src, attn_dst, gamma, beta,
          W1, b1, W2, b2, Wn, bn, out):
    table0 = nc.dram_tensor("table0", (NP, ROW), F32).ap()
    dst_term = nc.dram_tensor("dst_term", (NE, H), F32).ap()
    rows0 = nc.dram_tensor("rows0", (NE, ROW), F32).ap()
    table1s = nc.dram_tensor("table1s", (NP, HID), F32).ap()
    table1d = nc.dram_tensor("table1d", (NP, HID), F32).ap()
    recv_term = nc.dram_tensor("recv_term", (NE, HID), F32).ap()
    rows1 = nc.dram_tensor("rows1", (NE, HID), F32).ap()

    table0_q = table0.rearrange("(q b) c -> q b c", b=NB)
    table1s_q = table1s.rearrange("(q b) c -> q b c", b=NB)
    table1d_q = table1d.rearrange("(q b) c -> q b c", b=NB)
    dst_term_p = dst_term.rearrange("(p t) c -> p (t c)", t=LANE)
    recv_flat = recv_term.rearrange("(p t) c -> p (t c)", t=LANE)
    rows0_p = rows0.rearrange("(p t) c -> p t c", t=LANE)
    rows1_p = rows1.rearrange("(p t) c -> p t c", t=LANE)
    recv_p = recv_term.rearrange("(p t) c -> p t c", t=LANE)
    x_q = x.rearrange("(q b) c -> q b c", b=NB)
    out_q = out.rearrange("(q b) c -> q b c", b=NB)

    with ExitStack() as ctx:
        ctx.enter_context(nc.allow_non_contiguous_dma(reason="one column of the small tables: a few elements"))

        def sb(name, shape, dt=F32):
            return ctx.enter_context(nc.sbuf_tensor(name, shape, dt))

        def sem(name):
            return ctx.enter_context(nc.semaphore(name))

        ps = ctx.enter_context(nc.psum_tensor("ps", [P, 8, 512], F32))

        src_idx = sb("src_idx", [P, LANE], I32)
        same = sb("same", [P, LANE])
        node_wide = sb("node_wide", [P, NB * D])
        iota_q = sb("iota_q", [P, NC, P])
        below = sb("below", [P, NC, P])
        carry_sel = sb("carry_sel", [P, NC, P])
        zeros = sb("zeros", [P, ZERO_COLS])
        ident = sb("ident", [P, P])
        ones = sb("ones", [P, P])
        same_seg = sb("same_seg", [P, P])
        same_segT = sb("same_segT", [P, P])
        earlier = sb("earlier", [P, P])
        w0 = sb("w0", [P, 2 * ROW])
        acat = sb("acat", [D, 2 * H])
        wnT2 = sb("wnT2", [D, 2 * D])
        we_bd = sb("we_bd", [P, G0E * H])
        w1e_bd = sb("w1e_bd", [P, G1E * HID])
        w1n = sb("w1n", [P, 2, 2 * HID + D])
        w2 = sb("w2", [HID, D])
        b1_bc = sb("b1_bc", [P, HID])
        row_bc = sb("row_bc", [P, 4, D])
        a_dst = sb("a_dst", [P, NB, H])
        node_id = sb("node_id", [P, NB])
        node_half = sb("node_half", [P, NB])
        lane_of = sb("lane_of", [P, NB])
        upto = sb("upto", [P, NB + 1])
        degree = sb("degree", [P, NB])
        has = sb("has", [P, NB])
        inv_deg = sb("inv_deg", [P, NB])
        tmp_nb = sb("tmp_nb", [P, NB])
        start_idx = sb("start_idx", [P, NB], I32)
        end_idx = sb("end_idx", [P, NB + 2 * NC], I32)
        ends_i = sb("ends_i", [P, 4], I32)
        ends = sb("ends", [P, 5])
        k10 = sb("k10", [P, NK + 2])
        firsts = sb("firsts", [P, NK + 2])
        nexts = sb("nexts", [P, NK + 2])
        lows = sb("lows", [P, NK + 2])
        eps = sb("eps", [P, 1])
        scrap = sb("scrap", [P, 64])
        carry0 = sb("carry0", [P, ROW])
        carry1 = sb("carry1", [P, D])
        lane_rows = sb("lane_rows", [P, ROW])
        ix = [sb(f"ix{s}", [P, C0], I32) for s in range(4)]
        end_ix = [sb(f"end_ix{r}", [P, NC], I32) for r in range(2)]
        start_ix = [sb(f"start_ix{r}", [P, NC], I32) for r in range(2)]

        edge_arena = sb("edge_arena", [P, (RING0 + 2) * C0 * ROW])
        edge_terms = [sb(f"edge_terms{r}", [P, 4, P]) for r in range(4)]

        def part(arena, at, *shape):
            size = 1
            for s in shape:
                size *= s
            flat = arena[:, at:at + size]
            if len(shape) == 1:
                return flat
            if len(shape) == 2:
                return flat.rearrange("p (a b) -> p a b", b=shape[1])
            return flat.rearrange("p (a b c) -> p a b c", b=shape[1], c=shape[2])

        G0 = [part(edge_arena, s * C0 * ROW, C0, ROW) for s in range(RING0)]
        R0 = [part(edge_arena, (RING0 + r) * C0 * ROW, C0, ROW) for r in range(2)]
        W1R = C1 * HID
        G1 = [part(edge_arena, s * W1R, C1, HID) for s in range(RING1)]
        X1 = [part(edge_arena, (RING1 + s) * W1R, C1, HID) for s in range(RING1)]
        H1 = [part(edge_arena, (2 * RING1 + s) * W1R, C1, HID) for s in range(RING1)]
        score = sb("score", [P, C0, H])
        expo = sb("expo", [P, C0, 2 * H])
        wq = sb("wq", [P, C0, 2 * H])

        node_arena = sb("node_arena", [P, 12800])
        dst_i = part(node_arena, 0, LANE).bitcast(I32)
        LW = LANE + 2
        dst_hi = part(node_arena, LANE, LW // 2).bitcast(BF16)
        dst_lo = part(node_arena, LANE + LW // 2, LW // 2).bitcast(BF16)
        split_i = part(node_arena, LANE + LW, LANE).bitcast(I32)
        junk_v = part(node_arena, 2 * LANE + LW, LANE // 2).bitcast(BF16)
        junk_a = part(node_arena, 2 * LANE + LW + LANE // 2, LANE // 2).bitcast(BF16)
        at = 3 * LANE + LW
        onehot = [part(node_arena, at + r * NC * P // 2, NC * P // 2).bitcast(BF16).rearrange(
            "p (b q) -> p b q", q=P) for r in range(2)]
        at += NC * P
        tab0 = [part(node_arena, at + r * 6 * ROW, 6, ROW) for r in range(2)]
        RG0 = [part(node_arena, r * NC * ROW, NC, ROW) for r in range(2)]
        xc = [part(node_arena, 1440 + r * NC * D, NC, D) for r in range(2)]
        hc = [part(node_arena, 2720 + r * NC * ROW, NC, ROW) for r in range(2)]
        PSs = [part(node_arena, 4160 + r * NC * HID, NC, HID) for r in range(2)]
        PDs = [part(node_arena, 6720 + r * NC * HID, NC, HID) for r in range(2)]
        ya = part(node_arena, 9280, NC, D)
        yb = part(node_arena, 9920, NC, D)
        sq = part(node_arena, 10560, NC, D)
        x1T = [part(node_arena, 11200 + j * P, P) for j in range(2)]
        f8 = part(node_arena, 11456, NC, 2 * H)
        e8 = part(node_arena, 11536, NC, 2 * H)
        cc = part(node_arena, 11736, NC, ROW)
        z1 = part(node_arena, 11616, NC, H)
        z2 = part(node_arena, 11656, NC, H)
        mu = part(node_arena, 11696, NC)
        var = part(node_arena, 11706, NC)
        rstd = part(node_arena, 11716, NC)
        big_a = part(node_arena, 4160, H, P)
        big_b = part(node_arena, 4672, H, P)
        big_c = part(node_arena, 5184, H, P)
        mc = part(node_arena, 5696, H)
        RG1 = [part(node_arena, r * NC * HID, NC, HID) for r in range(2)]
        rgT = [part(node_arena, 2560 + j * P, P) for j in range(2)]
        fin = [part(node_arena, 2816 + r * NC * D, NC, D) for r in range(2)]

        weights_in, weights1_in = sem("weights_in"), sem("weights1_in")
        xT_in, dst_in, nexts_in, src_in, wraps_in = sem("xT_in"), sem("dst_in"), sem("nexts_in"), sem("src_in"), sem("wraps_in")
        cleared, consts = sem("cleared"), sem("consts")
        fused_mm, fused_in = sem("fused_mm"), sem("fused_in")
        tab_mm, tab_out, tab_stored = sem("tab_mm"), sem("tab_out"), sem("tab_stored")
        tab_st = [sem("tab_st0"), sem("tab_st1")]
        ends_ready, dvc = sem("ends_ready"), sem("dvc")
        onehot_ready = sem("onehot_ready")
        row_ready = [sem("row_ready0"), sem("row_ready1")]
        row_free = [sem("row_free0"), sem("row_free1")]
        upto_ready, nodes_ready = sem("upto_ready"), sem("nodes_ready")
        dv = sem("dv")
        seg_mm = sem("seg_mm")
        terms_zeroed, recv_zeroed = sem("terms_zeroed"), sem("recv_zeroed")
        terms_scattered, terms_in, lane_terms_in, terms_ready = sem("terms_scattered"), sem("terms_in"), sem("lane_terms_in"), sem("terms_ready")
        ix0_ready = sem("ix0_ready")
        gathered0 = [sem(f"gathered0_{s}") for s in range(RING0)]
        e16_in = [sem("e16_in0"), sem("e16_in1")]
        edge_mm, edge_mm_free = sem("edge_mm"), sem("edge_mm_free")
        dv0 = sem("dv0")
        expo_ready, wq_ready = sem("expo_ready"), sem("wq_ready")
        rows0_ready = sem("rows0_ready")
        rows0_stored = [sem("rows0_stored0"), sem("rows0_stored1")]
        carry_mm, carry_exp, carry_ready = sem("carry_mm"), sem("carry_exp"), sem("carry_ready")
        end_ix_ready, rg0_in = sem("end_ix_ready"), [sem("rg0_in0"), sem("rg0_in1")]
        xh_in, node0_used = [sem("xh_in0"), sem("xh_in1")], sem("node0_used")
        sel_ready, carried, x_used = sem("sel_ready"), sem("carried"), sem("carried_used")
        cc_ready, cc_free = sem("cc_ready"), sem("cc_free")
        dvn = sem("dvn")
        e8_ready, f8_ready = sem("e8_ready"), sem("f8_ready")
        dev_ready, sq_ready, var_ready, std_ready = sem("dev_ready"), sem("sq_ready"), sem("var_ready"), sem("std_ready")
        x1_ready, x1T_mm, x1T_ready, send_mm, recv_mm = sem("x1_ready"), sem("x1T_mm"), sem("x1T_ready"), sem("send_mm"), sem("recv_mm")
        pss_out, pds_out = sem("pss_out"), sem("pds_out")
        start_ix_ready = sem("start_ix_ready")
        pss_stored, pds_stored, pds_scattered = [sem("pss_st0"), sem("pss_st1")], [sem("pds_st0"), sem("pds_st1")], [sem("pds_sc0"), sem("pds_sc1")]
        lane_recv_in = sem("lane_recv_in")
        lead_in = sem("lead_in")
        ix1_ready = sem("ix1_ready")
        gathered1 = [sem(f"gathered1_{s}") for s in range(RING1)]
        recv_in = [sem(f"recv_in{s}") for s in range(RING1)]
        e32_in = [sem(f"e32_in{s}") for s in range(RING1)]
        edge1_mm, pre_ready, relu_done = sem("edge1_mm"), sem("pre_ready"), sem("relu_done")
        dv1, rows1_ready, recv_used = sem("dv1"), sem("rows1_ready"), sem("recv_used")
        rows1_stored = [sem(f"rows1_stored{s}") for s in range(RING1)]
        carry1_mm, carry1_cp = sem("carry1_mm"), sem("carry1_cp")
        rg1_in, rg1_used, end1_ix_ready = [sem("rg1_in0"), sem("rg1_in1")], sem("rg1_used"), sem("end1_ix_ready")
        sel1_ready, rgT_mm, rgT_ready, agg_mm, agg_used = sem("sel1_ready"), sem("rgT_mm"), sem("rgT_ready"), sem("agg_mm"), sem("agg_used")
        dvf, dev1_ready, sq1_ready, var1_ready, std1_ready, fin_ready = sem("dvf"), sem("dev1_ready"), sem("sq1_ready"), sem("var1_ready"), sem("std1_ready"), sem("fin_ready")
        fin_stored = [sem("fin_stored0"), sem("fin_stored1")]

        block = ctx.enter_context(nc.Block())

        PAIRS = NB // 2
        TABG = [min(3, PAIRS - 3 * g) for g in range((PAIRS + 2) // 3)]
        COLS = [(c, min(512, LANE + 1 - c)) for c in range(0, LANE + 1, 512)]

        @block.sync
        def _(sp):
            sp.wait_ge(cleared, 1)
            small = [(wnT2[:, 0:D], W_nodeT), (wnT2[:, D:2 * D], W_nodeT),
                     (w0[0:D, 0:D], W_node), (w0[D:2 * D, ROW:ROW + D], W_node)]
            small += [(acat[HD * h:HD * h + HD, h:h + 1], attn_src[h, :].rearrange("(d a) -> d a", a=1)) for h in range(H)]
            small += [(acat[HD * h:HD * h + HD, H + h:H + h + 1], attn_dst[h, :].rearrange("(d a) -> d a", a=1)) for h in range(H)]
            small += [(we_bd[F16 * j:F16 * j + F16, H * j:H * j + H], W_edge) for j in range(G0E)]
            for a, b in small:
                sp.dma_start(a, b).then_inc(weights_in, 16)
            assert len(small) == WEIGHT_DMAS_0
            for i, s in enumerate([*rows0_stored, *pss_stored, *pds_stored, *fin_stored, *rows1_stored]):
                sp.dma_start(scrap[:, 4 * i:4 * i + 4], zeros[:, 0:4]).then_inc(s, 16)
            sp.dma_start(node_wide[:, :], xT2).then_inc(xT_in, 16)
            sp.dma_start(dst_i, dst).then_inc(dst_in, 16)
            sp.dma_start(ends_i[0:P - 1, 1:2], dst[1:P, 0:1]).then_inc(nexts_in, 16)
            sp.dma_start(ends_i[1:P, 2:3], dst[0:P - 1, LANE - 1:LANE]).then_inc(nexts_in, 16)
            sp.dma_start(src_idx[:, :], src).then_inc(src_in, 16)
            for k in range(3):
                w = min(ZERO_COLS, LANE * H - k * ZERO_COLS)
                sp.dma_start(dst_term_p[:, k * ZERO_COLS:k * ZERO_COLS + w], zeros[:, 0:w]).then_inc(terms_zeroed, 16)
            sp.dma_start(dst_term_p[:, 3 * ZERO_COLS:LANE * H], zeros[:, 0:LANE * H - 3 * ZERO_COLS]).then_inc(terms_zeroed, 16)
            for g, m in enumerate(TABG):
                sp.wait_ge(tab_out, g + 1)
                sp.dma_start(table0_q[:, 6 * g:6 * g + 2 * m, :], tab0[g % 2][:, 0:2 * m, :]).then_inc(tab_st[g % 2], 16)
            later = [(w1e_bd[F32E * j:F32E * j + F32E, HID * j:HID * j + HID], W1[2 * D:2 * D + F32E, :]) for j in range(G1E)]
            for j in range(2):
                later += [(w1n[D * j:D * j + D, j, 0:HID], W1[0:D, :]), (w1n[D * j:D * j + D, j, HID:2 * HID], W1[D:2 * D, :]),
                          (w1n[D * j:D * j + D, j, 2 * HID:2 * HID + D], Wn)]
            later += [(w2[:, :], W2), (b1_bc[:, :], b1.partition_broadcast(P))]
            later += [(row_bc[:, i, :], v.partition_broadcast(P)) for i, v in enumerate((gamma, beta, b2, bn))]
            for a, b in later:
                sp.dma_start(a, b).then_inc(weights1_in, 16)
            assert len(later) == WEIGHT_DMAS_1
            for c in range(2):
                sp.dma_start(edge_terms[c][:, :, :], e16g[:, 4 * c:4 * c + 4, :]).then_inc(e16_in[c], 16)
            sp.wait_ge(upto_ready, 1)
            sp.dma_start(upto[1:P, 0:1], upto[0:P - 1, NB:NB + 1]).then_inc(wraps_in, 16)
            sp.wait_ge(terms_scattered, 16 * NB)
            sp.dma_start(node_wide[:, 0:LANE * H], dst_term_p).then_inc(terms_in, 16)

            def chunk0(c, slot, it):
                par = slot % 2
                for z in range(2):
                    sp.dma_start(recv_flat[:, bass.ds(c * (2 * ZERO_COLS) + z * ZERO_COLS, ZERO_COLS)],
                                 zeros[:, :]).then_inc(recv_zeroed, 16)
                sp.wait_ge(edge_mm, c + 1)
                if not (isinstance(c, int) and c + 2 >= K0):
                    sp.dma_start(edge_terms[par][:, :, :], e16g[:, bass.ds(c * 4 + 8, 4), :]).then_inc(e16_in[par], 16)
                sp.wait_ge(rows0_ready, c + 2)
                sp.dma_start(rows0_p[:, bass.ds(c * C0, C0), :], R0[par]).then_inc(rows0_stored[par], 16)

            with sp.Fori(0, (K0 - 5) // RING0) as it:
                for slot in range(RING0):
                    chunk0(it * RING0 + slot, slot, it)
            for c in range(K0 - 5, K0):
                chunk0(c, c % RING0, c // RING0)

            for par in range(2):
                sp.wait_ge(rows0_stored[par], 16 * (1 + K0 // 2 + (1 - par)))
            for r in range(2):
                sp.dma_start(xc[r], x_q[:, r * NC:r * NC + NC, :]).then_inc(xh_in[r], 16)
                sp.dma_start(hc[r], table0_q[:, r * NC:r * NC + NC, :]).then_inc(xh_in[r], 16)

            def node0(k, r, loads):
                sp.wait_ge(pss_out, k * NPC + (NPC + 2))
                sp.dma_start(table1s_q[:, bass.ds(k * NC, NC), :], PSs[r]).then_inc(pss_stored[r], 16)
                sp.wait_ge(pds_out, k * NPC + (NPC + 2))
                sp.dma_start(table1d_q[:, bass.ds(k * NC, NC), :], PDs[r]).then_inc(pds_stored[r], 16)
                if loads:
                    sp.wait_ge(node0_used, k + 1)
                    sp.dma_start(xc[r], x_q[:, bass.ds(k * NC + 2 * NC, NC), :]).then_inc(xh_in[r], 16)
                    sp.dma_start(hc[r], table0_q[:, bass.ds(k * NC + 2 * NC, NC), :]).then_inc(xh_in[r], 16)

            with sp.Fori(0, NK // 2 - 1) as it:
                for r in range(2):
                    node0(it * 2 + r, r, True)
            for k in (NK - 2, NK - 1):
                node0(k, k % 2, False)

            for s in range(RING1):
                sp.dma_start(edge_terms[s][:, 0:2, :], e32g[:, 2 * s:2 * s + 2, :]).then_inc(e32_in[s], 16)
            for r in range(2):
                sp.wait_ge(pds_scattered[r], 16 * (NB // 2 + 1))
            for s in range(RING1 - 1):
                sp.dma_start(X1[s], recv_p[:, s * C1:s * C1 + C1, :]).then_inc(recv_in[s], 16)
            sp.wait_ge(recv_used, 1)
            sp.dma_start(X1[3], recv_p[:, 3 * C1:4 * C1, :]).then_inc(recv_in[3], 16)

            def chunk1(c, s, loads):
                if loads:
                    sp.wait_ge(edge1_mm, c + 1)
                    sp.dma_start(edge_terms[s][:, 0:2, :], e32g[:, bass.ds(c * 2 + 2 * RING1, 2), :]).then_inc(e32_in[s], 16)
                    sp.wait_ge(recv_used, c + 2)
                    sp.dma_start(X1[s], recv_p[:, bass.ds(c * C1 + RING1 * C1, C1), :]).then_inc(recv_in[s], 16)
                sp.wait_ge(rows1_ready, c + 2)
                sp.dma_start(rows1_p[:, bass.ds(c * C1, C1), :], H1[s]).then_inc(rows1_stored[s], 16)

            with sp.Fori(0, K1 // RING1 - 1) as it:
                for s in range(RING1):
                    chunk1(it * RING1 + s, s, True)
            for c in range(K1 - RING1, K1):
                chunk1(c, c % RING1, False)

            def store_out(k, r):
                sp.wait_ge(fin_ready, k + 1)
                sp.dma_start(out_q[:, bass.ds(k * NC, NC), :], fin[r][0:REAL_Q]).then_inc(fin_stored[r], 16)

            with sp.Fori(0, NK // 2) as it:
                for r in range(2):
                    store_out(it * 2 + r, r)
            for r in range(2):
                sp.wait_ge(fin_stored[r], 16 * (NK // 2 + 1))
            sp.wait_ge(terms_zeroed, 64)
            sp.wait_ge(recv_zeroed, 32 * K0)
            for r in range(2):
                sp.wait_ge(pss_stored[r], 16 * (NK // 2 + 1))
                sp.wait_ge(pds_stored[r], 16 * (NK // 2 + 1))

        @block.gpsimd
        def _(pool):
            for a in (w0, we_bd, acat, w1e_bd, w1n):
                pool.memset(a[:], 0.0)
            pool.memset(zeros[:, :], 0.0)
            pool.memset(upto[0:1, 0:1], 0.0)
            pool.memset(ends_i[:, 1:2], 2 * NP)
            pool.memset(ends_i[:, 2:3], -1).then_inc(cleared, 1)
            pool.memset(ones[:, :], 1.0)
            pool.memset(ident[:, :], 0.0)
            pool.memset(eps[:, :], EPS_LN).then_inc(cleared, 1)
            pool.wait_ge(cleared, 2)
            pool.affine_select(out=ident[:, :], in_=ident[:, :], compare_op=ALU.not_equal, fill=1.0, base=0,
                               pattern=[[-1, P]], channel_multiplier=1)
            pool.affine_select(out=earlier[:, :], in_=ones[:, :], compare_op=ALU.is_gt, fill=0.0, base=0,
                               pattern=[[-1, P]], channel_multiplier=1)
            pool.iota(iota_q[:, :, :], pattern=[[1, NC], [NB, P]], base=0, channel_multiplier=0,
                      allow_small_or_imprecise_dtypes=True)
            pool.iota(node_id[:, :], pattern=[[1, NB]], base=0, channel_multiplier=NB, allow_small_or_imprecise_dtypes=True)
            pool.iota(k10[:, :], pattern=[[NC, NK + 2]], base=0, channel_multiplier=0, allow_small_or_imprecise_dtypes=True)
            pool.iota(dst_hi[:, LANE:LANE + 1], pattern=[[0, 1]], base=0, channel_multiplier=1,
                      allow_small_or_imprecise_dtypes=True)
            pool.memset(dst_lo[:, LANE:LANE + 1], 0.0).then_inc(consts, 1)

            for r in range(2):
                pool.dma_start(scrap[:, 56 + 4 * r:60 + 4 * r], zeros[:, 0:4]).then_inc(pds_scattered[r], 16)
            gather_turn = pool.alloc_register("gather_turn")
            free_turn = pool.alloc_register("free_turn")
            out_turn = pool.alloc_register("out_turn")

            def gather0(slot):
                for u in range(C0):
                    pool.indirect_dma_start(G0[slot][:, u, :], None, table0,
                                            bass.IndirectOffsetOnAxis(ap=ix[slot][:, u:u + 1], axis=0)).then_inc(gathered0[slot], 16)

            for r in range(2):
                pool.wait_ge(tab_st[r], 16 * (len(TABG) // 2 + (len(TABG) % 2) * (1 - r)))
            for slot in range(RING0):
                pool.wait_ge(ix0_ready, slot + 1)
                gather0(slot)
            pool.wait_ge(nodes_ready, 1)
            pool.indirect_dma_start(lane_rows[:, :], None, table0,
                                    bass.IndirectOffsetOnAxis(ap=ends_i[:, 0:1], axis=0)).then_inc(lane_terms_in, 16)
            pool.wait_ge(terms_zeroed, 64)
            for b in range(NB):
                pool.indirect_dma_start(dst_term, bass.IndirectOffsetOnAxis(ap=start_idx[:, b:b + 1], axis=0),
                                        a_dst[:, b, :], None, bounds_check=NE - 1, oob_is_err=False).then_inc(terms_scattered, 16)
            pool.reg_mov(gather_turn, RING0 + 1)
            pool.reg_mov(free_turn, 2)
            with pool.Fori(0, (K0 - 1) // RING0 - 1) as it:
                for slot in range(RING0):
                    pool.wait_ge(nodes_ready, 1)
                    pool.wait_ge(ix0_ready, gather_turn)
                    pool.wait_ge(rows0_ready, free_turn)
                    pool.reg_add(gather_turn, gather_turn, 1)
                    pool.reg_add(free_turn, free_turn, 1)
                    gather0(slot)
            pool.wait_ge(ix0_ready, K0)
            pool.wait_ge(rows0_ready, K0 - 3)
            gather0(0)

            def gather_last(k, r, rows, RG, done):
                for b in range(NC):
                    pool.indirect_dma_start(RG[r][:, b, :], None, rows,
                                            bass.IndirectOffsetOnAxis(ap=end_ix[r][:, b:b + 1], axis=0)).then_inc(done[r], 16)

            def scatter_first(r):
                for b in range(NC):
                    pool.indirect_dma_start(recv_term, bass.IndirectOffsetOnAxis(ap=start_ix[r][:, b:b + 1], axis=0),
                                            PDs[r][:, b, :], None, bounds_check=NE - 1, oob_is_err=False).then_inc(pds_scattered[r], 16)

            for par in range(2):
                pool.wait_ge(rows0_stored[par], 16 * (1 + K0 // 2 + (1 - par)))
            for r in range(2):
                pool.wait_ge(end_ix_ready, r + 1)
                gather_last(r, r, rows0, RG0, rg0_in)
            pool.wait_ge(recv_zeroed, 32 * K0)
            pool.reg_mov(gather_turn, 1)
            pool.reg_mov(free_turn, 3)
            pool.reg_mov(out_turn, NPC + 2)
            with pool.Fori(0, NK // 2 - 1) as it:
                for r in range(2):
                    pool.wait_ge(nodes_ready, 1)
                    pool.wait_ge(pds_out, out_turn)
                    pool.wait_ge(start_ix_ready, gather_turn)
                    pool.reg_add(out_turn, out_turn, NPC)
                    pool.reg_add(gather_turn, gather_turn, 1)
                    scatter_first(r)
                    pool.wait_ge(nodes_ready, 1)
                    pool.wait_ge(end_ix_ready, free_turn)
                    pool.reg_add(free_turn, free_turn, 1)
                    gather_last(0, r, rows0, RG0, rg0_in)
            for k in (NK - 2, NK - 1):
                pool.wait_ge(pds_out, k * NPC + NPC + 2)
                pool.wait_ge(start_ix_ready, k + 1)
                scatter_first(k % 2)

            def gather1(slot):
                for u in range(C1):
                    pool.indirect_dma_start(G1[slot][:, u, :], None, table1s,
                                            bass.IndirectOffsetOnAxis(ap=ix[slot][:, u:u + 1], axis=0)).then_inc(gathered1[slot], 16)

            for r in range(2):
                pool.wait_ge(pss_stored[r], 16 * (NK // 2 + 1))
                pool.wait_ge(pds_stored[r], 16 * (NK // 2 + 1))
            pool.indirect_dma_start(X1[3][:, C1 - 1, :], None, table1d,
                                    bass.IndirectOffsetOnAxis(ap=ends_i[:, 0:1], axis=0)).then_inc(lane_recv_in, 16)
            for slot in range(RING1):
                pool.wait_ge(ix1_ready, slot + 1)
                gather1(slot)
            pool.reg_mov(gather_turn, RING1 + 1)
            pool.reg_mov(free_turn, 1)
            with pool.Fori(0, K1 // RING1 - 1) as it:
                for slot in range(RING1):
                    pool.wait_ge(nodes_ready, 1)
                    pool.wait_ge(ix1_ready, gather_turn)
                    pool.wait_ge(relu_done, free_turn)
                    pool.reg_add(gather_turn, gather_turn, 1)
                    pool.reg_add(free_turn, free_turn, 1)
                    gather1(slot)

            for s in range(RING1):
                pool.wait_ge(rows1_stored[s], 16 * (K1 // RING1 + 1))
            for r in range(2):
                pool.wait_ge(end1_ix_ready, r + 1)
                gather_last(r, r, rows1, RG1, rg1_in)
            pool.reg_mov(gather_turn, 3)
            with pool.Fori(0, NK // 2 - 1) as it:
                for r in range(2):
                    pool.wait_ge(nodes_ready, 1)
                    pool.wait_ge(end1_ix_ready, gather_turn)
                    pool.reg_add(gather_turn, gather_turn, 1)
                    gather_last(0, r, rows1, RG1, rg1_in)

        @block.tensor
        def _(pe):
            def mm(out_, lhsT, rhs, start=True, stop=True):
                return pe.matmul(out_, lhsT, rhs, start=start, stop=stop)

            pe.wait_ge(weights_in, 16 * WEIGHT_DMAS_0)
            mm(ps[:, 7, 0:2 * H], wnT2[:, :], acat[:, :]).then_inc(fused_mm, 1)
            pe.wait_ge(xT_in, 16)
            pe.wait_ge(fused_in, 1)
            for g, m in enumerate(TABG):
                if g >= 4:
                    pe.wait_ge(tab_out, g - 3)
                for j in range(m):
                    pair = 3 * g + j
                    last = mm(ps[:, g % 4, j * 2 * ROW:(j + 1) * 2 * ROW], node_wide[:, pair * P:pair * P + P], w0[:, :])
                last.then_inc(tab_mm, 1)
            pe.wait_ge(seg_mm, 1)
            mm(ps[:, 7, 128:256], ones[:, :], below[:, 0, :]).then_inc(fused_mm, 1)
            pe.wait_ge(seg_mm, 2)
            pe.transpose(ps[:, 7, 256:384], same_seg[:, :], ident[:, :]).then_inc(fused_mm, 1)
            pe.wait_ge(seg_mm, 3)
            pe.wait_ge(tab_out, len(TABG))
            with pe.Fori(0, NK // 2) as it:
                for r in range(2):
                    pe.wait_ge(onehot_ready, it * 2 + (r + 1))
                    for b in range(NC):
                        pe.wait_ge(row_free[b % 2], it * NC + (r * NC // 2 + b // 2 + 1))
                        for c, w in COLS:
                            o = ps[:, 4 * (b % 2) + c // 512, 0:w]
                            mm(o, onehot[r][:, b, :], dst_hi[:, c:c + w], True, False)
                            last = mm(o, onehot[r][:, b, :], dst_lo[:, c:c + w], False, True)
                        last.then_inc(row_ready[b % 2], 1)
            for s in range(2):
                pe.wait_ge(row_free[s], NB // 2 + 1)

            def scores(c, par, it2):
                pe.wait_ge(e16_in[par], it2 * 16 + 16)
                pe.wait_ge(edge_mm_free, c + 1)
                for g in range(4):
                    last = mm(ps[:, par, 32 * g:32 * g + 32], edge_terms[par][:, g, :], we_bd[:, :])
                last.then_inc(edge_mm, 1)

            with pe.Fori(0, K0 // 2) as it:
                for par in range(2):
                    scores(it * 2 + par, par, it)
            scores(K0 - 1, 0, K0 // 2)

            for step in range(2):
                pe.wait_ge(carry_ready, step + 1)
                for h in range(H):
                    if step == 0:
                        last = mm(ps[:, 2, h * P:h * P + P], ones[:, :], big_a[:, h, :])
                    else:
                        last = pe.transpose(ps[:, 3, h * P:h * P + P], big_c[:, h, :], ident[:, :])
                last.then_inc(carry_mm, 1)
            pe.wait_ge(carry_ready, 3)
            tail = R0[0][:, C0 - 1, :]
            for h in range(H):
                mm(ps[:, 4, h * HD:h * HD + HD], big_b[:, h, :], tail[:, h * HD:h * HD + HD])
                last = mm(ps[:, 4, ZCOL + h:ZCOL + h + 1], big_b[:, h, :], tail[:, ZCOL + h:ZCOL + h + 1])
            last.then_inc(carry_mm, 1)
            pe.wait_ge(carry_ready, 4)

            def node0(k, r, it):
                pe.wait_ge(sel_ready, k + 1)
                pe.wait_ge(cc_ready, k + 1)
                for b in range(NC):
                    last = mm(ps[:, b // 5, (b % 5) * ROW:(b % 5 + 1) * ROW], carry_sel[:, b, :], carry0[:, :])
                last.then_inc(carried, 1)
                pe.wait_ge(x1_ready, k + 1)
                for g in range(NC // 2):
                    turn = (r + g) % 2
                    pe.transpose(ps[:, 2 + turn, 0:P], yb[:, 2 * g:2 * g + 2, :].rearrange("p a b -> p (a b)"),
                                 ident[:, :]).then_inc(x1T_mm, 1)
                    pe.wait_ge(x1T_ready, k * (NC // 2) + (g + 1))
                    pe.wait_ge(pss_out, k * NPC + (g + 1))
                    for j in range(2):
                        last = mm(ps[:, 4 + turn, j * HID:(j + 1) * HID], x1T[turn], w1n[:, j, 0:HID])
                    last.then_inc(send_mm, 1)
                    pe.wait_ge(pds_out, k * NPC + (g + 1))
                    for j in range(2):
                        last = mm(ps[:, 6 + turn, j * RECV:(j + 1) * RECV], x1T[turn], w1n[:, j, HID:HID + RECV])
                    last.then_inc(recv_mm, 1)

            pe.wait_ge(weights1_in, 16 * WEIGHT_DMAS_1)
            with pe.Fori(0, NK // 2) as it:
                for r in range(2):
                    node0(it * 2 + r, r, it)
            pe.wait_ge(pss_out, NB // 2 + 2)
            pe.wait_ge(pds_out, NB // 2 + 2)

            def edge1(c, s, it):
                pe.wait_ge(e32_in[s], it * 16 + 16)
                pe.wait_ge(pre_ready, c + 1)
                for g in range(2):
                    last = mm(ps[:, 2 * s + g, :], edge_terms[s][:, g, :], w1e_bd[:, :])
                last.then_inc(edge1_mm, 1)

            with pe.Fori(0, K1 // RING1) as it:
                for s in range(RING1):
                    edge1(it * RING1 + s, s, it)

            pe.wait_ge(rows1_ready, K1 + 1)
            pe.wait_ge(pre_ready, K1 + RING1)
            mm(ps[:, 0, 0:P], H1[(K1 - 1) % RING1][:, C1 - 1, :], same_segT[:, :]).then_inc(carry1_mm, 1)
            pe.wait_ge(carry1_cp, 1)
            mm(ps[:, 1, 0:D], rgT[0], w2[:, :]).then_inc(carry1_mm, 1)
            pe.wait_ge(carry1_cp, 2)

            def node1(k, r, it):
                pe.wait_ge(sel1_ready, k + 1)
                pe.wait_ge(rg1_in[r], it * (16 * NC) + 16 * NC)
                pe.wait_ge(agg_used, k + 1)
                for b in range(NC):
                    pe.transpose(ps[:, 4 + b % 2, 0:P], RG1[r][:, b, :], ident[:, :]).then_inc(rgT_mm, 1)
                    pe.wait_ge(rgT_ready, k * NC + (b + 1))
                    o = ps[:, 2 * r + b // 5, (b % 5) * D:(b % 5 + 1) * D]
                    mm(o, rgT[b % 2], w2[:, :], True, False)
                    last = mm(o, carry_sel[:, b, :], carry1[:, :], False, True)
                last.then_inc(agg_mm, 1)

            with pe.Fori(0, NK // 2) as it:
                for r in range(2):
                    node1(it * 2 + r, r, it)

        @block.scalar
        def _(act):
            def ix_copy(slot, cols, width, ready):
                act.activation(ix[slot][:, 0:width], src_idx[:, cols], ACT.Copy).then_inc(ready, 1)

            act.sem_inc(row_free[1], 1)
            act.sem_inc(pss_out, 2)
            act.sem_inc(cc_ready, 1)
            act.wait_ge(src_in, 16)
            for slot in range(RING0):
                ix_copy(slot, slice(slot * C0, slot * C0 + C0), C0, ix0_ready)

            act.wait_ge(ends_ready, 1)
            row = ps[:, 4:8, :].rearrange("p a b -> p (a b)")
            with act.Fori(0, NB // 2) as j:
                act.wait_ge(row_ready[1], j + 1)
                act.activation(junk_a, row[:, 0:LANE], ACT.Sign, bias=node_half[:, bass.ds(j * 2 + 1, 1)], scale=-1.0,
                               accum_out=upto[:, bass.ds(j * 2 + 2, 1)])
                act.activation(lane_of[:, bass.ds(j * 2 + 1, 1)], row[:, LANE:LANE + 1], ACT.Copy).then_inc(row_free[1], 1)

            def turn0(c, slot, copies):
                act.wait_ge(expo_ready, c + 1)
                act.activation(wq[:, :, :], expo[:, :, :], ACT.Exp).then_inc(wq_ready, 1)
                if copies:
                    ix_copy(slot, bass.ds(c * C0 + RING0 * C0, C0), C0, ix0_ready)

            with act.Fori(0, (K0 - 5) // RING0) as it:
                for slot in range(RING0):
                    turn0(it * RING0 + slot, slot, True)
            for c in range(K0 - 5, K0):
                turn0(c, c % RING0, c + RING0 < K0)

            for slot in range(RING1):
                ix_copy(slot, slice(slot * C1, slot * C1 + C1), C1, ix1_ready)
            act.wait_ge(carry_exp, 1)
            act.activation(big_c, big_b, ACT.Exp).then_inc(carry_exp, 1)

            def node0(k, r, it):
                act.wait_ge(carried, k + 1)
                act.wait_ge(cc_free, k + 1)
                act.activation(cc.rearrange("p (a b) c -> p a (b c)", a=2), ps[:, 0:2, 0:5 * ROW], ACT.Copy).then_inc(cc_ready, 1)
                act.wait_ge(e8_ready, k + 1)
                act.activation(f8, e8, ACT.Exp).then_inc(f8_ready, 1)
                for n in range(2):
                    norm(k * 2 + n, dev_ready, sq_ready, var_ready, std_ready)
                act.wait_ge(pss_stored[r], it * 16 + 16)
                act.wait_ge(x1_ready, k + 1)
                act.reg_add(spare, spare, 1)
                for g in range(NC // 2):
                    turn = (r + g) % 2
                    act.wait_ge(x1T_mm, k * (NC // 2) + (g + 1))
                    act.activation(x1T[turn], ps[:, 2 + turn, 0:P], ACT.Copy).then_inc(x1T_ready, 1)
                    act.wait_ge(send_mm, k * NPC + (g + 1))
                    act.activation(PSs[r][:, 2 * g:2 * g + 2, :].rearrange("p b f -> p (b f)"), ps[:, 4 + turn, 0:2 * HID],
                                   ACT.Copy).then_inc(pss_out, 1)

            def norm(turn, dev, squares, variance, std):
                act.wait_ge(dev, turn + 1)
                act.activation(sq, ya, ACT.Square).then_inc(squares, 1)
                act.wait_ge(variance, turn + 1)
                act.activation(rstd, var, ACT.Sqrt, bias=eps[:, 0:1], scale=1.0 / D).then_inc(std, 1)

            spare = act.alloc_register("spare")
            act.reg_mov(spare, 0)
            with act.Fori(0, NK // 2) as it:
                for r in range(2):
                    node0(it * 2 + r, r, it)

            def turn1(c, s, it, copies):
                act.wait_ge(rows1_stored[s], it * 16 + 16)
                act.wait_ge(pre_ready, c + (1 + RING1))
                act.activation(H1[s], G1[s], ACT.Relu).then_inc(relu_done, 1)
                if copies:
                    ix_copy(s, bass.ds(c * C1 + RING1 * C1, C1), C1, ix1_ready)

            with act.Fori(0, K1 // RING1 - 1) as it:
                for s in range(RING1):
                    turn1(it * RING1 + s, s, it, True)
            for c in range(K1 - RING1, K1):
                turn1(c, c % RING1, c // RING1, False)

            def node1(k):
                for b in range(NC):
                    act.wait_ge(rgT_mm, k * NC + (b + 1))
                    act.activation(rgT[b % 2], ps[:, 4 + b % 2, 0:P], ACT.Copy).then_inc(rgT_ready, 1)
                norm(k, dev1_ready, sq1_ready, var1_ready, std1_ready)

            with act.Fori(0, NK) as k:
                node1(k)

        @block.vector
        def _(dve):
            done = [0]

            def link(ins):
                done[0] += 1
                ins.then_inc(dv, 1)
                dve.wait_ge(dv, done[0])

            tt, ts, stt, scan = dve.tensor_tensor, dve.tensor_scalar, dve.scalar_tensor_tensor, dve.tensor_tensor_scan
            dve.sem_inc(row_free[0], 1)
            dve.sem_inc(edge_mm_free, 2)
            dve.sem_inc(pds_out, 2)
            dve.sem_inc(cc_free, 1)
            dve.sem_inc(pre_ready, RING1)
            dve.sem_inc(agg_used, 2)
            dve.memset(end_idx[:, NB:NB + 2 * NC], 0)
            dve.memset(R0[1][:, C0 - 1, :], 0.0).then_inc(rows0_ready, 1)

            dve.wait_ge(fused_mm, 1)
            dve.tensor_copy(w0[0:D, D:ROW], ps[0:D, 7, 0:2 * H])
            dve.tensor_copy(w0[D:2 * D, ROW + D:2 * ROW], ps[D:2 * D, 7, 0:2 * H]).then_inc(fused_in, 1)
            for g, m in enumerate(TABG):
                dve.wait_ge(tab_mm, g + 1)
                if g >= 2:
                    dve.wait_ge(tab_st[g % 2], 16 * (g // 2))
                bank = ps[:, g % 4, 0:2 * m * ROW].rearrange("p (b c) -> p b c", c=ROW)
                dve.tensor_copy(a_dst[:, 6 * g:6 * g + 2 * m, :], bank[:, :, MCOL:ROW])
                dve.tensor_copy(tab0[g % 2][:, 0:2 * m, :], bank).then_inc(tab_out, 1)

            dve.wait_ge(dst_in, 16)
            dve.wait_ge(nexts_in, 32)
            dve.wait_ge(consts, 1)
            dve.tensor_copy(ends_i[:, 0:1], dst_i[:, 0:1])
            link(dve.tensor_copy(ends_i[:, 3:4], dst_i[:, LANE - 1:LANE]))
            dve.tensor_copy(ends[:, 0:4], ends_i[:, :])
            link(dve.tensor_copy(ends[:, 4:5], ends_i[:, 0:1]))
            link(dve.memset(ends[0:1, 4:5], -1.0))
            for table, col in ((firsts, 0), (nexts, 1), (lows, 4)):
                ts(table[:, :], k10[:, :], ends[:, col:col + 1], -1.0, ALU.subtract, ALU.mult)
            link(ts(split_i, dst_i, 0xFF, None, ALU.bitwise_and))
            link(dve.tensor_copy(dst_lo[:, 0:LANE], split_i))
            link(ts(split_i, dst_i, 0xFF00, None, ALU.bitwise_and))
            dve.tensor_copy(dst_hi[:, 0:LANE], split_i)
            link(ts(node_half[:, :], node_id[:, :], 0.5, None, ALU.add))

            def lanes_hot(k, r):
                link(ts(below[:, :, :], iota_q[:, :, :], lows[:, k], None, ALU.is_ge))
                stt(onehot[r], iota_q[:, :, :], nexts[:, k], below[:, :, :], ALU.is_lt, ALU.mult).then_inc(onehot_ready, 1)

            lanes_hot(slice(0, 1), 0)
            link(dve.tensor_copy(node_half[:, 0:1], node_half[:, 0:1]))
            lanes_hot(slice(1, 2), 1)
            link(tt(same[:, 1:LANE], dst_i[:, 1:LANE], dst_i[:, 0:LANE - 1], ALU.is_equal))
            link(tt(same[:, 0:1], ends[:, 0:1], ends[:, 2:3], ALU.is_equal))
            ends_done = dve.tensor_copy(tmp_nb[:, 0:1], node_half[:, 0:1])
            ends_done.then_inc(ends_ready, 1)
            ts(below[:, 0, :], ident[:, :], ends[:, 3:4], None, ALU.mult).then_inc(seg_mm, 1)
            dve.wait_ge(fused_mm, 2)
            stt(same_seg[:, :], ps[:, 7, 128:256], ends[:, 0:1], earlier[:, :], ALU.is_equal, ALU.mult).then_inc(seg_mm, 1)
            dve.wait_ge(fused_mm, 3)
            dve.tensor_copy(same_segT[:, :], ps[:, 7, 256:384]).then_inc(seg_mm, 1)

            row = ps[:, 0:4, :].rearrange("p a b -> p (a b)")
            per = 2

            base = done[0]
            with dve.Fori(0, NK // 2) as it:
                for r in range(2):
                    for b in range(0, NC, 2):
                        col = it * (2 * NC) + (r * NC + b)
                        dve.wait_ge(row_ready[0], it * NC + (r * NC // 2 + b // 2 + 1))
                        ts(junk_v, row[:, 0:LANE], node_id[:, bass.ds(col, 1)], 0.0, ALU.is_le, ALU.add,
                           accum_out=upto[:, bass.ds(col + 1, 1)])
                        ts(lane_of[:, bass.ds(col, 1)], row[:, LANE:LANE + 1], 1.0, None, ALU.mult).then_inc(row_free[0], 1)
                    dve.wait_ge(row_ready[1], it * NC + (r * NC // 2 + NC // 2))
                    ts(below[:, :, :], iota_q[:, :, :], lows[:, bass.ds(it * 2 + (r + 2), 1)], None, ALU.is_ge).then_inc(dvc, 1)
                    dve.wait_ge(dvc, it * 2 + (r + 1))
                    stt(onehot[r], iota_q[:, :, :], nexts[:, bass.ds(it * 2 + (r + 2), 1)], below[:, :, :],
                        ALU.is_lt, ALU.mult).then_inc(onehot_ready, 1)

            dve.wait_ge(row_free[0], NB // 2 + 1)
            dve.wait_ge(row_free[1], NB // 2 + 1)
            odd = upto[:, 2:NB + 1:2]
            link(ts(odd, odd, 0.5, LANE / 2, ALU.mult, ALU.add))
            link(stt(upto[:, 1:NB + 1], lane_of[:, :], float(LANE), upto[:, 1:NB + 1], ALU.mult, ALU.add))
            link(ts(tmp_nb[:, :], upto[:, 1:NB + 1], 1.0, 0.0, ALU.subtract, ALU.max))
            dve.tensor_copy(end_idx[:, 0:NB], tmp_nb[:, :]).then_inc(upto_ready, 1)
            dve.wait_ge(upto_ready, 1)
            dve.wait_ge(wraps_in, 16)
            link(tt(degree[:, :], upto[:, 1:NB + 1], upto[:, 0:NB], ALU.subtract))
            link(ts(has[:, :], degree[:, :], 1.0, None, ALU.min))
            link(ts(degree[:, :], degree[:, :], 1.0, None, ALU.max))
            link(dve.reciprocal(inv_deg[:, :], degree[:, :]))
            link(tt(inv_deg[:, :], inv_deg[:, :], has[:, :], ALU.mult))
            link(ts(tmp_nb[:, :], has[:, :], -float(NOWHERE), float(NOWHERE), ALU.mult, ALU.add))
            link(tt(tmp_nb[:, :], tmp_nb[:, :], upto[:, 0:NB], ALU.add))
            link(dve.tensor_copy(start_idx[:, :], tmp_nb[:, :]))
            dve.tensor_copy(end_ix[0][:, :], end_idx[:, 0:NC])
            link(dve.tensor_copy(end_ix[1][:, :], end_idx[:, NC:2 * NC]))
            dve.sem_inc(nodes_ready, 1)

            terms = node_wide[:, 0:LANE * H].rearrange("p (t h) -> p t h", h=H)
            dve.wait_ge(terms_in, 16)
            dve.wait_ge(lane_terms_in, 16)
            for h in range(H):
                last = scan(terms[:, :, h], same[:, :], terms[:, :, h], lane_rows[:, MCOL + h:MCOL + h + 1], ALU.mult, ALU.add)
            link(last)
            dve.wait_ge(rows0_ready, 1)

            def wide(ap, shape):
                return ap.to_broadcast(shape)

            def turn0(c, slot, it):
                par = slot % 2
                G, R, before = G0[slot], R0[par], R0[1 - par][:, C0 - 1, :]
                same_c = same[:, bass.ds(c * C0, C0)]
                M = R[:, :, MCOL:ROW]
                dve.wait_ge(gathered0[slot], it * (16 * C0) + 16 * C0)
                tt(score[:, :, :], G[:, :, D:D + H], terms[:, bass.ds(c * C0, C0), :], ALU.add).then_inc(dv0, 1)
                dve.wait_ge(dv0, c * 4 + 1)
                dve.wait_ge(edge_mm, c + 1)
                tt(score[:, :, :], score[:, :, :], ps[:, par, 0:C0 * H].rearrange("p (t h) -> p t h", h=H), ALU.add).then_inc(edge_mm_free, 1)
                dve.wait_ge(edge_mm_free, c + 3)
                stt(score[:, :, :], score[:, :, :], SLOPE, score[:, :, :], ALU.mult, ALU.max).then_inc(dv0, 1)
                dve.wait_ge(dv0, c * 4 + 2)
                dve.wait_ge(rows0_stored[par], it * 32 + (16 * (slot // 2) + 16))
                for h in range(H):
                    last = scan(R[:, :, MCOL + h], same_c, score[:, :, h], before[:, MCOL + h:MCOL + h + 1], ALU.mult, ALU.max)
                last.then_inc(dv0, 1)
                dve.wait_ge(dv0, c * 4 + 3)
                tt(expo[:, :, 0:H], score[:, :, :], M, ALU.subtract)
                tt(expo[:, 1:C0, H:2 * H], M[:, 0:C0 - 1, :], M[:, 1:C0, :], ALU.subtract)
                tt(expo[:, 0, H:2 * H], before[:, MCOL:ROW], M[:, 0, :], ALU.subtract).then_inc(expo_ready, 1)
                dve.wait_ge(wq_ready, c + 1)
                tt(wq[:, :, H:2 * H], wq[:, :, H:2 * H], wide(same_c.unsqueeze(2), [P, C0, H]), ALU.mult)
                feats = G[:, :, 0:D].rearrange("p t (h d) -> p t h d", d=HD)
                tt(feats, feats, wide(wq[:, :, 0:H].unsqueeze(3), [P, C0, H, HD]), ALU.mult).then_inc(dv0, 1)
                dve.wait_ge(dv0, c * 4 + 4)
                dve.wait_ge(rows0_ready, c + 1)
                for f in range(D):
                    scan(R[:, :, f], wq[:, :, H + f // HD], G[:, :, f], before[:, f:f + 1], ALU.mult, ALU.add)
                for h in range(H):
                    last = scan(R[:, :, ZCOL + h], wq[:, :, H + h], wq[:, :, h], before[:, ZCOL + h:ZCOL + h + 1], ALU.mult, ALU.add)
                last.then_inc(rows0_ready, 1)

            with dve.Fori(0, K0 // RING0) as it:
                for slot in range(RING0):
                    turn0(it * RING0 + slot, slot, it)
            turn0(K0 - 1, 0, K0 // RING0)

            dve.wait_ge(rows0_ready, K0 + 1)
            tail = R0[0][:, C0 - 1, :]
            for h in range(H):
                last = ts(big_a[:, h, :], ident[:, :], tail[:, MCOL + h:MCOL + h + 1], None, ALU.mult)
            last.then_inc(carry_ready, 1)
            dve.wait_ge(carry_mm, 1)
            seg4 = wide(same_seg[:, :].unsqueeze(1), [P, H, P])
            link(tt(big_a, ps[:, 2, :].rearrange("p (h l) -> p h l", l=P), seg4, ALU.mult))
            link(dve.tensor_reduce(mc, big_a, AX.X, ALU.max))
            tt(big_b, big_a, wide(mc.unsqueeze(2), [P, H, P]), ALU.subtract).then_inc(carry_exp, 1)
            dve.wait_ge(carry_exp, 2)
            tt(big_c, big_c, seg4, ALU.mult).then_inc(carry_ready, 1)
            dve.wait_ge(carry_mm, 2)
            dve.tensor_copy(big_b.rearrange("p h l -> p (h l)"), ps[:, 3, :]).then_inc(carry_ready, 1)
            dve.wait_ge(carry_mm, 3)
            dve.tensor_copy(carry0[:, 0:MCOL], ps[:, 4, 0:MCOL])
            dve.tensor_copy(carry0[:, MCOL:ROW], mc).then_inc(carry_ready, 1)
            dve.sem_inc(end_ix_ready, 2)

            def choose(k, chain, ready):
                chain(ts(below[:, :, :], iota_q[:, :, :], nexts[:, bass.ds(k, 1)], None, ALU.is_lt))
                stt(carry_sel[:, :, :], iota_q[:, :, :], firsts[:, bass.ds(k, 1)], below[:, :, :],
                    ALU.is_equal, ALU.mult).then_inc(ready, 1)

            def norm(chain, turn, dev, squares, variance, std):
                chain(dve.tensor_reduce(mu, ya, AX.X, ALU.add))
                chain(ts(mu, mu, 1.0 / D, None, ALU.mult))
                tt(ya, ya, wide(mu.unsqueeze(2), [P, NC, D]), ALU.subtract).then_inc(dev, 1)
                dve.wait_ge(squares, turn + 1)
                dve.tensor_reduce(var, sq, AX.X, ALU.add).then_inc(variance, 1)
                dve.wait_ge(std, turn + 1)
                chain(dve.reciprocal(rstd, rstd))

            def chained(sem_, start, steps):
                n = [0]

                def chain(ins):
                    n[0] += 1
                    ins.then_inc(sem_, 1)
                    dve.wait_ge(sem_, start + n[0])

                def end():
                    assert n[0] == steps, n[0]
                return chain, end

            STEPS0 = 23

            def node0(k, r, it):
                chain, end = chained(dvn, k * STEPS0, STEPS0)
                choose(k, chain, sel_ready)
                dve.wait_ge(rg0_in[r], it * (16 * NC) + 16 * NC)
                dve.wait_ge(cc_ready, k + 2)
                dve.wait_ge(xh_in[r], it * 32 + 32)
                RG = RG0[r]
                chain(tt(z1, RG[:, :, MCOL:ROW], cc[:, :, MCOL:ROW], ALU.max))
                tt(e8[:, :, 0:H], RG[:, :, MCOL:ROW], z1, ALU.subtract)
                tt(e8[:, :, H:2 * H], cc[:, :, MCOL:ROW], z1, ALU.subtract).then_inc(e8_ready, 1)
                dve.wait_ge(f8_ready, k + 1)
                chain(tt(z1, RG[:, :, ZCOL:MCOL], f8[:, :, 0:H], ALU.mult))
                chain(tt(z2, cc[:, :, ZCOL:MCOL], f8[:, :, H:2 * H], ALU.mult))
                chain(tt(z1, z1, z2, ALU.add))
                chain(ts(z1, z1, EPS_SOFTMAX, None, ALU.add))
                chain(dve.reciprocal(z1, z1))
                chain(tt(z1, z1, wide(has[:, bass.ds(k * NC, NC)].unsqueeze(2), [P, NC, H]), ALU.mult))
                for i in range(2):
                    last = tt(e8[:, :, H * i:H * i + H], f8[:, :, H * i:H * i + H], z1, ALU.mult)
                chain(last)
                heads = lambda a: a.rearrange("p b (h d) -> p b h d", d=HD)
                tt(heads(ya), heads(RG[:, :, 0:D]), wide(e8[:, :, 0:H].unsqueeze(3), [P, NC, H, HD]), ALU.mult)
                chain(tt(heads(yb), heads(cc[:, :, 0:D]), wide(e8[:, :, H:2 * H].unsqueeze(3), [P, NC, H, HD]), ALU.mult))
                dve.sem_inc(cc_free, 1)
                ts(end_ix[r][:, :], end_idx[:, bass.ds(k * NC + 2 * NC, NC)], 1.0, None, ALU.mult).then_inc(end_ix_ready, 1)
                chain(tt(ya, ya, yb, ALU.add))
                chain(tt(ya, ya, hc[r][:, :, 0:D], ALU.add))
                norm(chain, k * 2, dev_ready, sq_ready, var_ready, std_ready)
                chain(tt(ya, ya, wide(rstd.unsqueeze(2), [P, NC, D]), ALU.mult))
                chain(tt(ya, ya, wide(row_bc[:, 0:1, :], [P, NC, D]), ALU.mult))
                chain(tt(ya, ya, wide(row_bc[:, 1:2, :], [P, NC, D]), ALU.add))
                chain(tt(ya, ya, xc[r], ALU.add))
                dve.sem_inc(node0_used, 1)
                norm(chain, k * 2 + 1, dev_ready, sq_ready, var_ready, std_ready)
                chain(tt(yb, ya, wide(rstd.unsqueeze(2), [P, NC, D]), ALU.mult))
                dve.sem_inc(x1_ready, 1)
                dve.wait_ge(pds_scattered[r], it * (16 * NC) + 16)
                dve.wait_ge(pds_stored[r], it * 16 + 16)
                ts(start_ix[r][:, :], start_idx[:, bass.ds(k * NC, NC)], 1.0, None, ALU.mult).then_inc(start_ix_ready, 1)
                for g in range(NPC):
                    bank = ps[:, 6 + (r + g) % 2, 0:2 * RECV].rearrange("p (b f) -> p b f", f=RECV)
                    pair = slice(2 * g, 2 * g + 2)
                    dve.wait_ge(recv_mm, k * NPC + (g + 1))
                    tt(PDs[r][:, pair, :], bank[:, :, 0:HID], wide(b1_bc[:, :].unsqueeze(1), [P, 2, HID]), ALU.add)
                    tt(node_wide[:, bass.ds(k * (NC * D) + 2 * g * D, 2 * D)].rearrange("p (b f) -> p b f", f=D),
                       bank[:, :, HID:RECV], yb[:, pair, :], ALU.add).then_inc(pds_out, 1)
                end()

            dve.wait_ge(weights1_in, 16 * WEIGHT_DMAS_1)
            with dve.Fori(0, NK // 2) as it:
                for r in range(2):
                    node0(it * 2 + r, r, it)

            link(dve.memset(H1[RING1 - 1][:, C1 - 1, :], 0.0))
            dve.sem_inc(rows1_ready, 1)
            dve.wait_ge(lane_recv_in, 16)

            HOLDS, STEPS1 = C1, 2 * C1 - 1

            def turn1(c, s, it, start, first=False, final=False):
                X, Xb = X1[s], X1[(s - 1) % RING1]
                Hc, Hb = H1[(s - 1) % RING1], H1[(s - 2) % RING1]
                if not final:
                    dve.wait_ge(recv_in[s], it * 16 + 16)
                if not first:
                    dve.wait_ge(relu_done, c)
                    dve.wait_ge(rows1_ready, c)
                n = 0
                for u in range(C1):
                    if not final:
                        if u:
                            dve.wait_ge(dv1, start + (n - (0 if first else 1)))
                        stt(X[:, u, :], X[:, u - 1, :] if u else Xb[:, C1 - 1, :], same[:, bass.ds(c * C1 + u, 1)],
                            X[:, u, :], ALU.mult, ALU.add).then_inc(dv1, 1)
                        n += 1
                    if not first:
                        if u:
                            dve.wait_ge(dv1, start + (n - (0 if final else 1)))
                        a = stt(Hc[:, u, :], Hc[:, u - 1, :] if u else Hb[:, C1 - 1, :], same[:, bass.ds(c * C1 - C1 + u, 1)],
                                Hc[:, u, :], ALU.mult, ALU.add)
                        if u < C1 - 1:
                            a.then_inc(dv1, 1)
                            n += 1
                        else:
                            a.then_inc(rows1_ready, 1)
                if final:
                    return
                assert n == (HOLDS if first else STEPS1)
                dve.wait_ge(dv1, start + n)
                dve.wait_ge(gathered1[s], it * (16 * C1) + 16 * C1)
                tt(G1[s], G1[s], X, ALU.add).then_inc(recv_used, 1)
                dve.wait_ge(recv_used, c + 1)
                dve.wait_ge(edge1_mm, c + 1)
                for g in range(2):
                    part_g = G1[s][:, G1E * g:G1E * g + G1E, :].rearrange("p t f -> p (t f)")
                    last = tt(part_g, part_g, ps[:, 2 * s + g, :], ALU.add)
                last.then_inc(pre_ready, 1)

            turn1(0, 0, 0, 0, first=True)
            with dve.Fori(0, K1 // RING1 - 1) as it:
                for i in range(RING1):
                    c = it * RING1 + (i + 1)
                    turn1(c, (i + 1) % RING1, it + (i + 1) // RING1, it * (RING1 * STEPS1) + (HOLDS + i * STEPS1))
            for c in range(K1 - RING1 + 1, K1):
                turn1(c, c % RING1, c // RING1, HOLDS + (c - 1) * STEPS1)
            turn1(K1, K1 % RING1, K1 // RING1, HOLDS + (K1 - 1) * STEPS1, final=True)

            dve.wait_ge(rg0_in[0], 16 * NB // 2)
            dve.wait_ge(rg0_in[1], 16 * NB // 2)
            dve.tensor_copy(end_ix[0][:, :], end_idx[:, 0:NC])
            link(dve.tensor_copy(end_ix[1][:, :], end_idx[:, NC:2 * NC]))
            dve.sem_inc(end1_ix_ready, 2)
            dve.wait_ge(carry1_mm, 1)
            dve.tensor_copy(rgT[0], ps[:, 0, 0:P]).then_inc(carry1_cp, 1)
            dve.wait_ge(carry1_mm, 2)
            dve.tensor_copy(carry1[:, :], ps[:, 1, 0:D]).then_inc(carry1_cp, 1)

            STEPS2 = 8

            def node1(k, r, it):
                chain, end = chained(dvf, k * STEPS2, STEPS2)
                choose(k, chain, sel1_ready)
                five = lambda a: a.rearrange("p (a b) d -> p a b d", b=5)
                per_node = lambda a: a[:, bass.ds(k * NC, NC)]
                dve.wait_ge(agg_mm, k + 1)
                ts(end_ix[r][:, :], end_idx[:, bass.ds(k * NC + 2 * NC, NC)], 1.0, None, ALU.mult).then_inc(end1_ix_ready, 1)
                tt(sq, wide(per_node(has).unsqueeze(2), [P, NC, D]), wide(row_bc[:, 2:3, :], [P, NC, D]), ALU.mult)
                chain(tt(five(ya), ps[:, 2 * r:2 * r + 2, 0:5 * D].rearrange("p a (b d) -> p a b d", d=D),
                         wide(per_node(inv_deg).rearrange("p (a b) -> p a b", b=5).unsqueeze(3), [P, 2, 5, D]), ALU.mult))
                dve.sem_inc(agg_used, 1)
                chain(tt(ya, ya, sq, ALU.add))
                chain(tt(ya, ya, node_wide[:, bass.ds(k * (NC * D), NC * D)].rearrange("p (b d) -> p b d", d=D), ALU.add))
                chain(tt(ya, ya, wide(row_bc[:, 3:4, :], [P, NC, D]), ALU.add))
                norm(chain, k, dev1_ready, sq1_ready, var1_ready, std1_ready)
                dve.wait_ge(fin_stored[r], it * 16 + 16)
                tt(fin[r], ya, wide(rstd.unsqueeze(2), [P, NC, D]), ALU.mult).then_inc(fin_ready, 1)
                end()

            with dve.Fori(0, NK // 2) as it:
                for r in range(2):
                    node1(it * 2 + r, r, it)


def kernel(**inputs):
    import numpy as np
    import concourse.bacc as bacc
    from concourse.bass_utils import run_bass_kernel_spmd

    a = {k: np.ascontiguousarray(v) for k, v in inputs.items()}
    xp = np.concatenate([a["x"], np.zeros((NP - N, D), a["x"].dtype)])
    lanes = lambda v, fill: np.concatenate([v, np.full((NE - E,) + v.shape[1:], fill, v.dtype)])

    def grouped(v, per):
        f = v.shape[1]
        v = lanes(v, 0).reshape(P, LANE // per, per, f)
        return np.ascontiguousarray(v.transpose(2, 3, 1, 0).reshape(per * f, LANE // per, P))

    arrays = {
        "x_d": xp,
        "xT2_d": np.ascontiguousarray(xp.reshape(P, NB // 2, 2, D).transpose(2, 3, 1, 0).reshape(2 * D, NB // 2 * P)),
        "src_d": lanes(a["src"], 0).reshape(P, LANE),
        "dst_d": lanes(a["dst"], N).reshape(P, LANE),
        "e16g_d": grouped(a["edge_attr_16"], G0E),
        "e32g_d": grouped(a["edge_attr_32"], G1E),
        "W_node_d": a["L0_gnn_W_node"],
        "W_nodeT_d": np.ascontiguousarray(a["L0_gnn_W_node"].T),
    }
    for name in ("L0_gnn_W_edge", "L0_gnn_attn_src", "L0_gnn_attn_dst", "L0_gnn_ln_gamma", "L0_gnn_ln_beta",
                 "L1_gnn_W1", "L1_gnn_b1", "L1_gnn_W2", "L1_gnn_b2", "L1_gnn_Wn", "L1_gnn_bn"):
        arrays[name + "_d"] = a[name]
    nc = bacc.Bacc("TRN2", target_bir_lowering=False, num_devices=1)
    args = [nc.dram_tensor(n, v.shape, mybir.dt.from_np(v.dtype), kind="ExternalInput").ap() for n, v in arrays.items()]
    args.append(nc.dram_tensor("out_d", (N, D), F32, kind="ExternalOutput").ap())
    build(nc, *args)
    return run_bass_kernel_spmd(nc, [arrays], core_ids=[0]).results[0]["out_d"]
```

```python
from contextlib import ExitStack

import concourse.bass as bass
from concourse import mybir

F32 = mybir.dt.float32
BF16 = mybir.dt.bfloat16
I32 = mybir.dt.int32
ALU = mybir.AluOpType
ACT = mybir.ActivationFunctionType
AX = mybir.AxisListType

P = 128
N, E = 12500, 200000
D, H, HD = 64, 4, 16
F16, F32E = 16, 32
HID = 128
RECV = HID + D
SLOPE, EPS_SOFTMAX, EPS_LN = 0.2, 1e-8, 1e-5

LANE = 1568
NE = P * LANE
NB = 100
NP = P * NB
NC = 10
QUADS = [(0, 4), (4, 8), (8, NC)]
NPC = NC // 2
NK = NB // NC
REAL_Q = N // NB

ROW = D + 2 * H
ZCOL, MCOL = D, D + H
C0 = 32
K0 = LANE // C0
RING0 = 4
G0E = P // F16
C1 = 8
K1 = LANE // C1
RING1 = 4
G1E = P // F32E
WEIGHT_DMAS_0, WEIGHT_DMAS_1 = 4 + 2 * H + P // F16, P // F32E + 12
ZERO_COLS = 2048
NOWHERE = 1 << 20


def build(nc, x, xT2, src, dst, e16g, e32g, W_node, W_nodeT, W_edge, attn_src, attn_dst, gamma, beta,
          W1, b1, W2, b2, Wn, bn, out):
    table0 = nc.dram_tensor("table0", (NP, ROW), F32).ap()
    dst_term = nc.dram_tensor("dst_term", (NE, H), F32).ap()
    rows0 = nc.dram_tensor("rows0", (NE, ROW), F32).ap()
    table1s = nc.dram_tensor("table1s", (NP, HID), F32).ap()
    table1d = nc.dram_tensor("table1d", (NP, HID), F32).ap()
    recv_term = nc.dram_tensor("recv_term", (NE, HID), F32).ap()
    rows1 = nc.dram_tensor("rows1", (NE, HID), F32).ap()

    table0_q = table0.rearrange("(q b) c -> q b c", b=NB)
    table1s_q = table1s.rearrange("(q b) c -> q b c", b=NB)
    table1d_q = table1d.rearrange("(q b) c -> q b c", b=NB)
    dst_term_p = dst_term.rearrange("(p t) c -> p (t c)", t=LANE)
    recv_flat = recv_term.rearrange("(p t) c -> p (t c)", t=LANE)
    rows0_p = rows0.rearrange("(p t) c -> p t c", t=LANE)
    rows1_p = rows1.rearrange("(p t) c -> p t c", t=LANE)
    recv_p = recv_term.rearrange("(p t) c -> p t c", t=LANE)
    x_q = x.rearrange("(q b) c -> q b c", b=NB)
    out_q = out.rearrange("(q b) c -> q b c", b=NB)

    with ExitStack() as ctx:
        ctx.enter_context(nc.allow_non_contiguous_dma(reason="one column of the small tables: a few elements"))

        def sb(name, shape, dt=F32):
            return ctx.enter_context(nc.sbuf_tensor(name, shape, dt))

        def sem(name):
            return ctx.enter_context(nc.semaphore(name))

        ps = ctx.enter_context(nc.psum_tensor("ps", [P, 8, 512], F32))

        src_idx = sb("src_idx", [P, LANE], I32)
        same = sb("same", [P, LANE])
        node_wide = sb("node_wide", [P, NB * D])
        iota_q = sb("iota_q", [P, NC, P])
        below = sb("below", [P, NC, P])
        carry_sel = sb("carry_sel", [P, NC, P])
        zeros = sb("zeros", [P, ZERO_COLS])
        ident = sb("ident", [P, P])
        ones = sb("ones", [P, P])
        same_seg = sb("same_seg", [P, P])
        same_segT = sb("same_segT", [P, P])
        earlier = sb("earlier", [P, P])
        w0 = sb("w0", [P, 2 * ROW])
        acat = sb("acat", [D, 2 * H])
        wnT2 = sb("wnT2", [D, 2 * D])
        we_bd = sb("we_bd", [P, G0E * H])
        w1e_bd = sb("w1e_bd", [P, G1E * HID])
        w1n = sb("w1n", [P, 2, 2 * HID + D])
        bias_row = sb("bias_row", [1, RECV])
        w2 = sb("w2", [HID, D])
        row_bc = sb("row_bc", [P, 3, D])
        a_dst = sb("a_dst", [P, NB, H])
        node_id = sb("node_id", [P, NB])
        node_half = sb("node_half", [P, NB])
        lane_of = sb("lane_of", [P, NB])
        upto = sb("upto", [P, NB + 1])
        degree = sb("degree", [P, NB])
        has = sb("has", [P, NB])
        inv_deg = sb("inv_deg", [P, NB])
        tmp_nb = sb("tmp_nb", [P, NB])
        start_idx = sb("start_idx", [P, NB], I32)
        end_idx = sb("end_idx", [P, NB + 2 * NC], I32)
        ends_i = sb("ends_i", [P, 4], I32)
        ends = sb("ends", [P, 6])
        k10 = sb("k10", [P, NK + 2])
        firsts = sb("firsts", [P, NK + 2])
        nexts = sb("nexts", [P, NK + 2])
        lows = sb("lows", [P, NK + 2])
        eps = sb("eps", [P, 1])
        scrap = sb("scrap", [P, 64])
        carry0 = sb("carry0", [P, ROW])
        carry1 = sb("carry1", [P, D])
        lane_rows = sb("lane_rows", [P, ROW])
        ix = [sb(f"ix{s}", [P, C0], I32) for s in range(4)]
        end_ix = [sb(f"end_ix{r}", [P, NC], I32) for r in range(2)]
        start_ix = [sb(f"start_ix{r}", [P, NC], I32) for r in range(2)]

        edge_arena = sb("edge_arena", [P, (RING0 + 2) * C0 * ROW])
        edge_terms = [sb(f"edge_terms{r}", [P, 4, P]) for r in range(4)]

        def part(arena, at, *shape):
            size = 1
            for s in shape:
                size *= s
            flat = arena[:, at:at + size]
            if len(shape) == 1:
                return flat
            if len(shape) == 2:
                return flat.rearrange("p (a b) -> p a b", b=shape[1])
            return flat.rearrange("p (a b c) -> p a b c", b=shape[1], c=shape[2])

        G0 = [part(edge_arena, s * C0 * ROW, C0, ROW) for s in range(RING0)]
        R0 = [part(edge_arena, (RING0 + r) * C0 * ROW, C0, ROW) for r in range(2)]
        W1R = C1 * HID
        G1 = [part(edge_arena, s * W1R, C1, HID) for s in range(RING1)]
        X1 = [part(edge_arena, (RING1 + s) * W1R, C1, HID) for s in range(RING1)]
        H1 = [part(edge_arena, (2 * RING1 + s) * W1R, C1, HID) for s in range(RING1)]
        score = sb("score", [P, C0, H])
        expo = sb("expo", [P, C0, 2 * H])
        wq = sb("wq", [P, C0, 2 * H])

        node_arena = sb("node_arena", [P, 13120])
        dst_i = part(node_arena, 0, LANE).bitcast(I32)
        LW = LANE + 2
        dst_hi = part(node_arena, LANE, LW // 2).bitcast(BF16)
        dst_lo = part(node_arena, LANE + LW // 2, LW // 2).bitcast(BF16)
        split_i = part(node_arena, LANE + LW, LANE).bitcast(I32)
        junk_v = part(node_arena, 2 * LANE + LW, LANE // 2).bitcast(BF16)
        junk_a = part(node_arena, 2 * LANE + LW + LANE // 2, LANE // 2).bitcast(BF16)
        at = 3 * LANE + LW
        onehot = [part(node_arena, at + r * NC * P // 2, NC * P // 2).bitcast(BF16).rearrange(
            "p (b q) -> p b q", q=P) for r in range(2)]
        at += NC * P
        tab0 = [part(node_arena, at + r * 6 * ROW, 6, ROW) for r in range(2)]
        RG0 = [part(node_arena, r * NC * ROW, NC, ROW) for r in range(2)]
        xc = [part(node_arena, 1440 + r * NC * D, NC, D) for r in range(2)]
        hc = [part(node_arena, 2720 + r * NC * ROW, NC, ROW) for r in range(2)]
        PSs = [part(node_arena, 4160 + r * NC * HID, NC, HID) for r in range(2)]
        PDs = [part(node_arena, 6720 + r * NC * HID, NC, HID) for r in range(2)]
        ya = part(node_arena, 9280, NC, D)
        x1c = [part(node_arena, (9920, 12456)[r], NC, D) for r in range(2)]
        sq = part(node_arena, 10560, NC, D)
        x1T = [part(node_arena, 11200 + j * P, P) for j in range(2)]
        f8 = part(node_arena, 11456, NC, 2 * H)
        e8 = part(node_arena, 11536, NC, 2 * H)
        cc = part(node_arena, 11736, NC, ROW)
        z1 = part(node_arena, 11616, NC, H)
        z2 = part(node_arena, 11656, NC, H)
        mu = part(node_arena, 11696, NC)
        var = part(node_arena, 11706, NC)
        rstd = part(node_arena, 11716, NC)
        big_a = part(node_arena, 4160, H, P)
        big_b = part(node_arena, 4672, H, P)
        big_c = part(node_arena, 5184, H, P)
        mc = part(node_arena, 5696, H)
        RG1 = [part(node_arena, r * NC * HID, NC, HID) for r in range(2)]
        rgT = [part(node_arena, 6560 + j * 4 * P, 4 * P) for j in range(len(QUADS))]
        b2_part = part(node_arena, 0, NB, D)
        fin = [part(node_arena, 2560 + r * NC * D, NC, D) for r in range(2)]

        PAIRS = NB // 2
        weights_in, weights1_in = sem("weights_in"), sem("weights1_in")
        xT_in, dst_in, nexts_in, src_in, wraps_in = sem("xT_in"), sem("dst_in"), sem("nexts_in"), sem("src_in"), sem("wraps_in")
        cleared, consts = sem("cleared"), sem("consts")
        fused_mm, fused_in = sem("fused_mm"), sem("fused_in")
        tab_mm, tab_out, tab_stored = sem("tab_mm"), sem("tab_out"), sem("tab_stored")
        tab_st = [sem("tab_st0"), sem("tab_st1")]
        ends_ready, dvc = sem("ends_ready"), sem("dvc")
        onehot_ready = sem("onehot_ready")
        row_ready = [sem("row_ready0"), sem("row_ready1")]
        row_free = [sem("row_free0"), sem("row_free1")]
        upto_ready, nodes_ready = sem("upto_ready"), sem("nodes_ready")
        dv = sem("dv")
        seg_mm = sem("seg_mm")
        terms_zeroed, recv_zeroed = sem("terms_zeroed"), sem("recv_zeroed")
        terms_scattered, terms_in, lane_terms_in, terms_ready = sem("terms_scattered"), sem("terms_in"), sem("lane_terms_in"), sem("terms_ready")
        ix0_ready = sem("ix0_ready")
        gathered0 = [sem(f"gathered0_{s}") for s in range(RING0)]
        e16_in = [sem("e16_in0"), sem("e16_in1")]
        edge_mm, edge_mm_free = sem("edge_mm"), sem("edge_mm_free")
        dv0 = sem("dv0")
        expo_ready, wq_ready = sem("expo_ready"), sem("wq_ready")
        rows0_ready = sem("rows0_ready")
        rows0_stored = [sem("rows0_stored0"), sem("rows0_stored1")]
        carry_mm, carry_exp, carry_ready = sem("carry_mm"), sem("carry_exp"), sem("carry_ready")
        end_ix_ready, rg0_in = sem("end_ix_ready"), [sem("rg0_in0"), sem("rg0_in1")]
        xh_in, node0_used = [sem("xh_in0"), sem("xh_in1")], sem("node0_used")
        sel_ready, carried, x_used = sem("sel_ready"), sem("carried"), sem("carried_used")
        cc_ready, cc_free = sem("cc_ready"), sem("cc_free")
        dvn = sem("dvn")
        e8_ready, f8_ready = sem("e8_ready"), sem("f8_ready")
        own_term, var_ready, std_ready = sem("own_term"), sem("var_ready"), sem("std_ready")
        x1_ready, x1T_mm, x1T_ready, send_mm, recv_mm = sem("x1_ready"), sem("x1T_mm"), sem("x1T_ready"), sem("send_mm"), sem("recv_mm")
        pss_out, pds_out = sem("pss_out"), sem("pds_out")
        start_ix_ready = sem("start_ix_ready")
        pss_stored, pds_stored, pds_scattered = [sem("pss_st0"), sem("pss_st1")], [sem("pds_st0"), sem("pds_st1")], [sem("pds_sc0"), sem("pds_sc1")]
        lane_recv_in = sem("lane_recv_in")
        lead_in = sem("lead_in")
        ix1_ready = sem("ix1_ready")
        gathered1 = [sem(f"gathered1_{s}") for s in range(RING1)]
        recv_in = [sem(f"recv_in{s}") for s in range(RING1)]
        e32_in = [sem(f"e32_in{s}") for s in range(RING1)]
        edge1_mm, pre_ready, relu_done = sem("edge1_mm"), sem("pre_ready"), sem("relu_done")
        dv1, rows1_ready, recv_used = sem("dv1"), sem("rows1_ready"), sem("recv_used")
        rows1_stored = [sem(f"rows1_stored{s}") for s in range(RING1)]
        carry1_mm, carry1_cp = sem("carry1_mm"), sem("carry1_cp")
        rg1_in, rg1_used, end1_ix_ready = [sem("rg1_in0"), sem("rg1_in1")], sem("rg1_used"), sem("end1_ix_ready")
        sel1_ready, rgT_mm, rgT_ready, agg_mm, agg_used = sem("sel1_ready"), sem("rgT_mm"), sem("rgT_ready"), sem("agg_mm"), sem("agg_used")
        dvf, var1_ready, std1_ready, fin_ready = sem("dvf"), sem("var1_ready"), sem("std1_ready"), sem("fin_ready")
        fin_stored = [sem("fin_stored0"), sem("fin_stored1")]

        block = ctx.enter_context(nc.Block())

        TABG = [min(3, PAIRS - 3 * g) for g in range((PAIRS + 2) // 3)]
        COLS = [(c, min(512, LANE + 1 - c)) for c in range(0, LANE + 1, 512)]

        @block.sync
        def _(sp):
            sp.wait_ge(cleared, 1)
            small = [(wnT2[:, 0:D], W_nodeT), (wnT2[:, D:2 * D], W_nodeT),
                     (w0[0:D, 0:D], W_node), (w0[D:2 * D, ROW:ROW + D], W_node)]
            small += [(acat[HD * h:HD * h + HD, h:h + 1], attn_src[h, :].rearrange("(d a) -> d a", a=1)) for h in range(H)]
            small += [(acat[HD * h:HD * h + HD, H + h:H + h + 1], attn_dst[h, :].rearrange("(d a) -> d a", a=1)) for h in range(H)]
            small += [(we_bd[F16 * j:F16 * j + F16, H * j:H * j + H], W_edge) for j in range(G0E)]
            for a, b in small:
                sp.dma_start(a, b).then_inc(weights_in, 16)
            assert len(small) == WEIGHT_DMAS_0
            for i, s in enumerate([*rows0_stored, *pss_stored, *pds_stored, *fin_stored, *rows1_stored]):
                sp.dma_start(scrap[:, 4 * i:4 * i + 4], zeros[:, 0:4]).then_inc(s, 16)
            sp.dma_start(node_wide[:, :], xT2).then_inc(xT_in, 16)
            sp.dma_start(dst_i, dst).then_inc(dst_in, 16)
            sp.dma_start(ends_i[0:P - 1, 1:2], dst[1:P, 0:1]).then_inc(nexts_in, 16)
            sp.dma_start(ends_i[1:P, 2:3], dst[0:P - 1, LANE - 1:LANE]).then_inc(nexts_in, 16)
            sp.dma_start(src_idx[:, :], src).then_inc(src_in, 16)
            for k in range(3):
                w = min(ZERO_COLS, LANE * H - k * ZERO_COLS)
                sp.dma_start(dst_term_p[:, k * ZERO_COLS:k * ZERO_COLS + w], zeros[:, 0:w]).then_inc(terms_zeroed, 16)
            sp.dma_start(dst_term_p[:, 3 * ZERO_COLS:LANE * H], zeros[:, 0:LANE * H - 3 * ZERO_COLS]).then_inc(terms_zeroed, 16)
            for g, m in enumerate(TABG):
                sp.wait_ge(tab_out, g + 1)
                sp.dma_start(table0_q[:, 6 * g:6 * g + 2 * m, :], tab0[g % 2][:, 0:2 * m, :]).then_inc(tab_st[g % 2], 16)
            later = [(w1e_bd[F32E * j:F32E * j + F32E, HID * j:HID * j + HID], W1[2 * D:2 * D + F32E, :]) for j in range(G1E)]
            for j in range(2):
                later += [(w1n[D * j:D * j + D, j, 0:HID], W1[0:D, :]), (w1n[D * j:D * j + D, j, HID:2 * HID], W1[D:2 * D, :]),
                          (w1n[D * j:D * j + D, j, 2 * HID:2 * HID + D], Wn)]
            later += [(w2[:, :], W2), (bias_row[:, 0:HID], b1.unsqueeze(0)), (bias_row[:, HID:RECV], bn.unsqueeze(0))]
            later += [(row_bc[:, i, :], v.partition_broadcast(P)) for i, v in enumerate((gamma, beta, b2))]
            for a, b in later:
                sp.dma_start(a, b).then_inc(weights1_in, 16)
            assert len(later) == WEIGHT_DMAS_1
            for c in range(2):
                sp.dma_start(edge_terms[c][:, :, :], e16g[:, 4 * c:4 * c + 4, :]).then_inc(e16_in[c], 16)
            sp.wait_ge(upto_ready, 1)
            sp.dma_start(upto[1:P, 0:1], upto[0:P - 1, NB:NB + 1]).then_inc(wraps_in, 16)
            sp.wait_ge(terms_scattered, 16 * NB)
            sp.dma_start(node_wide[:, 0:LANE * H], dst_term_p).then_inc(terms_in, 16)

            def chunk0(c, slot, it):
                par = slot % 2
                for z in range(2):
                    sp.dma_start(recv_flat[:, bass.ds(c * (2 * ZERO_COLS) + z * ZERO_COLS, ZERO_COLS)],
                                 zeros[:, :]).then_inc(recv_zeroed, 16)
                sp.wait_ge(edge_mm, c + 1)
                if not (isinstance(c, int) and c + 2 >= K0):
                    sp.dma_start(edge_terms[par][:, :, :], e16g[:, bass.ds(c * 4 + 8, 4), :]).then_inc(e16_in[par], 16)
                sp.wait_ge(rows0_ready, c + 2)
                sp.dma_start(rows0_p[:, bass.ds(c * C0, C0), :], R0[par]).then_inc(rows0_stored[par], 16)

            with sp.Fori(0, (K0 - 5) // RING0) as it:
                for slot in range(RING0):
                    chunk0(it * RING0 + slot, slot, it)
            for c in range(K0 - 5, K0):
                chunk0(c, c % RING0, c // RING0)

            for par in range(2):
                sp.wait_ge(rows0_stored[par], 16 * (1 + K0 // 2 + (1 - par)))
            for r in range(2):
                sp.dma_start(xc[r], x_q[:, r * NC:r * NC + NC, :]).then_inc(xh_in[r], 16)
                sp.dma_start(hc[r], table0_q[:, r * NC:r * NC + NC, :]).then_inc(xh_in[r], 16)

            def tables(k, r):
                sp.wait_ge(pss_out, k * NPC + (NPC + 2))
                sp.dma_start(table1s_q[:, bass.ds(k * NC, NC), :], PSs[r]).then_inc(pss_stored[r], 16)
                sp.wait_ge(pds_out, k * NPC + (NPC + 2))
                sp.dma_start(table1d_q[:, bass.ds(k * NC, NC), :], PDs[r]).then_inc(pds_stored[r], 16)

            def node_rows(k, r):
                sp.wait_ge(node0_used, k + 1)
                sp.dma_start(xc[r], x_q[:, bass.ds(k * NC + 2 * NC, NC), :]).then_inc(xh_in[r], 16)
                sp.dma_start(hc[r], table0_q[:, bass.ds(k * NC + 2 * NC, NC), :]).then_inc(xh_in[r], 16)

            node_rows(0, 0)
            with sp.Fori(0, NK // 2 - 2) as it:
                for r in range(2):
                    node_rows(it * 2 + (r + 1), 1 - r)
                    tables(it * 2 + r, r)
            node_rows(NK - 3, 1)
            for k in range(NK - 4, NK):
                tables(k, k % 2)

            for s in range(RING1):
                sp.dma_start(edge_terms[s][:, 0:2, :], e32g[:, 2 * s:2 * s + 2, :]).then_inc(e32_in[s], 16)
            for r in range(2):
                sp.wait_ge(pds_scattered[r], 16 * (NB // 2 + 1))
            for s in range(RING1 - 1):
                sp.dma_start(X1[s], recv_p[:, s * C1:s * C1 + C1, :]).then_inc(recv_in[s], 16)
            sp.wait_ge(recv_used, 1)
            sp.dma_start(X1[3], recv_p[:, 3 * C1:4 * C1, :]).then_inc(recv_in[3], 16)

            def chunk1(c, s, loads):
                if loads:
                    sp.wait_ge(edge1_mm, c + 1)
                    sp.dma_start(edge_terms[s][:, 0:2, :], e32g[:, bass.ds(c * 2 + 2 * RING1, 2), :]).then_inc(e32_in[s], 16)
                    sp.wait_ge(recv_used, c + 2)
                    sp.dma_start(X1[s], recv_p[:, bass.ds(c * C1 + RING1 * C1, C1), :]).then_inc(recv_in[s], 16)
                sp.wait_ge(rows1_ready, c + 2)
                sp.dma_start(rows1_p[:, bass.ds(c * C1, C1), :], H1[s]).then_inc(rows1_stored[s], 16)

            with sp.Fori(0, K1 // RING1 - 1) as it:
                for s in range(RING1):
                    chunk1(it * RING1 + s, s, True)
            for c in range(K1 - RING1, K1):
                chunk1(c, c % RING1, False)

            def store_out(k, r):
                sp.wait_ge(fin_ready, k + 1)
                sp.dma_start(out_q[:, bass.ds(k * NC, NC), :], fin[r][0:REAL_Q]).then_inc(fin_stored[r], 16)

            with sp.Fori(0, NK // 2) as it:
                for r in range(2):
                    store_out(it * 2 + r, r)
            for r in range(2):
                sp.wait_ge(fin_stored[r], 16 * (NK // 2 + 1))
            sp.wait_ge(terms_zeroed, 64)
            sp.wait_ge(recv_zeroed, 32 * K0)
            for r in range(2):
                sp.wait_ge(pss_stored[r], 16 * (NK // 2 + 1))
                sp.wait_ge(pds_stored[r], 16 * (NK // 2 + 1))

        @block.gpsimd
        def _(pool):
            for a in (w0, we_bd, acat, w1e_bd, w1n):
                pool.memset(a[:], 0.0)
            pool.memset(zeros[:, :], 0.0)
            pool.memset(upto[0:1, 0:1], 0.0)
            pool.memset(ends_i[:, 1:2], 2 * NP)
            pool.memset(ends_i[:, 2:3], -1).then_inc(cleared, 1)
            pool.memset(ones[:, :], 1.0)
            pool.memset(ident[:, :], 0.0)
            pool.memset(eps[:, :], EPS_LN).then_inc(cleared, 1)
            pool.wait_ge(cleared, 2)
            pool.affine_select(out=ident[:, :], in_=ident[:, :], compare_op=ALU.not_equal, fill=1.0, base=0,
                               pattern=[[-1, P]], channel_multiplier=1)
            pool.affine_select(out=earlier[:, :], in_=ones[:, :], compare_op=ALU.is_gt, fill=0.0, base=0,
                               pattern=[[-1, P]], channel_multiplier=1)
            pool.iota(iota_q[:, :, :], pattern=[[1, NC], [NB, P]], base=0, channel_multiplier=0,
                      allow_small_or_imprecise_dtypes=True)
            pool.iota(node_id[:, :], pattern=[[1, NB]], base=0, channel_multiplier=NB, allow_small_or_imprecise_dtypes=True)
            pool.iota(k10[:, :], pattern=[[NC, NK + 2]], base=0, channel_multiplier=0, allow_small_or_imprecise_dtypes=True)
            pool.iota(dst_hi[:, LANE:LANE + 1], pattern=[[0, 1]], base=0, channel_multiplier=1,
                      allow_small_or_imprecise_dtypes=True)
            pool.memset(dst_lo[:, LANE:LANE + 1], 0.0).then_inc(consts, 1)

            for r in range(2):
                pool.dma_start(scrap[:, 56 + 4 * r:60 + 4 * r], zeros[:, 0:4]).then_inc(pds_scattered[r], 16)
            gather_turn = pool.alloc_register("gather_turn")
            free_turn = pool.alloc_register("free_turn")
            out_turn = pool.alloc_register("out_turn")

            def gather0(slot):
                for u in range(C0):
                    pool.indirect_dma_start(G0[slot][:, u, :], None, table0,
                                            bass.IndirectOffsetOnAxis(ap=ix[slot][:, u:u + 1], axis=0)).then_inc(gathered0[slot], 16)

            for r in range(2):
                pool.wait_ge(tab_st[r], 16 * (len(TABG) // 2 + (len(TABG) % 2) * (1 - r)))
            for slot in range(RING0):
                pool.wait_ge(ix0_ready, slot + 1)
                gather0(slot)
            pool.wait_ge(nodes_ready, 1)
            pool.indirect_dma_start(lane_rows[:, :], None, table0,
                                    bass.IndirectOffsetOnAxis(ap=ends_i[:, 0:1], axis=0)).then_inc(lane_terms_in, 16)
            pool.wait_ge(terms_zeroed, 64)
            for b in range(NB):
                pool.indirect_dma_start(dst_term, bass.IndirectOffsetOnAxis(ap=start_idx[:, b:b + 1], axis=0),
                                        a_dst[:, b, :], None, bounds_check=NE - 1, oob_is_err=False).then_inc(terms_scattered, 16)
            pool.reg_mov(gather_turn, RING0 + 1)
            pool.reg_mov(free_turn, 2)
            with pool.Fori(0, (K0 - 1) // RING0 - 1) as it:
                for slot in range(RING0):
                    pool.wait_ge(nodes_ready, 1)
                    pool.wait_ge(ix0_ready, gather_turn)
                    pool.wait_ge(rows0_ready, free_turn)
                    pool.reg_add(gather_turn, gather_turn, 1)
                    pool.reg_add(free_turn, free_turn, 1)
                    gather0(slot)
            pool.wait_ge(ix0_ready, K0)
            pool.wait_ge(rows0_ready, K0 - 3)
            gather0(0)

            def gather_last(r, rows, RG, done):
                for b in range(NC):
                    pool.indirect_dma_start(RG[r][:, b, :], None, rows,
                                            bass.IndirectOffsetOnAxis(ap=end_ix[r][:, b:b + 1], axis=0)).then_inc(done[r], 16)

            def scatter_first(r):
                for b in range(NC):
                    pool.indirect_dma_start(recv_term, bass.IndirectOffsetOnAxis(ap=start_ix[r][:, b:b + 1], axis=0),
                                            PDs[r][:, b, :], None, bounds_check=NE - 1, oob_is_err=False).then_inc(pds_scattered[r], 16)

            for par in range(2):
                pool.wait_ge(rows0_stored[par], 16 * (1 + K0 // 2 + (1 - par)))
            for r in range(2):
                pool.wait_ge(end_ix_ready, r + 1)
                gather_last(r, rows0, RG0, rg0_in)
            pool.wait_ge(recv_zeroed, 32 * K0)
            pool.wait_ge(end_ix_ready, 3)
            gather_last(0, rows0, RG0, rg0_in)
            pool.reg_mov(gather_turn, 1)
            pool.reg_mov(free_turn, 4)
            pool.reg_mov(out_turn, NPC + 2)
            with pool.Fori(0, NK // 2 - 2) as it:
                for r in range(2):
                    pool.wait_ge(nodes_ready, 1)
                    pool.wait_ge(end_ix_ready, free_turn)
                    pool.reg_add(free_turn, free_turn, 1)
                    gather_last(1 - r, rows0, RG0, rg0_in)
                    pool.wait_ge(nodes_ready, 1)
                    pool.wait_ge(pds_out, out_turn)
                    pool.wait_ge(start_ix_ready, gather_turn)
                    pool.reg_add(out_turn, out_turn, NPC)
                    pool.reg_add(gather_turn, gather_turn, 1)
                    scatter_first(r)
            pool.wait_ge(end_ix_ready, NK)
            gather_last(1, rows0, RG0, rg0_in)
            for k in range(NK - 4, NK):
                pool.wait_ge(pds_out, k * NPC + NPC + 2)
                pool.wait_ge(start_ix_ready, k + 1)
                scatter_first(k % 2)

            def gather1(slot):
                for u in range(C1):
                    pool.indirect_dma_start(G1[slot][:, u, :], None, table1s,
                                            bass.IndirectOffsetOnAxis(ap=ix[slot][:, u:u + 1], axis=0)).then_inc(gathered1[slot], 16)

            for r in range(2):
                pool.wait_ge(pss_stored[r], 16 * (NK // 2 + 1))
                pool.wait_ge(pds_stored[r], 16 * (NK // 2 + 1))
            pool.indirect_dma_start(X1[3][:, C1 - 1, :], None, table1d,
                                    bass.IndirectOffsetOnAxis(ap=ends_i[:, 0:1], axis=0)).then_inc(lane_recv_in, 16)
            for slot in range(RING1):
                pool.wait_ge(ix1_ready, slot + 1)
                gather1(slot)
            pool.reg_mov(gather_turn, RING1 + 1)
            pool.reg_mov(free_turn, 1)
            with pool.Fori(0, K1 // RING1 - 1) as it:
                for slot in range(RING1):
                    pool.wait_ge(nodes_ready, 1)
                    pool.wait_ge(ix1_ready, gather_turn)
                    pool.wait_ge(relu_done, free_turn)
                    pool.reg_add(gather_turn, gather_turn, 1)
                    pool.reg_add(free_turn, free_turn, 1)
                    gather1(slot)

            for s in range(RING1):
                pool.wait_ge(rows1_stored[s], 16 * (K1 // RING1 + 1))
            for r in range(2):
                pool.wait_ge(end1_ix_ready, r + 1)
                gather_last(r, rows1, RG1, rg1_in)
            pool.reg_mov(gather_turn, 3)
            with pool.Fori(0, NK // 2 - 1) as it:
                for r in range(2):
                    pool.wait_ge(nodes_ready, 1)
                    pool.wait_ge(end1_ix_ready, gather_turn)
                    pool.reg_add(gather_turn, gather_turn, 1)
                    gather_last(r, rows1, RG1, rg1_in)

        @block.tensor
        def _(pe):
            def mm(out_, lhsT, rhs, start=True, stop=True):
                return pe.matmul(out_, lhsT, rhs, start=start, stop=stop)

            pe.wait_ge(weights_in, 16 * WEIGHT_DMAS_0)
            mm(ps[:, 7, 0:2 * H], wnT2[:, :], acat[:, :]).then_inc(fused_mm, 1)
            pe.wait_ge(xT_in, 16)
            pe.wait_ge(fused_in, 1)
            for g, m in enumerate(TABG):
                if g >= 4:
                    pe.wait_ge(tab_out, g - 3)
                for j in range(m):
                    pair = 3 * g + j
                    last = mm(ps[:, g % 4, j * 2 * ROW:(j + 1) * 2 * ROW], node_wide[:, pair * P:pair * P + P], w0[:, :])
                last.then_inc(tab_mm, 1)
            pe.wait_ge(seg_mm, 1)
            mm(ps[:, 7, 128:256], ones[:, :], below[:, 0, :]).then_inc(fused_mm, 1)
            pe.wait_ge(seg_mm, 2)
            pe.transpose(ps[:, 7, 256:384], same_seg[:, :], ident[:, :]).then_inc(fused_mm, 1)
            pe.wait_ge(seg_mm, 3)
            pe.wait_ge(tab_out, len(TABG))
            with pe.Fori(0, NK // 2) as it:
                for r in range(2):
                    pe.wait_ge(onehot_ready, it * 2 + (r + 1))
                    for b in range(NC):
                        pe.wait_ge(row_free[b % 2], it * NC + (r * NC // 2 + b // 2 + 1))
                        for c, w in COLS:
                            o = ps[:, 4 * (b % 2) + c // 512, 0:w]
                            mm(o, onehot[r][:, b, :], dst_hi[:, c:c + w], True, False)
                            last = mm(o, onehot[r][:, b, :], dst_lo[:, c:c + w], False, True)
                        last.then_inc(row_ready[b % 2], 1)
            for s in range(2):
                pe.wait_ge(row_free[s], NB // 2 + 1)

            def scores(c, par, it2):
                pe.wait_ge(e16_in[par], it2 * 16 + 16)
                pe.wait_ge(edge_mm_free, c + 1)
                for g in range(4):
                    last = mm(ps[:, par, 32 * g:32 * g + 32], edge_terms[par][:, g, :], we_bd[:, :])
                last.then_inc(edge_mm, 1)

            with pe.Fori(0, K0 // 2) as it:
                for par in range(2):
                    scores(it * 2 + par, par, it)
            scores(K0 - 1, 0, K0 // 2)

            for step in range(2):
                pe.wait_ge(carry_ready, step + 1)
                for h in range(H):
                    if step == 0:
                        last = mm(ps[:, 2, h * P:h * P + P], ones[:, :], big_a[:, h, :])
                    else:
                        last = pe.transpose(ps[:, 3, h * P:h * P + P], big_c[:, h, :], ident[:, :])
                last.then_inc(carry_mm, 1)
            pe.wait_ge(carry_ready, 3)
            tail = R0[0][:, C0 - 1, :]
            for h in range(H):
                mm(ps[:, 4, h * HD:h * HD + HD], big_b[:, h, :], tail[:, h * HD:h * HD + HD])
                last = mm(ps[:, 4, ZCOL + h:ZCOL + h + 1], big_b[:, h, :], tail[:, ZCOL + h:ZCOL + h + 1])
            last.then_inc(carry_mm, 1)
            pe.wait_ge(carry_ready, 4)

            def carry(k):
                pe.wait_ge(sel_ready, k + 1)
                pe.wait_ge(cc_ready, k + 1)
                for b in range(NC):
                    last = mm(ps[:, b // 5, (b % 5) * ROW:(b % 5 + 1) * ROW], carry_sel[:, b, :], carry0[:, :])
                last.then_inc(carried, 1)

            def project(k, r, next_carry):
                def turned(g):
                    pe.transpose(ps[:, 2 + (r + g) % 2, 0:P], x1c[r][:, 2 * g:2 * g + 2, :].rearrange("p a b -> p (a b)"),
                                 ident[:, :]).then_inc(x1T_mm, 1)

                pe.wait_ge(x1_ready, k + 1)
                turned(0)
                for g in range(NPC):
                    turn = (r + g) % 2
                    if g + 1 < NPC:
                        turned(g + 1)
                    pe.wait_ge(x1T_ready, k * NPC + (g + 1))
                    pe.wait_ge(pss_out, k * NPC + (g + 1))
                    for j in range(2):
                        last = mm(ps[:, 4 + turn, j * HID:(j + 1) * HID], x1T[turn], w1n[:, j, 0:HID])
                    last.then_inc(send_mm, 1)
                    pe.wait_ge(pds_out, k * NPC + (g + 1))
                    for j in range(2):
                        o = ps[:, 6 + turn, j * RECV:(j + 1) * RECV]
                        mm(o, x1T[turn], w1n[:, j, HID:HID + RECV], True, False)
                        last = mm(o, ones[0:1, :], bias_row[:, :], False, True)
                    last.then_inc(recv_mm, 1)
                    if g == 2 and next_carry:
                        carry(k + 2)

            pe.wait_ge(weights1_in, 16 * WEIGHT_DMAS_1)
            pe.wait_ge(own_term, 1)
            carry(0)
            carry(1)
            with pe.Fori(0, NK // 2 - 1) as it:
                for r in range(2):
                    project(it * 2 + r, r, True)
            for k in (NK - 2, NK - 1):
                project(k, k % 2, False)
            pe.wait_ge(pss_out, NB // 2 + 2)
            pe.wait_ge(pds_out, NB // 2 + 2)

            def edge1(c, s, it):
                pe.wait_ge(e32_in[s], it * 16 + 16)
                pe.wait_ge(pre_ready, c + 1)
                for g in range(2):
                    last = mm(ps[:, 2 * s + g, :], edge_terms[s][:, g, :], w1e_bd[:, :])
                last.then_inc(edge1_mm, 1)

            with pe.Fori(0, K1 // RING1) as it:
                for s in range(RING1):
                    edge1(it * RING1 + s, s, it)

            pe.wait_ge(rows1_ready, K1 + 1)
            pe.wait_ge(pre_ready, K1 + RING1)
            mm(ps[:, 0, 0:P], H1[(K1 - 1) % RING1][:, C1 - 1, :], same_segT[:, :]).then_inc(carry1_mm, 1)
            pe.wait_ge(carry1_cp, 1)
            mm(ps[:, 1, 0:D], rgT[0][:, 0:P], w2[:, :]).then_inc(carry1_mm, 1)
            pe.wait_ge(carry1_cp, 2)

            def node1(k, r, it):
                pe.wait_ge(rg1_in[r], it * (16 * NC) + 16 * NC)
                pe.wait_ge(rgT_ready, k * len(QUADS) + len(QUADS))
                for n, (lo, hi) in enumerate(QUADS):
                    for b in range(lo, hi):
                        last = pe.transpose(ps[:, 4 + n, (b - lo) * P:(b - lo + 1) * P], RG1[r][:, b, :], ident[:, :])
                    last.then_inc(rgT_mm, 1)
                pe.wait_ge(sel1_ready, k + 1)
                pe.wait_ge(agg_used, k + 1)
                for n, (lo, hi) in enumerate(QUADS):
                    pe.wait_ge(rgT_ready, k * len(QUADS) + (n + 1 + len(QUADS)))
                    for b in range(lo, hi):
                        o = ps[:, 2 * r + b // 5, (b % 5) * D:(b % 5 + 1) * D]
                        mm(o, rgT[n][:, (b - lo) * P:(b - lo + 1) * P], w2[:, :], True, False)
                        last = mm(o, carry_sel[:, b, :], carry1[:, :], False, True)
                last.then_inc(agg_mm, 1)

            with pe.Fori(0, NK // 2) as it:
                for r in range(2):
                    node1(it * 2 + r, r, it)

        @block.scalar
        def _(act):
            def ix_copy(slot, cols, width, ready):
                act.activation(ix[slot][:, 0:width], src_idx[:, cols], ACT.Copy).then_inc(ready, 1)

            act.sem_inc(row_free[1], 1)
            act.sem_inc(pss_out, 2)
            act.sem_inc(cc_ready, 1)
            act.wait_ge(src_in, 16)
            for slot in range(RING0):
                ix_copy(slot, slice(slot * C0, slot * C0 + C0), C0, ix0_ready)

            act.wait_ge(ends_ready, 1)
            row = ps[:, 4:8, :].rearrange("p a b -> p (a b)")
            with act.Fori(0, NB // 2) as j:
                act.wait_ge(row_ready[1], j + 1)
                act.activation(junk_a, row[:, 0:LANE], ACT.Sign, bias=node_half[:, bass.ds(j * 2 + 1, 1)], scale=-1.0,
                               accum_out=upto[:, bass.ds(j * 2 + 2, 1)])
                act.activation(lane_of[:, bass.ds(j * 2 + 1, 1)], row[:, LANE:LANE + 1], ACT.Copy).then_inc(row_free[1], 1)

            def turn0(c, slot, copies):
                act.wait_ge(expo_ready, c + 1)
                act.activation(wq[:, :, :], expo[:, :, :], ACT.Exp).then_inc(wq_ready, 1)
                if copies:
                    ix_copy(slot, bass.ds(c * C0 + RING0 * C0, C0), C0, ix0_ready)

            with act.Fori(0, (K0 - 5) // RING0) as it:
                for slot in range(RING0):
                    turn0(it * RING0 + slot, slot, True)
            for c in range(K0 - 5, K0):
                turn0(c, c % RING0, c + RING0 < K0)

            for slot in range(RING1):
                ix_copy(slot, slice(slot * C1, slot * C1 + C1), C1, ix1_ready)
            act.wait_ge(carry_exp, 1)
            act.activation(big_c, big_b, ACT.Exp).then_inc(carry_exp, 1)

            def root(turn, variance, std):
                act.wait_ge(variance, turn + 1)
                act.activation(rstd, var, ACT.Sqrt, bias=eps[:, 0:1], scale=1.0 / D).then_inc(std, 1)

            def carries_out(k):
                act.wait_ge(carried, k + 1)
                act.wait_ge(cc_free, k + 1)
                act.activation(cc.rearrange("p (a b) c -> p a (b c)", a=2), ps[:, 0:2, 0:5 * ROW], ACT.Copy).then_inc(cc_ready, 1)

            def project(k, r, pairs):
                for g in pairs:
                    turn = (r + g) % 2
                    pair = slice(2 * g, 2 * g + 2)
                    act.wait_ge(x1T_mm, k * NPC + (g + 1 + NPC))
                    act.activation(x1T[turn], ps[:, 2 + turn, 0:P], ACT.Copy).then_inc(x1T_ready, 1)
                    act.wait_ge(send_mm, k * NPC + (g + 1))
                    act.activation(PSs[r][:, pair, :].rearrange("p b f -> p (b f)"), ps[:, 4 + turn, 0:2 * HID],
                                   ACT.Copy).then_inc(pss_out, 1)
                    bank = ps[:, 6 + turn, 0:2 * RECV].rearrange("p (b f) -> p b f", f=RECV)
                    act.wait_ge(recv_mm, k * NPC + (g + 1))
                    act.activation(PDs[r][:, pair, :], bank[:, :, 0:HID], ACT.Copy)
                    act.activation(node_wide[:, bass.ds(k * (NC * D) + 2 * g * D, 2 * D)].rearrange("p (b f) -> p b f", f=D),
                                   bank[:, :, HID:RECV], ACT.Copy).then_inc(pds_out, 1)

            def slots(k, r, it):
                act.wait_ge(pss_stored[r], it * 16 + 16)
                act.wait_ge(pds_stored[r], it * 16 + 16)
                act.wait_ge(pds_scattered[r], it * (16 * NC) + 16)
                act.reg_add(spare, spare, 1)
                act.activation(start_ix[r][:, :], start_idx[:, bass.ds(k * NC, NC)], ACT.Copy).then_inc(start_ix_ready, 1)

            def turn(k, r, it, last=False):
                act.wait_ge(e8_ready, k + 1)
                act.activation(f8, e8, ACT.Exp).then_inc(f8_ready, 1)
                if r is not None:
                    slots(k - 1, r, it)
                    project(k - 1, r, (0, 1, 2))
                root(k * 2, var_ready, std_ready)
                if not last:
                    carries_out(k + 1)
                if r is not None:
                    project(k - 1, r, (3, 4))
                root(k * 2 + 1, var_ready, std_ready)

            spare = act.alloc_register("spare")
            act.reg_mov(spare, 0)
            carries_out(0)
            turn(0, None, None)
            with act.Fori(0, NK // 2 - 1) as it:
                for r in range(2):
                    turn(it * 2 + (r + 1), r, it)
            turn(NK - 1, 0, NK // 2 - 1, last=True)
            slots(NK - 1, 1, NK // 2 - 1)
            project(NK - 1, 1, range(NPC))

            def turn1(c, s, it, copies):
                act.wait_ge(rows1_stored[s], it * 16 + 16)
                act.wait_ge(pre_ready, c + (1 + RING1))
                act.activation(H1[s], G1[s], ACT.Relu).then_inc(relu_done, 1)
                if copies:
                    ix_copy(s, bass.ds(c * C1 + RING1 * C1, C1), C1, ix1_ready)

            with act.Fori(0, K1 // RING1 - 1) as it:
                for s in range(RING1):
                    turn1(it * RING1 + s, s, it, True)
            for c in range(K1 - RING1, K1):
                turn1(c, c % RING1, c // RING1, False)

            def turned(k, r):
                for n, (lo, hi) in enumerate(QUADS):
                    act.wait_ge(rgT_mm, k * len(QUADS) + (n + 1))
                    act.activation(rgT[n][:, 0:(hi - lo) * P], ps[:, 4 + n, 0:(hi - lo) * P], ACT.Copy).then_inc(rgT_ready, 1)
                act.activation(end_ix[r][:, :], end_idx[:, bass.ds(k * NC + 2 * NC, NC)], ACT.Copy).then_inc(end1_ix_ready, 1)

            act.wait_ge(carry1_cp, 2)
            turned(0, 0)
            with act.Fori(0, NK // 2 - 1) as it:
                for r in range(2):
                    turned(it * 2 + (r + 1), 1 - r)
                    root(it * 2 + r, var1_ready, std1_ready)
            turned(NK - 1, 1)
            root(NK - 2, var1_ready, std1_ready)
            root(NK - 1, var1_ready, std1_ready)

        @block.vector
        def _(dve):
            done = [0]

            def link(ins):
                done[0] += 1
                ins.then_inc(dv, 1)
                dve.wait_ge(dv, done[0])

            tt, ts, stt, scan = dve.tensor_tensor, dve.tensor_scalar, dve.scalar_tensor_tensor, dve.tensor_tensor_scan
            dve.sem_inc(row_free[0], 1)
            dve.sem_inc(edge_mm_free, 2)
            dve.sem_inc(pds_out, 2)
            dve.sem_inc(cc_free, 1)
            dve.sem_inc(pre_ready, RING1)
            dve.sem_inc(agg_used, 2)
            dve.sem_inc(x1T_mm, NPC)
            dve.sem_inc(rgT_ready, len(QUADS))
            dve.memset(end_idx[:, NB:NB + 2 * NC], 0)
            dve.memset(R0[1][:, C0 - 1, :], 0.0).then_inc(rows0_ready, 1)

            dve.wait_ge(fused_mm, 1)
            dve.tensor_copy(w0[0:D, D:ROW], ps[0:D, 7, 0:2 * H])
            dve.tensor_copy(w0[D:2 * D, ROW + D:2 * ROW], ps[D:2 * D, 7, 0:2 * H]).then_inc(fused_in, 1)
            for g, m in enumerate(TABG):
                dve.wait_ge(tab_mm, g + 1)
                if g >= 2:
                    dve.wait_ge(tab_st[g % 2], 16 * (g // 2))
                bank = ps[:, g % 4, 0:2 * m * ROW].rearrange("p (b c) -> p b c", c=ROW)
                dve.tensor_copy(a_dst[:, 6 * g:6 * g + 2 * m, :], bank[:, :, MCOL:ROW])
                dve.tensor_copy(tab0[g % 2][:, 0:2 * m, :], bank).then_inc(tab_out, 1)

            dve.wait_ge(dst_in, 16)
            dve.wait_ge(nexts_in, 32)
            dve.wait_ge(consts, 1)
            dve.tensor_copy(ends_i[:, 0:1], dst_i[:, 0:1])
            link(dve.tensor_copy(ends_i[:, 3:4], dst_i[:, LANE - 1:LANE]))
            dve.tensor_copy(ends[:, 0:4], ends_i[:, :])
            link(dve.tensor_copy(ends[:, 4:5], ends_i[:, 0:1]))
            link(dve.memset(ends[0:1, 4:5], -1.0))
            link(tt(ends[:, 5:6], ends[:, 0:1], ends[:, 1:2], ALU.is_equal))
            link(stt(ends[:, 5:6], ends[:, 5:6], float(4 * NP), ends[:, 0:1], ALU.mult, ALU.add))
            for table, col in ((firsts, 5), (nexts, 1), (lows, 4)):
                ts(table[:, :], k10[:, :], ends[:, col:col + 1], -1.0, ALU.subtract, ALU.mult)
            link(ts(split_i, dst_i, 0xFF, None, ALU.bitwise_and))
            link(dve.tensor_copy(dst_lo[:, 0:LANE], split_i))
            link(ts(split_i, dst_i, 0xFF00, None, ALU.bitwise_and))
            dve.tensor_copy(dst_hi[:, 0:LANE], split_i)
            link(ts(node_half[:, :], node_id[:, :], 0.5, None, ALU.add))

            def lanes_hot(k, r):
                link(ts(below[:, :, :], iota_q[:, :, :], lows[:, k], None, ALU.is_ge))
                stt(onehot[r], iota_q[:, :, :], nexts[:, k], below[:, :, :], ALU.is_lt, ALU.mult).then_inc(onehot_ready, 1)

            lanes_hot(slice(0, 1), 0)
            link(dve.tensor_copy(node_half[:, 0:1], node_half[:, 0:1]))
            lanes_hot(slice(1, 2), 1)
            link(tt(same[:, 1:LANE], dst_i[:, 1:LANE], dst_i[:, 0:LANE - 1], ALU.is_equal))
            link(tt(same[:, 0:1], ends[:, 0:1], ends[:, 2:3], ALU.is_equal))
            ends_done = dve.tensor_copy(tmp_nb[:, 0:1], node_half[:, 0:1])
            ends_done.then_inc(ends_ready, 1)
            ts(below[:, 0, :], ident[:, :], ends[:, 3:4], None, ALU.mult).then_inc(seg_mm, 1)
            dve.wait_ge(fused_mm, 2)
            stt(same_seg[:, :], ps[:, 7, 128:256], ends[:, 0:1], earlier[:, :], ALU.is_equal, ALU.mult).then_inc(seg_mm, 1)
            dve.wait_ge(fused_mm, 3)
            dve.tensor_copy(same_segT[:, :], ps[:, 7, 256:384]).then_inc(seg_mm, 1)

            row = ps[:, 0:4, :].rearrange("p a b -> p (a b)")
            per = 2

            base = done[0]
            with dve.Fori(0, NK // 2) as it:
                for r in range(2):
                    for b in range(0, NC, 2):
                        col = it * (2 * NC) + (r * NC + b)
                        dve.wait_ge(row_ready[0], it * NC + (r * NC // 2 + b // 2 + 1))
                        ts(junk_v, row[:, 0:LANE], node_id[:, bass.ds(col, 1)], 0.0, ALU.is_le, ALU.add,
                           accum_out=upto[:, bass.ds(col + 1, 1)])
                        ts(lane_of[:, bass.ds(col, 1)], row[:, LANE:LANE + 1], 1.0, None, ALU.mult).then_inc(row_free[0], 1)
                    dve.wait_ge(row_ready[1], it * NC + (r * NC // 2 + NC // 2))
                    ts(below[:, :, :], iota_q[:, :, :], lows[:, bass.ds(it * 2 + (r + 2), 1)], None, ALU.is_ge).then_inc(dvc, 1)
                    dve.wait_ge(dvc, it * 2 + (r + 1))
                    stt(onehot[r], iota_q[:, :, :], nexts[:, bass.ds(it * 2 + (r + 2), 1)], below[:, :, :],
                        ALU.is_lt, ALU.mult).then_inc(onehot_ready, 1)

            dve.wait_ge(row_free[0], NB // 2 + 1)
            dve.wait_ge(row_free[1], NB // 2 + 1)
            odd = upto[:, 2:NB + 1:2]
            link(ts(odd, odd, 0.5, LANE / 2, ALU.mult, ALU.add))
            link(stt(upto[:, 1:NB + 1], lane_of[:, :], float(LANE), upto[:, 1:NB + 1], ALU.mult, ALU.add))
            link(ts(tmp_nb[:, :], upto[:, 1:NB + 1], 1.0, 0.0, ALU.subtract, ALU.max))
            dve.tensor_copy(end_idx[:, 0:NB], tmp_nb[:, :]).then_inc(upto_ready, 1)
            dve.wait_ge(upto_ready, 1)
            dve.wait_ge(wraps_in, 16)
            link(tt(degree[:, :], upto[:, 1:NB + 1], upto[:, 0:NB], ALU.subtract))
            link(ts(has[:, :], degree[:, :], 1.0, None, ALU.min))
            link(ts(degree[:, :], degree[:, :], 1.0, None, ALU.max))
            link(dve.reciprocal(inv_deg[:, :], degree[:, :]))
            link(tt(inv_deg[:, :], inv_deg[:, :], has[:, :], ALU.mult))
            link(ts(tmp_nb[:, :], has[:, :], -float(NOWHERE), float(NOWHERE), ALU.mult, ALU.add))
            link(tt(tmp_nb[:, :], tmp_nb[:, :], upto[:, 0:NB], ALU.add))
            link(dve.tensor_copy(start_idx[:, :], tmp_nb[:, :]))
            dve.tensor_copy(end_ix[0][:, :], end_idx[:, 0:NC])
            link(dve.tensor_copy(end_ix[1][:, :], end_idx[:, NC:2 * NC]))
            dve.sem_inc(nodes_ready, 1)

            terms = node_wide[:, 0:LANE * H].rearrange("p (t h) -> p t h", h=H)
            dve.wait_ge(terms_in, 16)
            dve.wait_ge(lane_terms_in, 16)
            for h in range(H):
                last = scan(terms[:, :, h], same[:, :], terms[:, :, h], lane_rows[:, MCOL + h:MCOL + h + 1], ALU.mult, ALU.add)
            link(last)
            dve.wait_ge(rows0_ready, 1)

            def wide(ap, shape):
                return ap.to_broadcast(shape)

            def turn0(c, slot, it):
                par = slot % 2
                G, R, before = G0[slot], R0[par], R0[1 - par][:, C0 - 1, :]
                same_c = same[:, bass.ds(c * C0, C0)]
                M = R[:, :, MCOL:ROW]
                dve.wait_ge(gathered0[slot], it * (16 * C0) + 16 * C0)
                tt(score[:, :, :], G[:, :, D:D + H], terms[:, bass.ds(c * C0, C0), :], ALU.add).then_inc(dv0, 1)
                dve.wait_ge(dv0, c * 4 + 1)
                dve.wait_ge(edge_mm, c + 1)
                tt(score[:, :, :], score[:, :, :], ps[:, par, 0:C0 * H].rearrange("p (t h) -> p t h", h=H), ALU.add).then_inc(edge_mm_free, 1)
                dve.wait_ge(edge_mm_free, c + 3)
                stt(score[:, :, :], score[:, :, :], SLOPE, score[:, :, :], ALU.mult, ALU.max).then_inc(dv0, 1)
                dve.wait_ge(dv0, c * 4 + 2)
                dve.wait_ge(rows0_stored[par], it * 32 + (16 * (slot // 2) + 16))
                for h in range(H):
                    last = scan(R[:, :, MCOL + h], same_c, score[:, :, h], before[:, MCOL + h:MCOL + h + 1], ALU.mult, ALU.max)
                last.then_inc(dv0, 1)
                dve.wait_ge(dv0, c * 4 + 3)
                tt(expo[:, :, 0:H], score[:, :, :], M, ALU.subtract)
                tt(expo[:, 1:C0, H:2 * H], M[:, 0:C0 - 1, :], M[:, 1:C0, :], ALU.subtract)
                tt(expo[:, 0, H:2 * H], before[:, MCOL:ROW], M[:, 0, :], ALU.subtract).then_inc(expo_ready, 1)
                dve.wait_ge(wq_ready, c + 1)
                tt(wq[:, :, H:2 * H], wq[:, :, H:2 * H], wide(same_c.unsqueeze(2), [P, C0, H]), ALU.mult)
                feats = G[:, :, 0:D].rearrange("p t (h d) -> p t h d", d=HD)
                tt(feats, feats, wide(wq[:, :, 0:H].unsqueeze(3), [P, C0, H, HD]), ALU.mult).then_inc(dv0, 1)
                dve.wait_ge(dv0, c * 4 + 4)
                dve.wait_ge(rows0_ready, c + 1)
                for f in range(D):
                    scan(R[:, :, f], wq[:, :, H + f // HD], G[:, :, f], before[:, f:f + 1], ALU.mult, ALU.add)
                for h in range(H):
                    last = scan(R[:, :, ZCOL + h], wq[:, :, H + h], wq[:, :, h], before[:, ZCOL + h:ZCOL + h + 1], ALU.mult, ALU.add)
                last.then_inc(rows0_ready, 1)

            with dve.Fori(0, K0 // RING0) as it:
                for slot in range(RING0):
                    turn0(it * RING0 + slot, slot, it)
            turn0(K0 - 1, 0, K0 // RING0)

            dve.wait_ge(rows0_ready, K0 + 1)
            tail = R0[0][:, C0 - 1, :]
            for h in range(H):
                last = ts(big_a[:, h, :], ident[:, :], tail[:, MCOL + h:MCOL + h + 1], None, ALU.mult)
            last.then_inc(carry_ready, 1)
            dve.wait_ge(carry_mm, 1)
            seg4 = wide(same_seg[:, :].unsqueeze(1), [P, H, P])
            link(tt(big_a, ps[:, 2, :].rearrange("p (h l) -> p h l", l=P), seg4, ALU.mult))
            link(dve.tensor_reduce(mc, big_a, AX.X, ALU.max))
            tt(big_b, big_a, wide(mc.unsqueeze(2), [P, H, P]), ALU.subtract).then_inc(carry_exp, 1)
            dve.wait_ge(carry_exp, 2)
            tt(big_c, big_c, seg4, ALU.mult).then_inc(carry_ready, 1)
            dve.wait_ge(carry_mm, 2)
            dve.tensor_copy(big_b.rearrange("p h l -> p (h l)"), ps[:, 3, :]).then_inc(carry_ready, 1)
            dve.wait_ge(carry_mm, 3)
            dve.tensor_copy(carry0[:, 0:MCOL], ps[:, 4, 0:MCOL])
            dve.tensor_copy(carry0[:, MCOL:ROW], mc).then_inc(carry_ready, 1)
            dve.sem_inc(end_ix_ready, 2)

            def choose(k, ready):
                ts(carry_sel[:, :, :], iota_q[:, :, :], firsts[:, bass.ds(k, 1)], None, ALU.is_equal).then_inc(ready, 1)

            def norm(chain, turn, variance, std):
                chain(dve.tensor_reduce(mu, ya, AX.X, ALU.add))
                chain(ts(mu, mu, 1.0 / D, None, ALU.mult))
                chain(tt(ya, ya, wide(mu.unsqueeze(2), [P, NC, D]), ALU.subtract))
                chain(tt(sq, ya, ya, ALU.mult))
                dve.tensor_reduce(var, sq, AX.X, ALU.add).then_inc(variance, 1)
                dve.wait_ge(std, turn + 1)
                chain(dve.reciprocal(rstd, rstd))

            def chained(sem_, start, steps):
                n = [0]

                def chain(ins):
                    n[0] += 1
                    ins.then_inc(sem_, 1)
                    dve.wait_ge(sem_, start + n[0])

                def end():
                    assert n[0] == steps, n[0]
                return chain, end

            STEPS0 = 24

            def node0(k, r, it, first=False, more=True):
                chain, end = chained(dvn, k * STEPS0, STEPS0)
                RG, x1 = RG0[r], x1c[r]
                if more:
                    dve.wait_ge(carried, k + 1)
                    choose(k + 1, sel_ready)
                dve.wait_ge(rg0_in[r], it * (16 * NC) + 16 * NC)
                dve.wait_ge(cc_ready, k + 2)
                dve.wait_ge(xh_in[r], it * 32 + 32)
                chain(tt(z1, RG[:, :, MCOL:ROW], cc[:, :, MCOL:ROW], ALU.max))
                tt(e8[:, :, 0:H], RG[:, :, MCOL:ROW], z1, ALU.subtract)
                tt(e8[:, :, H:2 * H], cc[:, :, MCOL:ROW], z1, ALU.subtract).then_inc(e8_ready, 1)
                dve.wait_ge(f8_ready, k + 1)
                tt(z1, RG[:, :, ZCOL:MCOL], f8[:, :, 0:H], ALU.mult)
                chain(tt(z2, cc[:, :, ZCOL:MCOL], f8[:, :, H:2 * H], ALU.mult))
                chain(tt(z1, z1, z2, ALU.add))
                chain(ts(z1, z1, EPS_SOFTMAX, None, ALU.add))
                chain(dve.reciprocal(z1, z1))
                chain(tt(z1, z1, wide(has[:, bass.ds(k * NC, NC)].unsqueeze(2), [P, NC, H]), ALU.mult))
                for i in range(2):
                    last = tt(e8[:, :, H * i:H * i + H], f8[:, :, H * i:H * i + H], z1, ALU.mult)
                chain(last)
                heads = lambda a: a.rearrange("p b (h d) -> p b h d", d=HD)
                tt(heads(ya), heads(RG[:, :, 0:D]), wide(e8[:, :, 0:H].unsqueeze(3), [P, NC, H, HD]), ALU.mult)
                chain(tt(heads(sq), heads(cc[:, :, 0:D]), wide(e8[:, :, H:2 * H].unsqueeze(3), [P, NC, H, HD]), ALU.mult))
                dve.sem_inc(cc_free, 1)
                ts(end_ix[r][:, :], end_idx[:, bass.ds(k * NC + 2 * NC, NC)], 1.0, None, ALU.mult).then_inc(end_ix_ready, 1)
                chain(tt(ya, ya, sq, ALU.add))
                chain(tt(ya, ya, hc[r][:, :, 0:D], ALU.add))
                norm(chain, k * 2, var_ready, std_ready)
                chain(tt(ya, ya, wide(rstd.unsqueeze(2), [P, NC, D]), ALU.mult))
                chain(tt(ya, ya, wide(row_bc[:, 0:1, :], [P, NC, D]), ALU.mult))
                chain(tt(ya, ya, wide(row_bc[:, 1:2, :], [P, NC, D]), ALU.add))
                chain(tt(ya, ya, xc[r], ALU.add))
                dve.sem_inc(node0_used, 1)
                norm(chain, k * 2 + 1, var_ready, std_ready)
                if not first:
                    dve.wait_ge(x1T_mm, k * NPC)
                tt(x1, ya, wide(rstd.unsqueeze(2), [P, NC, D]), ALU.mult).then_inc(x1_ready, 1)
                end()

            dve.wait_ge(weights1_in, 16 * WEIGHT_DMAS_1)
            for j in range(2):
                own = w1n[D * j:D * j + D, j, 2 * HID:2 * HID + D]
                last = tt(own, own, ident[D * j:D * j + D, D * j:D * j + D], ALU.add)
            last.then_inc(own_term, 1)
            choose(0, sel_ready)
            node0(0, 0, 0, first=True)
            with dve.Fori(0, NK // 2 - 1) as it:
                for r in range(2):
                    node0(it * 2 + (r + 1), 1 - r, it + r)
            node0(NK - 1, 1, NK // 2 - 1, more=False)

            dve.wait_ge(pds_out, NB // 2 + 2)
            for r in range(2):
                dve.wait_ge(pss_stored[r], 16 * (NK // 2 + 1))
            own = node_wide[:, :].rearrange("p (b d) -> p b d", d=D)
            link(tt(b2_part, wide(has[:, :].unsqueeze(2), [P, NB, D]), wide(row_bc[:, 2:3, :], [P, NB, D]), ALU.mult))
            link(tt(own, own, b2_part, ALU.add))

            link(dve.memset(H1[RING1 - 1][:, C1 - 1, :], 0.0))
            dve.sem_inc(rows1_ready, 1)
            dve.wait_ge(lane_recv_in, 16)

            HOLDS, STEPS1 = C1, 2 * C1 - 1

            def turn1(c, s, it, start, first=False, final=False):
                X, Xb = X1[s], X1[(s - 1) % RING1]
                Hc, Hb = H1[(s - 1) % RING1], H1[(s - 2) % RING1]
                if not final:
                    dve.wait_ge(recv_in[s], it * 16 + 16)
                if not first:
                    dve.wait_ge(relu_done, c)
                    dve.wait_ge(rows1_ready, c)
                n = 0
                for u in range(C1):
                    if not final:
                        if u:
                            dve.wait_ge(dv1, start + (n - (0 if first else 1)))
                        stt(X[:, u, :], X[:, u - 1, :] if u else Xb[:, C1 - 1, :], same[:, bass.ds(c * C1 + u, 1)],
                            X[:, u, :], ALU.mult, ALU.add).then_inc(dv1, 1)
                        n += 1
                    if not first:
                        if u:
                            dve.wait_ge(dv1, start + (n - (0 if final else 1)))
                        a = stt(Hc[:, u, :], Hc[:, u - 1, :] if u else Hb[:, C1 - 1, :], same[:, bass.ds(c * C1 - C1 + u, 1)],
                                Hc[:, u, :], ALU.mult, ALU.add)
                        if u < C1 - 1:
                            a.then_inc(dv1, 1)
                            n += 1
                        else:
                            a.then_inc(rows1_ready, 1)
                if final:
                    return
                assert n == (HOLDS if first else STEPS1)
                dve.wait_ge(dv1, start + n)
                dve.wait_ge(gathered1[s], it * (16 * C1) + 16 * C1)
                tt(G1[s], G1[s], X, ALU.add).then_inc(recv_used, 1)
                dve.wait_ge(recv_used, c + 1)
                dve.wait_ge(edge1_mm, c + 1)
                for g in range(2):
                    part_g = G1[s][:, G1E * g:G1E * g + G1E, :].rearrange("p t f -> p (t f)")
                    last = tt(part_g, part_g, ps[:, 2 * s + g, :], ALU.add)
                last.then_inc(pre_ready, 1)

            turn1(0, 0, 0, 0, first=True)
            with dve.Fori(0, K1 // RING1 - 1) as it:
                for i in range(RING1):
                    c = it * RING1 + (i + 1)
                    turn1(c, (i + 1) % RING1, it + (i + 1) // RING1, it * (RING1 * STEPS1) + (HOLDS + i * STEPS1))
            for c in range(K1 - RING1 + 1, K1):
                turn1(c, c % RING1, c // RING1, HOLDS + (c - 1) * STEPS1)
            turn1(K1, K1 % RING1, K1 // RING1, HOLDS + (K1 - 1) * STEPS1, final=True)

            dve.wait_ge(rg0_in[0], 16 * NB // 2)
            dve.wait_ge(rg0_in[1], 16 * NB // 2)
            dve.tensor_copy(end_ix[0][:, :], end_idx[:, 0:NC])
            link(dve.tensor_copy(end_ix[1][:, :], end_idx[:, NC:2 * NC]))
            dve.sem_inc(end1_ix_ready, 2)
            dve.wait_ge(carry1_mm, 1)
            dve.tensor_copy(rgT[0][:, 0:P], ps[:, 0, 0:P]).then_inc(carry1_cp, 1)
            dve.wait_ge(carry1_mm, 2)
            dve.tensor_copy(carry1[:, :], ps[:, 1, 0:D]).then_inc(carry1_cp, 1)

            STEPS2 = 7

            def node1(k, r, it, more=True):
                chain, end = chained(dvf, k * STEPS2, STEPS2)
                five = lambda a: a.rearrange("p (a b) d -> p a b d", b=5)
                dve.wait_ge(agg_mm, k + 1)
                if more:
                    choose(k + 1, sel1_ready)
                chain(tt(five(ya), ps[:, 2 * r:2 * r + 2, 0:5 * D].rearrange("p a (b d) -> p a b d", d=D),
                         wide(inv_deg[:, bass.ds(k * NC, NC)].rearrange("p (a b) -> p a b", b=5).unsqueeze(3), [P, 2, 5, D]), ALU.mult))
                dve.sem_inc(agg_used, 1)
                chain(tt(ya, ya, node_wide[:, bass.ds(k * (NC * D), NC * D)].rearrange("p (b d) -> p b d", d=D), ALU.add))
                norm(chain, k, var1_ready, std1_ready)
                dve.wait_ge(fin_stored[r], it * 16 + 16)
                tt(fin[r], ya, wide(rstd.unsqueeze(2), [P, NC, D]), ALU.mult).then_inc(fin_ready, 1)
                dve.wait_ge(fin_ready, k + 1)
                end()

            choose(0, sel1_ready)
            with dve.Fori(0, NK // 2 - 1) as it:
                for r in range(2):
                    node1(it * 2 + r, r, it)
            node1(NK - 2, 0, NK // 2 - 1)
            node1(NK - 1, 1, NK // 2 - 1, more=False)


def kernel(**inputs):
    import numpy as np
    import concourse.bacc as bacc
    from concourse.bass_utils import run_bass_kernel_spmd

    a = {k: np.ascontiguousarray(v) for k, v in inputs.items()}
    xp = np.concatenate([a["x"], np.zeros((NP - N, D), a["x"].dtype)])
    lanes = lambda v, fill: np.concatenate([v, np.full((NE - E,) + v.shape[1:], fill, v.dtype)])

    def grouped(v, per):
        f = v.shape[1]
        v = lanes(v, 0).reshape(P, LANE // per, per, f)
        return np.ascontiguousarray(v.transpose(2, 3, 1, 0).reshape(per * f, LANE // per, P))

    arrays = {
        "x_d": xp,
        "xT2_d": np.ascontiguousarray(xp.reshape(P, NB // 2, 2, D).transpose(2, 3, 1, 0).reshape(2 * D, NB // 2 * P)),
        "src_d": lanes(a["src"], 0).reshape(P, LANE),
        "dst_d": lanes(a["dst"], N).reshape(P, LANE),
        "e16g_d": grouped(a["edge_attr_16"], G0E),
        "e32g_d": grouped(a["edge_attr_32"], G1E),
        "W_node_d": a["L0_gnn_W_node"],
        "W_nodeT_d": np.ascontiguousarray(a["L0_gnn_W_node"].T),
    }
    for name in ("L0_gnn_W_edge", "L0_gnn_attn_src", "L0_gnn_attn_dst", "L0_gnn_ln_gamma", "L0_gnn_ln_beta",
                 "L1_gnn_W1", "L1_gnn_b1", "L1_gnn_W2", "L1_gnn_b2", "L1_gnn_Wn", "L1_gnn_bn"):
        arrays[name + "_d"] = a[name]
    nc = bacc.Bacc("TRN2", target_bir_lowering=False, num_devices=1)
    args = [nc.dram_tensor(n, v.shape, mybir.dt.from_np(v.dtype), kind="ExternalInput").ap() for n, v in arrays.items()]
    args.append(nc.dram_tensor("out_d", (N, D), F32, kind="ExternalOutput").ap())
    build(nc, *args)
    return run_bass_kernel_spmd(nc, [arrays], core_ids=[0]).results[0]["out_d"]
```

```python
from contextlib import ExitStack

import concourse.bass as bass
from concourse import mybir

F32 = mybir.dt.float32
BF16 = mybir.dt.bfloat16
I32 = mybir.dt.int32
ALU = mybir.AluOpType
ACT = mybir.ActivationFunctionType
AX = mybir.AxisListType

P = 128
N, E = 12500, 200000
D, H, HD = 64, 4, 16
F16, F32E = 16, 32
HID = 128
RECV = HID + D
SLOPE, EPS_SOFTMAX, EPS_LN = 0.2, 1e-8, 1e-5

LANE = 1568
NE = P * LANE
NB = 100
NP = P * NB
NC = 10
QUADS = [(0, 4), (4, 8), (8, NC)]
NPC = NC // 2
NK = NB // NC
REAL_Q = N // NB

ROW = D + 2 * H
ZCOL, MCOL = D, D + H
C0 = 32
K0 = LANE // C0
RING0 = 4
G0E = P // F16
C1 = 8
K1 = LANE // C1
RING1 = 4
BANK = 512
LOW = BANK - 1
HIGH = LANE - LOW
G1E = P // F32E
WEIGHT_DMAS_0, WEIGHT_DMAS_1 = 3, 9
XPARTS = 5
SPREAD = 5
TABS = 4
ZERO_COLS = 2048
NOWHERE = 1 << 20


def build(nc, x, xT2, src, dst, e16g, e32g, W_node2, W_nodeT2, attn2, W_edge_bd, W1e_bd, W1n, gamma, beta,
          b1, W2, b2, bn, out):
    table0 = nc.dram_tensor("table0", (NP, ROW), F32).ap()
    dst_term = nc.dram_tensor("dst_term", (NE, H), F32).ap()
    rows0 = nc.dram_tensor("rows0", (NE, ROW), F32).ap()
    table1s = nc.dram_tensor("table1s", (NP, HID), F32).ap()
    table1d = nc.dram_tensor("table1d", (NP, HID), F32).ap()
    recv_term = nc.dram_tensor("recv_term", (NE, HID), F32).ap()
    rows1 = nc.dram_tensor("rows1", (NE, HID), F32).ap()

    table0_q = table0.rearrange("(q b) c -> q b c", b=NB)
    table1s_q = table1s.rearrange("(q b) c -> q b c", b=NB)
    table1d_q = table1d.rearrange("(q b) c -> q b c", b=NB)
    dst_term_p = dst_term.rearrange("(p t) c -> p (t c)", t=LANE)
    recv_flat = recv_term.rearrange("(p t) c -> p (t c)", t=LANE)
    rows0_p = rows0.rearrange("(p t) c -> p t c", t=LANE)
    rows1_p = rows1.rearrange("(p t) c -> p t c", t=LANE)
    recv_p = recv_term.rearrange("(p t) c -> p t c", t=LANE)
    x_q = x.rearrange("(q b) c -> q b c", b=NB)
    out_q = out.rearrange("(q b) c -> q b c", b=NB)

    with ExitStack() as ctx:
        ctx.enter_context(nc.allow_non_contiguous_dma(reason="one column of the small tables: a few elements"))

        def sb(name, shape, dt=F32):
            return ctx.enter_context(nc.sbuf_tensor(name, shape, dt))

        def sem(name):
            return ctx.enter_context(nc.semaphore(name))

        ps = ctx.enter_context(nc.psum_tensor("ps", [P, 8, 512], F32))

        src_idx = sb("src_idx", [P, LANE], I32)
        same = sb("same", [P, LANE])
        node_wide = sb("node_wide", [P, NB * D])
        iota_q = sb("iota_q", [P, NC, P])
        below = sb("below", [P, NC, P])
        carry_sel = sb("carry_sel", [P, NC, P])
        zeros = sb("zeros", [P, ZERO_COLS])
        ident = sb("ident", [P, P])
        ones = sb("ones", [P, P])
        same_seg = sb("same_seg", [P, P])
        same_segT = sb("same_segT", [P, P])
        earlier = sb("earlier", [P, P])
        w0 = sb("w0", [P, 2 * ROW])
        acat = sb("acat", [D, 2 * H])
        wnT2 = sb("wnT2", [D, 2 * D])
        we_bd = sb("we_bd", [P, G0E * H])
        w1e_bd = sb("w1e_bd", [P, G1E * HID])
        w1n = sb("w1n", [P, 2, 2 * HID + D])
        bias = sb("bias", [3, RECV])
        bias_rest = sb("bias_rest", [3, RECV])
        bias_sum = sb("bias_sum", [3, RECV])
        bias_part = sb("bias_part", [3, 2, RECV], BF16)
        bias_parts = sb("bias_parts", [3, RECV], BF16)
        ones3 = sb("ones3", [3, P], BF16)
        w2 = sb("w2", [HID, D])
        row_bc = sb("row_bc", [P, 3, D])
        a_dst = sb("a_dst", [P, NB, H])
        node_id = sb("node_id", [P, NB])
        node_half = sb("node_half", [P, NB])
        row_base = sb("row_base", [P, NB])
        sign_sum = sb("sign_sum", [P, NB])
        upto = sb("upto", [P, NB + 1])
        degree = sb("degree", [P, NB])
        has = sb("has", [P, NB])
        inv_deg = sb("inv_deg", [P, NB])
        tmp_nb = sb("tmp_nb", [P, NB])
        start_idx = sb("start_idx", [P, NB], I32)
        end_idx = sb("end_idx", [P, NB + 2 * NC], I32)
        ends_i = sb("ends_i", [P, 4], I32)
        ends = sb("ends", [P, 6])
        k10 = sb("k10", [P, NK + 2])
        firsts = sb("firsts", [P, NK + 2])
        nexts = sb("nexts", [P, NK + 2])
        lows = sb("lows", [P, NK + 2])
        eps = sb("eps", [P, 1])
        scrap = sb("scrap", [P, 64])
        carry0 = sb("carry0", [P, ROW])
        carry1 = sb("carry1", [P, D])
        lane_rows = sb("lane_rows", [P, ROW])
        ix = [sb(f"ix{s}", [P, C0], I32) for s in range(4)]
        end_ix = [sb(f"end_ix{r}", [P, NC], I32) for r in range(2)]
        start_ix = [sb(f"start_ix{r}", [P, NC], I32) for r in range(2)]

        edge_arena = sb("edge_arena", [P, (RING0 + 2) * C0 * ROW])
        edge_terms = [sb(f"edge_terms{r}", [P, 4, P]) for r in range(4)]

        def part(arena, at, *shape):
            size = 1
            for s in shape:
                size *= s
            flat = arena[:, at:at + size]
            if len(shape) == 1:
                return flat
            if len(shape) == 2:
                return flat.rearrange("p (a b) -> p a b", b=shape[1])
            return flat.rearrange("p (a b c) -> p a b c", b=shape[1], c=shape[2])

        G0 = [part(edge_arena, s * C0 * ROW, C0, ROW) for s in range(RING0)]
        R0 = [part(edge_arena, (RING0 + r) * C0 * ROW, C0, ROW) for r in range(2)]
        W1R = C1 * HID
        G1 = [part(edge_arena, s * W1R, C1, HID) for s in range(RING1)]
        X1 = [part(edge_arena, (RING1 + s) * W1R, C1, HID) for s in range(RING1)]
        H1 = [part(edge_arena, (2 * RING1 + s) * W1R, C1, HID) for s in range(RING1)]
        score = sb("score", [P, C0, H])
        expo = sb("expo", [P, C0, 2 * H])
        wq = sb("wq", [P, C0, 2 * H])

        node_arena = sb("node_arena", [P, 13120])
        dst_i = part(node_arena, 0, LANE).bitcast(I32)
        LW = LANE + 2
        dst_hi = part(node_arena, LANE, LW // 2).bitcast(BF16)
        dst_lo = part(node_arena, LANE + LW // 2, LW // 2).bitcast(BF16)
        split_i = part(node_arena, LANE + LW, LANE).bitcast(I32)
        at = 2 * LANE + LW
        onehot = [part(node_arena, at + r * NC * P // 2, NC * P // 2).bitcast(BF16).rearrange(
            "p (b q) -> p b q", q=P) for r in range(2)]
        at += NC * P
        tab0 = [part(node_arena, at + r * 6 * ROW, 6, ROW) for r in range(TABS)]
        at += TABS * 6 * ROW
        junk_v = [part(node_arena, at + i * BANK // 2, BANK // 2).bitcast(BF16) for i in range(2)]
        at += BANK
        junk_a = [part(node_arena, at + i * (HIGH + 1) // 2, (HIGH + 1) // 2).bitcast(BF16) for i in range(2)]
        RG0 = [part(node_arena, r * NC * ROW, NC, ROW) for r in range(2)]
        xc = [part(node_arena, 1440 + r * NC * D, NC, D) for r in range(2)]
        hc = [part(node_arena, 2720 + r * NC * ROW, NC, ROW) for r in range(2)]
        PSs = [part(node_arena, 4160 + r * NC * HID, NC, HID) for r in range(2)]
        PDs = [part(node_arena, 6720 + r * NC * HID, NC, HID) for r in range(2)]
        ya = part(node_arena, 9280, NC, D)
        x1c = [part(node_arena, (9920, 12456)[r], NC, D) for r in range(2)]
        sq = part(node_arena, 10560, NC, D)
        x1T = [part(node_arena, 11200 + j * P, P) for j in range(2)]
        f8 = part(node_arena, 11456, NC, 2 * H)
        e8 = part(node_arena, 11536, NC, 2 * H)
        cc = part(node_arena, 11736, NC, ROW)
        z1 = part(node_arena, 11616, NC, H)
        z2 = part(node_arena, 11656, NC, H)
        mu = part(node_arena, 11696, NC)
        var = part(node_arena, 11706, NC)
        rstd = part(node_arena, 11716, NC)
        big_a = part(node_arena, 4160, H, P)
        big_b = part(node_arena, 4672, H, P)
        big_c = part(node_arena, 5184, H, P)
        mc = part(node_arena, 5696, H)
        RG1 = [part(node_arena, r * NC * HID, NC, HID) for r in range(2)]
        rgT = [part(node_arena, 6560 + j * 4 * P, 4 * P) for j in range(len(QUADS))]
        b2_part = part(node_arena, 0, NB, D)
        fin = [part(node_arena, 2560 + r * NC * D, NC, D) for r in range(2)]

        PAIRS = NB // 2
        weights_in, weights1_in = sem("weights_in"), sem("weights1_in")
        xT_in = [sem(f"xT_in{i}") for i in range(XPARTS)]
        dst_in, nexts_in, src_in, wraps_in = sem("dst_in"), sem("nexts_in"), sem("src_in"), sem("wraps_in")
        cleared, consts = sem("cleared"), sem("consts")
        fused_mm, fused_in = sem("fused_mm"), sem("fused_in")
        tab_mm, tab_out, tab_stored = sem("tab_mm"), sem("tab_out"), sem("tab_stored")
        tab_st = [sem(f"tab_st{i}") for i in range(TABS)]
        starts_ready = sem("starts_ready")
        ends_ready, dvc = sem("ends_ready"), sem("dvc")
        onehot_ready = sem("onehot_ready")
        row_ready = [sem("row_ready0"), sem("row_ready1")]
        row_free = [sem("row_free0"), sem("row_free1")]
        upto_ready, nodes_ready = sem("upto_ready"), sem("nodes_ready")
        dv = sem("dv")
        seg_mm = sem("seg_mm")
        terms_zeroed, recv_zeroed = sem("terms_zeroed"), sem("recv_zeroed")
        terms_scattered, terms_in, lane_terms_in, terms_ready = sem("terms_scattered"), sem("terms_in"), sem("lane_terms_in"), sem("terms_ready")
        ix0_ready = sem("ix0_ready")
        gathered0 = [sem(f"gathered0_{s}") for s in range(RING0)]
        e16_in = [sem("e16_in0"), sem("e16_in1")]
        edge_mm, edge_mm_free = sem("edge_mm"), sem("edge_mm_free")
        dv0 = sem("dv0")
        expo_ready, wq_ready = sem("expo_ready"), sem("wq_ready")
        rows0_ready = sem("rows0_ready")
        rows0_stored = [sem("rows0_stored0"), sem("rows0_stored1")]
        carry_mm, carry_exp, carry_ready = sem("carry_mm"), sem("carry_exp"), sem("carry_ready")
        end_ix_ready, rg0_in = sem("end_ix_ready"), [sem("rg0_in0"), sem("rg0_in1")]
        xh_in, node0_used = [sem("xh_in0"), sem("xh_in1")], sem("node0_used")
        sel_ready, carried, x_used = sem("sel_ready"), sem("carried"), sem("carried_used")
        cc_ready, cc_free = sem("cc_ready"), sem("cc_free")
        dvn = sem("dvn")
        e8_ready, f8_ready = sem("e8_ready"), sem("f8_ready")
        own_term, var_ready, std_ready = sem("own_term"), sem("var_ready"), sem("std_ready")
        x1_ready, x1T_mm, x1T_ready, send_mm, recv_mm = sem("x1_ready"), sem("x1T_mm"), sem("x1T_ready"), sem("send_mm"), sem("recv_mm")
        pss_out, pds_out = sem("pss_out"), sem("pds_out")
        start_ix_ready = sem("start_ix_ready")
        pss_stored, pds_stored, pds_scattered = [sem("pss_st0"), sem("pss_st1")], [sem("pds_st0"), sem("pds_st1")], [sem("pds_sc0"), sem("pds_sc1")]
        lane_recv_in = sem("lane_recv_in")
        lead_in = sem("lead_in")
        ix1_ready = sem("ix1_ready")
        gathered1 = [sem(f"gathered1_{s}") for s in range(RING1)]
        recv_in = [sem(f"recv_in{s}") for s in range(RING1)]
        e32_in = [sem(f"e32_in{s}") for s in range(RING1)]
        edge1_mm, pre_ready, relu_done = sem("edge1_mm"), sem("pre_ready"), sem("relu_done")
        dv1, rows1_ready, recv_used = sem("dv1"), sem("rows1_ready"), sem("recv_used")
        rows1_stored = [sem(f"rows1_stored{s}") for s in range(RING1)]
        carry1_mm, carry1_cp = sem("carry1_mm"), sem("carry1_cp")
        rg1_in, rg1_used, end1_ix_ready = [sem("rg1_in0"), sem("rg1_in1")], sem("rg1_used"), sem("end1_ix_ready")
        sel1_ready, rgT_mm, rgT_ready, agg_mm, agg_used = sem("sel1_ready"), sem("rgT_mm"), sem("rgT_ready"), sem("agg_mm"), sem("agg_used")
        dvf, var1_ready, std1_ready, fin_ready = sem("dvf"), sem("var1_ready"), sem("std1_ready"), sem("fin_ready")
        fin_stored = [sem("fin_stored0"), sem("fin_stored1")]

        block = ctx.enter_context(nc.Block())

        TABG = [min(3, PAIRS - 3 * g) for g in range((PAIRS + 2) // 3)]
        COLS = [(c, min(BANK, LANE + 1 - c)) for c in range(0, LANE + 1, BANK)]

        @block.sync
        def _(sp):
            for a, b in ((wnT2[:, :], W_nodeT2), (acat[:, :], attn2), (w0[:, :], W_node2)):
                sp.dma_start(a, b).then_inc(weights_in, 16)
            for i in range(XPARTS):
                w = NB // 2 * P // XPARTS
                sp.dma_start(node_wide[:, i * w:i * w + w], xT2[:, i * w:i * w + w]).then_inc(xT_in[i], 16)
            sp.dma_start(dst_i, dst).then_inc(dst_in, 16)
            sp.wait_ge(cleared, 1)
            sp.dma_start(ends_i[0:P - 1, 1:2], dst[1:P, 0:1]).then_inc(nexts_in, 16)
            sp.dma_start(ends_i[1:P, 2:3], dst[0:P - 1, LANE - 1:LANE]).then_inc(nexts_in, 16)
            sp.dma_start(src_idx[:, :], src).then_inc(src_in, 16)
            for g, m in enumerate(TABG):
                sp.wait_ge(tab_out, g + 1)
                sp.dma_start(table0_q[:, 6 * g:6 * g + 2 * m, :], tab0[g % TABS][:, 0:2 * m, :]).then_inc(tab_st[g % TABS], 16)
            sp.wait_ge(cleared, 2)
            for i, s in enumerate([*rows0_stored, *pss_stored, *pds_stored, *fin_stored, *rows1_stored]):
                sp.dma_start(scrap[:, 4 * i:4 * i + 4], zeros[:, 0:4]).then_inc(s, 16)
            for k in range(3):
                w = min(ZERO_COLS, LANE * H - k * ZERO_COLS)
                sp.dma_start(dst_term_p[:, k * ZERO_COLS:k * ZERO_COLS + w], zeros[:, 0:w]).then_inc(terms_zeroed, 16)
            sp.dma_start(dst_term_p[:, 3 * ZERO_COLS:LANE * H], zeros[:, 0:LANE * H - 3 * ZERO_COLS]).then_inc(terms_zeroed, 16)
            later = [(we_bd[:, :], W_edge_bd), (w1e_bd[:, :], W1e_bd), (w1n[:, :, :], W1n), (w2[:, :], W2),
                     (bias[:, 0:HID], b1.partition_broadcast(3)), (bias[:, HID:RECV], bn.partition_broadcast(3))]
            later += [(row_bc[:, i, :], v.partition_broadcast(P)) for i, v in enumerate((gamma, beta, b2))]
            for a, b in later:
                sp.dma_start(a, b).then_inc(weights1_in, 16)
            assert len(later) == WEIGHT_DMAS_1
            for c in range(2):
                sp.dma_start(edge_terms[c][:, :, :], e16g[:, 4 * c:4 * c + 4, :]).then_inc(e16_in[c], 16)
            sp.wait_ge(upto_ready, 1)
            sp.dma_start(upto[1:P, 0:1], upto[0:P - 1, NB:NB + 1]).then_inc(wraps_in, 16)
            sp.wait_ge(terms_scattered, 16 * NB)
            sp.dma_start(node_wide[:, 0:LANE * H], dst_term_p).then_inc(terms_in, 16)

            def chunk0(c, slot, it):
                par = slot % 2
                for z in range(2):
                    sp.dma_start(recv_flat[:, bass.ds(c * (2 * ZERO_COLS) + z * ZERO_COLS, ZERO_COLS)],
                                 zeros[:, :]).then_inc(recv_zeroed, 16)
                sp.wait_ge(edge_mm, c + 1)
                if not (isinstance(c, int) and c + 2 >= K0):
                    sp.dma_start(edge_terms[par][:, :, :], e16g[:, bass.ds(c * 4 + 8, 4), :]).then_inc(e16_in[par], 16)
                sp.wait_ge(rows0_ready, c + 2)
                sp.dma_start(rows0_p[:, bass.ds(c * C0, C0), :], R0[par]).then_inc(rows0_stored[par], 16)

            with sp.Fori(0, (K0 - 5) // RING0) as it:
                for slot in range(RING0):
                    chunk0(it * RING0 + slot, slot, it)
            for c in range(K0 - 5, K0):
                chunk0(c, c % RING0, c // RING0)

            for par in range(2):
                sp.wait_ge(rows0_stored[par], 16 * (1 + K0 // 2 + (1 - par)))
            for r in range(2):
                sp.dma_start(xc[r], x_q[:, r * NC:r * NC + NC, :]).then_inc(xh_in[r], 16)
                sp.dma_start(hc[r], table0_q[:, r * NC:r * NC + NC, :]).then_inc(xh_in[r], 16)

            def tables(k, r):
                sp.wait_ge(pss_out, k * NPC + (NPC + 2))
                sp.dma_start(table1s_q[:, bass.ds(k * NC, NC), :], PSs[r]).then_inc(pss_stored[r], 16)
                sp.wait_ge(pds_out, k * NPC + (NPC + 2))
                sp.dma_start(table1d_q[:, bass.ds(k * NC, NC), :], PDs[r]).then_inc(pds_stored[r], 16)

            def node_rows(k, r):
                sp.wait_ge(node0_used, k + 1)
                sp.dma_start(xc[r], x_q[:, bass.ds(k * NC + 2 * NC, NC), :]).then_inc(xh_in[r], 16)
                sp.dma_start(hc[r], table0_q[:, bass.ds(k * NC + 2 * NC, NC), :]).then_inc(xh_in[r], 16)

            node_rows(0, 0)
            with sp.Fori(0, NK // 2 - 2) as it:
                for r in range(2):
                    node_rows(it * 2 + (r + 1), 1 - r)
                    tables(it * 2 + r, r)
            node_rows(NK - 3, 1)
            for k in range(NK - 4, NK):
                tables(k, k % 2)

            for s in range(RING1):
                sp.dma_start(edge_terms[s][:, 0:2, :], e32g[:, 2 * s:2 * s + 2, :]).then_inc(e32_in[s], 16)
            for r in range(2):
                sp.wait_ge(pds_scattered[r], 16 * (NB // 2 + 1))
            for s in range(RING1 - 1):
                sp.dma_start(X1[s], recv_p[:, s * C1:s * C1 + C1, :]).then_inc(recv_in[s], 16)
            sp.wait_ge(recv_used, 1)
            sp.dma_start(X1[3], recv_p[:, 3 * C1:4 * C1, :]).then_inc(recv_in[3], 16)

            def chunk1(c, s, loads):
                if loads:
                    sp.wait_ge(edge1_mm, c + 1)
                    sp.dma_start(edge_terms[s][:, 0:2, :], e32g[:, bass.ds(c * 2 + 2 * RING1, 2), :]).then_inc(e32_in[s], 16)
                    sp.wait_ge(recv_used, c + 2)
                    sp.dma_start(X1[s], recv_p[:, bass.ds(c * C1 + RING1 * C1, C1), :]).then_inc(recv_in[s], 16)
                sp.wait_ge(rows1_ready, c + 2)
                sp.dma_start(rows1_p[:, bass.ds(c * C1, C1), :], H1[s]).then_inc(rows1_stored[s], 16)

            with sp.Fori(0, K1 // RING1 - 1) as it:
                for s in range(RING1):
                    chunk1(it * RING1 + s, s, True)
            for c in range(K1 - RING1, K1):
                chunk1(c, c % RING1, False)

            def store_out(k, r):
                sp.wait_ge(fin_ready, k + 1)
                sp.dma_start(out_q[:, bass.ds(k * NC, NC), :], fin[r][0:REAL_Q]).then_inc(fin_stored[r], 16)

            with sp.Fori(0, NK // 2) as it:
                for r in range(2):
                    store_out(it * 2 + r, r)
            for r in range(2):
                sp.wait_ge(fin_stored[r], 16 * (NK // 2 + 1))
            sp.wait_ge(terms_zeroed, 64)
            sp.wait_ge(recv_zeroed, 32 * K0)
            for r in range(2):
                sp.wait_ge(pss_stored[r], 16 * (NK // 2 + 1))
                sp.wait_ge(pds_stored[r], 16 * (NK // 2 + 1))

        @block.gpsimd
        def _(pool):
            pool.memset(ends_i[:, 1:2], 2 * NP)
            pool.memset(ends_i[:, 2:3], -1).then_inc(cleared, 1)
            pool.memset(zeros[:, :], 0.0)
            pool.memset(upto[:, 0:1], 0.0)
            pool.memset(ones[:, :], 1.0)
            pool.memset(ident[:, :], 0.0)
            pool.memset(eps[:, :], EPS_LN).then_inc(cleared, 1)
            pool.wait_ge(cleared, 2)
            pool.affine_select(out=ident[:, :], in_=ident[:, :], compare_op=ALU.not_equal, fill=1.0, base=0,
                               pattern=[[-1, P]], channel_multiplier=1)
            pool.affine_select(out=earlier[:, :], in_=ones[:, :], compare_op=ALU.is_gt, fill=0.0, base=0,
                               pattern=[[-1, P]], channel_multiplier=1)
            pool.iota(iota_q[:, :, :], pattern=[[1, NC], [NB, P]], base=0, channel_multiplier=0,
                      allow_small_or_imprecise_dtypes=True)
            pool.iota(node_id[:, :], pattern=[[1, NB]], base=0, channel_multiplier=NB, allow_small_or_imprecise_dtypes=True)
            pool.iota(k10[:, :], pattern=[[NC, NK + 2]], base=0, channel_multiplier=0, allow_small_or_imprecise_dtypes=True)
            pool.iota(dst_hi[:, 0:1], pattern=[[0, 1]], base=0, channel_multiplier=1,
                      allow_small_or_imprecise_dtypes=True)
            pool.memset(dst_lo[:, 0:1], 0.0).then_inc(consts, 1)

            for r in range(2):
                pool.dma_start(scrap[:, 56 + 4 * r:60 + 4 * r], zeros[:, 0:4]).then_inc(pds_scattered[r], 16)
            gather_turn = pool.alloc_register("gather_turn")
            free_turn = pool.alloc_register("free_turn")
            out_turn = pool.alloc_register("out_turn")

            def gather0(slot):
                for u in range(C0):
                    pool.indirect_dma_start(G0[slot][:, u, :], None, table0,
                                            bass.IndirectOffsetOnAxis(ap=ix[slot][:, u:u + 1], axis=0)).then_inc(gathered0[slot], 16)

            for r in range(TABS):
                pool.wait_ge(tab_st[r], 16 * len(range(r, len(TABG), TABS)))
            pool.wait_ge(ends_ready, 1)
            pool.indirect_dma_start(lane_rows[:, :], None, table0,
                                    bass.IndirectOffsetOnAxis(ap=ends_i[:, 0:1], axis=0)).then_inc(lane_terms_in, 16)

            def gather_columns(lo, hi):
                for t in range(lo, hi):
                    slot, u = divmod(t, C0)
                    if u == 0:
                        pool.wait_ge(ix0_ready, slot + 1)
                    pool.indirect_dma_start(G0[slot][:, u, :], None, table0,
                                            bass.IndirectOffsetOnAxis(ap=ix[slot][:, u:u + 1], axis=0)).then_inc(gathered0[slot], 16)

            def scatter_terms(lo, hi):
                for b in range(lo, hi):
                    pool.indirect_dma_start(dst_term, bass.IndirectOffsetOnAxis(ap=start_idx[:, b:b + 1], axis=0),
                                            a_dst[:, b, :], None, bounds_check=NE - 1, oob_is_err=False).then_inc(terms_scattered, 16)

            gather_columns(0, C0)
            pool.wait_ge(terms_zeroed, 64)
            for k in range(NK):
                pool.wait_ge(starts_ready, k + 1)
                scatter_terms(max(1, k * NC), k * NC + NC)
                gather_columns(C0 + SPREAD * k, C0 + SPREAD * k + SPREAD)
            pool.wait_ge(nodes_ready, 1)
            scatter_terms(0, 1)
            gather_columns(C0 + SPREAD * NK, RING0 * C0)
            pool.reg_mov(gather_turn, RING0 + 1)
            pool.reg_mov(free_turn, 2)
            with pool.Fori(0, (K0 - 1) // RING0 - 1) as it:
                for slot in range(RING0):
                    pool.wait_ge(nodes_ready, 1)
                    pool.wait_ge(ix0_ready, gather_turn)
                    pool.wait_ge(rows0_ready, free_turn)
                    pool.reg_add(gather_turn, gather_turn, 1)
                    pool.reg_add(free_turn, free_turn, 1)
                    gather0(slot)
            pool.wait_ge(ix0_ready, K0)
            pool.wait_ge(rows0_ready, K0 - 3)
            gather0(0)

            def gather_last(r, rows, RG, done):
                for b in range(NC):
                    pool.indirect_dma_start(RG[r][:, b, :], None, rows,
                                            bass.IndirectOffsetOnAxis(ap=end_ix[r][:, b:b + 1], axis=0)).then_inc(done[r], 16)

            def scatter_first(r):
                for b in range(NC):
                    pool.indirect_dma_start(recv_term, bass.IndirectOffsetOnAxis(ap=start_ix[r][:, b:b + 1], axis=0),
                                            PDs[r][:, b, :], None, bounds_check=NE - 1, oob_is_err=False).then_inc(pds_scattered[r], 16)

            for par in range(2):
                pool.wait_ge(rows0_stored[par], 16 * (1 + K0 // 2 + (1 - par)))
            for r in range(2):
                pool.wait_ge(end_ix_ready, r + 1)
                gather_last(r, rows0, RG0, rg0_in)
            pool.wait_ge(recv_zeroed, 32 * K0)
            pool.wait_ge(end_ix_ready, 3)
            gather_last(0, rows0, RG0, rg0_in)
            pool.reg_mov(gather_turn, 1)
            pool.reg_mov(free_turn, 4)
            pool.reg_mov(out_turn, NPC + 2)
            with pool.Fori(0, NK // 2 - 2) as it:
                for r in range(2):
                    pool.wait_ge(nodes_ready, 1)
                    pool.wait_ge(end_ix_ready, free_turn)
                    pool.reg_add(free_turn, free_turn, 1)
                    gather_last(1 - r, rows0, RG0, rg0_in)
                    pool.wait_ge(nodes_ready, 1)
                    pool.wait_ge(pds_out, out_turn)
                    pool.wait_ge(start_ix_ready, gather_turn)
                    pool.reg_add(out_turn, out_turn, NPC)
                    pool.reg_add(gather_turn, gather_turn, 1)
                    scatter_first(r)
            pool.wait_ge(end_ix_ready, NK)
            gather_last(1, rows0, RG0, rg0_in)
            for k in range(NK - 4, NK):
                pool.wait_ge(pds_out, k * NPC + NPC + 2)
                pool.wait_ge(start_ix_ready, k + 1)
                scatter_first(k % 2)

            def gather1(slot):
                for u in range(C1):
                    pool.indirect_dma_start(G1[slot][:, u, :], None, table1s,
                                            bass.IndirectOffsetOnAxis(ap=ix[slot][:, u:u + 1], axis=0)).then_inc(gathered1[slot], 16)

            for r in range(2):
                pool.wait_ge(pss_stored[r], 16 * (NK // 2 + 1))
                pool.wait_ge(pds_stored[r], 16 * (NK // 2 + 1))
            pool.indirect_dma_start(X1[3][:, C1 - 1, :], None, table1d,
                                    bass.IndirectOffsetOnAxis(ap=ends_i[:, 0:1], axis=0)).then_inc(lane_recv_in, 16)
            for slot in range(RING1):
                pool.wait_ge(ix1_ready, slot + 1)
                gather1(slot)
            pool.reg_mov(gather_turn, RING1 + 1)
            pool.reg_mov(free_turn, 1)
            with pool.Fori(0, K1 // RING1 - 1) as it:
                for slot in range(RING1):
                    pool.wait_ge(nodes_ready, 1)
                    pool.wait_ge(ix1_ready, gather_turn)
                    pool.wait_ge(relu_done, free_turn)
                    pool.reg_add(gather_turn, gather_turn, 1)
                    pool.reg_add(free_turn, free_turn, 1)
                    gather1(slot)

            for s in range(RING1):
                pool.wait_ge(rows1_stored[s], 16 * (K1 // RING1 + 1))
            for r in range(2):
                pool.wait_ge(end1_ix_ready, r + 1)
                gather_last(r, rows1, RG1, rg1_in)
            pool.reg_mov(gather_turn, 3)
            with pool.Fori(0, NK // 2 - 1) as it:
                for r in range(2):
                    pool.wait_ge(nodes_ready, 1)
                    pool.wait_ge(end1_ix_ready, gather_turn)
                    pool.reg_add(gather_turn, gather_turn, 1)
                    gather_last(r, rows1, RG1, rg1_in)

        @block.tensor
        def _(pe):
            def mm(out_, lhsT, rhs, start=True, stop=True):
                return pe.matmul(out_, lhsT, rhs, start=start, stop=stop)

            pe.wait_ge(weights_in, 16 * WEIGHT_DMAS_0)
            mm(ps[:, 7, 0:2 * H], wnT2[:, :], acat[:, :]).then_inc(fused_mm, 1)
            pe.wait_ge(fused_in, 1)
            for g, m in enumerate(TABG):
                if g >= 4:
                    pe.wait_ge(tab_out, g - 3)
                for j in range(m):
                    pair = 3 * g + j
                    if pair % (PAIRS // XPARTS) == 0:
                        pe.wait_ge(xT_in[pair // (PAIRS // XPARTS)], 16)
                    last = mm(ps[:, g % 4, j * 2 * ROW:(j + 1) * 2 * ROW], node_wide[:, pair * P:pair * P + P], w0[:, :])
                last.then_inc(tab_mm, 1)
            pe.wait_ge(tab_out, len(TABG))
            with pe.Fori(0, NK // 2) as it:
                for r in range(2):
                    pe.wait_ge(onehot_ready, it * 2 + (r + 1))
                    for b in range(NC):
                        pe.wait_ge(row_free[b % 2], it * (2 * NC) + (r * NC + b // 2 * 2 + 2))
                        for c, w in COLS:
                            o = ps[:, 4 * (b % 2) + c // BANK, 0:w]
                            mm(o, onehot[r][:, b, :], dst_hi[:, c:c + w], True, False)
                            last = mm(o, onehot[r][:, b, :], dst_lo[:, c:c + w], False, True)
                        last.then_inc(row_ready[b % 2], 1)
            for s in range(2):
                pe.wait_ge(row_free[s], NB + 2)
            pe.wait_ge(seg_mm, 1)
            mm(ps[:, 7, 128:256], ones[:, :], below[:, 0, :]).then_inc(fused_mm, 1)
            pe.wait_ge(seg_mm, 2)
            pe.transpose(ps[:, 7, 256:384], same_seg[:, :], ident[:, :]).then_inc(fused_mm, 1)

            def scores(c, par, it2):
                pe.wait_ge(e16_in[par], it2 * 16 + 16)
                pe.wait_ge(edge_mm_free, c + 1)
                for g in range(4):
                    last = mm(ps[:, par, 32 * g:32 * g + 32], edge_terms[par][:, g, :], we_bd[:, :])
                last.then_inc(edge_mm, 1)

            with pe.Fori(0, K0 // 2) as it:
                for par in range(2):
                    scores(it * 2 + par, par, it)
            scores(K0 - 1, 0, K0 // 2)

            for step in range(2):
                pe.wait_ge(carry_ready, step + 1)
                for h in range(H):
                    if step == 0:
                        last = mm(ps[:, 2, h * P:h * P + P], ones[:, :], big_a[:, h, :])
                    else:
                        last = pe.transpose(ps[:, 3, h * P:h * P + P], big_c[:, h, :], ident[:, :])
                last.then_inc(carry_mm, 1)
            pe.wait_ge(carry_ready, 3)
            tail = R0[0][:, C0 - 1, :]
            for h in range(H):
                mm(ps[:, 4, h * HD:h * HD + HD], big_b[:, h, :], tail[:, h * HD:h * HD + HD])
                last = mm(ps[:, 4, ZCOL + h:ZCOL + h + 1], big_b[:, h, :], tail[:, ZCOL + h:ZCOL + h + 1])
            last.then_inc(carry_mm, 1)
            pe.wait_ge(carry_ready, 4)

            def carry(k):
                pe.wait_ge(sel_ready, k + 1)
                pe.wait_ge(cc_ready, k + 1)
                for b in range(NC):
                    last = mm(ps[:, b // 5, (b % 5) * ROW:(b % 5 + 1) * ROW], carry_sel[:, b, :], carry0[:, :])
                last.then_inc(carried, 1)

            def project(k, r, next_carry):
                def turned(g):
                    pe.transpose(ps[:, 2 + (r + g) % 2, 0:P], x1c[r][:, 2 * g:2 * g + 2, :].rearrange("p a b -> p (a b)"),
                                 ident[:, :]).then_inc(x1T_mm, 1)

                pe.wait_ge(x1_ready, k + 1)
                turned(0)
                for g in range(NPC):
                    turn = (r + g) % 2
                    if g + 1 < NPC:
                        turned(g + 1)
                    pe.wait_ge(x1T_ready, k * NPC + (g + 1))
                    pe.wait_ge(pss_out, k * NPC + (g + 1))
                    for j in range(2):
                        last = mm(ps[:, 4 + turn, j * HID:(j + 1) * HID], x1T[turn], w1n[:, j, 0:HID])
                    last.then_inc(send_mm, 1)
                    pe.wait_ge(pds_out, k * NPC + (g + 1))
                    for j in range(2):
                        o = ps[:, 6 + turn, j * RECV:(j + 1) * RECV]
                        mm(o, x1T[turn], w1n[:, j, HID:HID + RECV], True, False)
                        last = mm(o, ones3[:, :], bias_parts[:, :], False, True)
                    last.then_inc(recv_mm, 1)
                    if g == 2 and next_carry:
                        carry(k + 2)

            pe.wait_ge(weights1_in, 16 * WEIGHT_DMAS_1)
            pe.wait_ge(own_term, 2)
            carry(0)
            carry(1)
            with pe.Fori(0, NK // 2 - 1) as it:
                for r in range(2):
                    project(it * 2 + r, r, True)
            for k in (NK - 2, NK - 1):
                project(k, k % 2, False)
            pe.wait_ge(pss_out, NB // 2 + 2)
            pe.wait_ge(pds_out, NB // 2 + 2)

            def edge1(c, s, it):
                pe.wait_ge(e32_in[s], it * 16 + 16)
                pe.wait_ge(pre_ready, c + 1)
                for g in range(2):
                    last = mm(ps[:, 2 * s + g, :], edge_terms[s][:, g, :], w1e_bd[:, :])
                last.then_inc(edge1_mm, 1)

            with pe.Fori(0, K1 // RING1) as it:
                for s in range(RING1):
                    edge1(it * RING1 + s, s, it)

            pe.wait_ge(rows1_ready, K1 + 1)
            pe.wait_ge(pre_ready, K1 + RING1)
            mm(ps[:, 0, 0:P], H1[(K1 - 1) % RING1][:, C1 - 1, :], same_segT[:, :]).then_inc(carry1_mm, 1)
            pe.wait_ge(carry1_cp, 1)
            mm(ps[:, 1, 0:D], rgT[0][:, 0:P], w2[:, :]).then_inc(carry1_mm, 1)
            pe.wait_ge(carry1_cp, 2)

            def node1(k, r, it):
                pe.wait_ge(rg1_in[r], it * (16 * NC) + 16 * NC)
                pe.wait_ge(rgT_ready, k * len(QUADS) + len(QUADS))
                for n, (lo, hi) in enumerate(QUADS):
                    for b in range(lo, hi):
                        last = pe.transpose(ps[:, 4 + n, (b - lo) * P:(b - lo + 1) * P], RG1[r][:, b, :], ident[:, :])
                    last.then_inc(rgT_mm, 1)
                pe.wait_ge(sel1_ready, k + 1)
                pe.wait_ge(agg_used, k + 1)
                for n, (lo, hi) in enumerate(QUADS):
                    pe.wait_ge(rgT_ready, k * len(QUADS) + (n + 1 + len(QUADS)))
                    for b in range(lo, hi):
                        o = ps[:, 2 * r + b // 5, (b % 5) * D:(b % 5 + 1) * D]
                        mm(o, rgT[n][:, (b - lo) * P:(b - lo + 1) * P], w2[:, :], True, False)
                        last = mm(o, carry_sel[:, b, :], carry1[:, :], False, True)
                last.then_inc(agg_mm, 1)

            with pe.Fori(0, NK // 2) as it:
                for r in range(2):
                    node1(it * 2 + r, r, it)

        @block.scalar
        def _(act):
            def ix_copy(slot, cols, width, ready):
                act.activation(ix[slot][:, 0:width], src_idx[:, cols], ACT.Copy).then_inc(ready, 1)

            for s in range(2):
                act.sem_inc(row_free[s], 1)
            act.sem_inc(pss_out, 2)
            act.sem_inc(cc_ready, 1)
            act.wait_ge(src_in, 16)
            for slot in range(RING0):
                ix_copy(slot, slice(slot * C0, slot * C0 + C0), C0, ix0_ready)

            act.wait_ge(ends_ready, 1)
            rows = [ps[:, 4 * i:4 * i + 4, :].rearrange("p a b -> p (a b)") for i in range(2)]
            with act.Fori(0, NB // 2) as j:
                for i in range(2):
                    act.wait_ge(row_ready[i], j + 1)
                    act.activation(junk_a[i][:, 0:HIGH], rows[i][:, BANK:LANE + 1], ACT.Sign, bias=node_half[:, bass.ds(j * 2 + i, 1)],
                                   scale=-1.0, accum_out=sign_sum[:, bass.ds(j * 2 + i, 1)]).then_inc(row_free[i], 1)

            def turn0(c, slot, copies):
                act.wait_ge(expo_ready, c + 1)
                act.activation(wq[:, :, :], expo[:, :, :], ACT.Exp).then_inc(wq_ready, 1)
                if copies:
                    ix_copy(slot, bass.ds(c * C0 + RING0 * C0, C0), C0, ix0_ready)

            with act.Fori(0, (K0 - 5) // RING0) as it:
                for slot in range(RING0):
                    turn0(it * RING0 + slot, slot, True)
            for c in range(K0 - 5, K0):
                turn0(c, c % RING0, c + RING0 < K0)

            for slot in range(RING1):
                ix_copy(slot, slice(slot * C1, slot * C1 + C1), C1, ix1_ready)
            act.wait_ge(carry_exp, 1)
            act.activation(big_c, big_b, ACT.Exp).then_inc(carry_exp, 1)

            def root(turn, variance, std):
                act.wait_ge(variance, turn + 1)
                act.activation(rstd, var, ACT.Sqrt, bias=eps[:, 0:1], scale=1.0 / D).then_inc(std, 1)

            def carries_out(k):
                act.wait_ge(carried, k + 1)
                act.wait_ge(cc_free, k + 1)
                act.activation(cc.rearrange("p (a b) c -> p a (b c)", a=2), ps[:, 0:2, 0:5 * ROW], ACT.Copy).then_inc(cc_ready, 1)

            def project(k, r, pairs):
                def transposed(g):
                    turn = (r + g) % 2
                    act.wait_ge(x1T_mm, k * NPC + (g + 1 + NPC))
                    act.activation(x1T[turn], ps[:, 2 + turn, 0:P], ACT.Copy).then_inc(x1T_ready, 1)

                for g in pairs:
                    turn = (r + g) % 2
                    pair = slice(2 * g, 2 * g + 2)
                    if g == 0:
                        transposed(0)
                    if g + 1 < NPC:
                        transposed(g + 1)
                    act.wait_ge(send_mm, k * NPC + (g + 1))
                    act.activation(PSs[r][:, pair, :].rearrange("p b f -> p (b f)"), ps[:, 4 + turn, 0:2 * HID],
                                   ACT.Copy).then_inc(pss_out, 1)
                    bank = ps[:, 6 + turn, 0:2 * RECV].rearrange("p (b f) -> p b f", f=RECV)
                    act.wait_ge(recv_mm, k * NPC + (g + 1))
                    act.activation(PDs[r][:, pair, :], bank[:, :, 0:HID], ACT.Copy)
                    act.activation(node_wide[:, bass.ds(k * (NC * D) + 2 * g * D, 2 * D)].rearrange("p (b f) -> p b f", f=D),
                                   bank[:, :, HID:RECV], ACT.Copy).then_inc(pds_out, 1)

            def slots(k, r, it):
                act.wait_ge(pss_stored[r], it * 16 + 16)
                act.wait_ge(pds_stored[r], it * 16 + 16)
                act.wait_ge(pds_scattered[r], it * (16 * NC) + 16)
                act.reg_add(spare, spare, 1)
                act.activation(start_ix[r][:, :], start_idx[:, bass.ds(k * NC, NC)], ACT.Copy).then_inc(start_ix_ready, 1)

            def turn(k, r, it, last=False):
                act.wait_ge(e8_ready, k + 1)
                act.activation(f8, e8, ACT.Exp).then_inc(f8_ready, 1)
                if r is not None:
                    slots(k - 1, r, it)
                    project(k - 1, r, (0, 1, 2))
                root(k * 2, var_ready, std_ready)
                if not last:
                    carries_out(k + 1)
                if r is not None:
                    project(k - 1, r, (3, 4))
                root(k * 2 + 1, var_ready, std_ready)

            spare = act.alloc_register("spare")
            act.reg_mov(spare, 0)
            carries_out(0)
            turn(0, None, None)
            with act.Fori(0, NK // 2 - 1) as it:
                for r in range(2):
                    turn(it * 2 + (r + 1), r, it)
            turn(NK - 1, 0, NK // 2 - 1, last=True)
            slots(NK - 1, 1, NK // 2 - 1)
            project(NK - 1, 1, range(NPC))

            def turn1(c, s, it, copies):
                act.wait_ge(rows1_stored[s], it * 16 + 16)
                act.wait_ge(pre_ready, c + (1 + RING1))
                act.activation(H1[s], G1[s], ACT.Relu).then_inc(relu_done, 1)
                if copies:
                    ix_copy(s, bass.ds(c * C1 + RING1 * C1, C1), C1, ix1_ready)

            with act.Fori(0, K1 // RING1 - 1) as it:
                for s in range(RING1):
                    turn1(it * RING1 + s, s, it, True)
            for c in range(K1 - RING1, K1):
                turn1(c, c % RING1, c // RING1, False)

            def turned(k, r):
                for n, (lo, hi) in enumerate(QUADS):
                    act.wait_ge(rgT_mm, k * len(QUADS) + (n + 1))
                    act.activation(rgT[n][:, 0:(hi - lo) * P], ps[:, 4 + n, 0:(hi - lo) * P], ACT.Copy).then_inc(rgT_ready, 1)
                act.activation(end_ix[r][:, :], end_idx[:, bass.ds(k * NC + 2 * NC, NC)], ACT.Copy).then_inc(end1_ix_ready, 1)

            act.wait_ge(carry1_cp, 2)
            turned(0, 0)
            with act.Fori(0, NK // 2 - 1) as it:
                for r in range(2):
                    turned(it * 2 + (r + 1), 1 - r)
                    root(it * 2 + r, var1_ready, std1_ready)
            turned(NK - 1, 1)
            root(NK - 2, var1_ready, std1_ready)
            root(NK - 1, var1_ready, std1_ready)

        @block.vector
        def _(dve):
            done = [0]

            def link(ins):
                done[0] += 1
                ins.then_inc(dv, 1)
                dve.wait_ge(dv, done[0])

            tt, ts, stt, scan = dve.tensor_tensor, dve.tensor_scalar, dve.scalar_tensor_tensor, dve.tensor_tensor_scan
            for s in range(2):
                dve.sem_inc(row_free[s], 1)
            dve.sem_inc(edge_mm_free, 2)
            dve.sem_inc(pds_out, 2)
            dve.sem_inc(cc_free, 1)
            dve.sem_inc(pre_ready, RING1)
            dve.sem_inc(agg_used, 2)
            dve.sem_inc(x1T_mm, NPC)
            dve.sem_inc(rgT_ready, len(QUADS))
            dve.memset(end_idx[:, NB:NB + 2 * NC], 0)
            dve.memset(R0[1][:, C0 - 1, :], 0.0).then_inc(rows0_ready, 1)

            dve.wait_ge(fused_mm, 1)
            dve.tensor_copy(w0[0:D, D:ROW], ps[0:D, 7, 0:2 * H])
            dve.tensor_copy(w0[D:2 * D, ROW + D:2 * ROW], ps[D:2 * D, 7, 0:2 * H]).then_inc(fused_in, 1)
            for g, m in enumerate(TABG):
                dve.wait_ge(tab_mm, g + 1)
                if g >= TABS:
                    dve.wait_ge(tab_st[g % TABS], 16 * (g // TABS))
                bank = ps[:, g % 4, 0:2 * m * ROW].rearrange("p (b c) -> p b c", c=ROW)
                dve.tensor_copy(a_dst[:, 6 * g:6 * g + 2 * m, :], bank[:, :, MCOL:ROW])
                dve.tensor_copy(tab0[g % TABS][:, 0:2 * m, :], bank).then_inc(tab_out, 1)

            dve.wait_ge(dst_in, 16)
            dve.wait_ge(nexts_in, 32)
            dve.wait_ge(consts, 1)
            dve.tensor_copy(ends_i[:, 0:1], dst_i[:, 0:1])
            link(dve.tensor_copy(ends_i[:, 3:4], dst_i[:, LANE - 1:LANE]))
            dve.tensor_copy(ends[:, 0:4], ends_i[:, :])
            link(dve.tensor_copy(ends[:, 4:5], ends_i[:, 0:1]))
            link(dve.memset(ends[0:1, 4:5], -1.0))
            link(tt(ends[:, 5:6], ends[:, 0:1], ends[:, 1:2], ALU.is_equal))
            link(stt(ends[:, 5:6], ends[:, 5:6], float(4 * NP), ends[:, 0:1], ALU.mult, ALU.add))
            for table, col in ((firsts, 5), (nexts, 1), (lows, 4)):
                ts(table[:, :], k10[:, :], ends[:, col:col + 1], -1.0, ALU.subtract, ALU.mult)
            link(ts(split_i, dst_i, 0xFF, None, ALU.bitwise_and))
            link(dve.tensor_copy(dst_lo[:, 1:LANE + 1], split_i))
            link(ts(split_i, dst_i, 0xFF00, None, ALU.bitwise_and))
            dve.tensor_copy(dst_hi[:, 1:LANE + 1], split_i)
            link(ts(node_half[:, :], node_id[:, :], 0.5, None, ALU.add))

            dve.sem_inc(ends_ready, 1)

            def not_before(k):
                return ts(below[:, :, :], iota_q[:, :, :], lows[:, k], None, ALU.is_ge)

            def lanes_hot(k, r):
                stt(onehot[r], iota_q[:, :, :], nexts[:, k], below[:, :, :], ALU.is_lt, ALU.mult).then_inc(onehot_ready, 1)

            link(not_before(slice(0, 1)))
            lanes_hot(slice(0, 1), 0)

            rows = [ps[:, 4 * i, :] for i in range(2)]
            STEPSC = 6

            with dve.Fori(0, NK // 2) as it:
                for r in range(2):
                    n = [0]

                    def step(ins):
                        n[0] += 1
                        ins.then_inc(dvc, 1)
                        dve.wait_ge(dvc, it * (2 * STEPSC) + (r * STEPSC + n[0]))

                    for b in range(NC):
                        if b == 1:
                            dve.wait_ge(onehot_ready, it * 2 + (r + 1))
                            step(not_before(bass.ds(it * 2 + (r + 1), 1)))
                        if b == 4:
                            lanes_hot(bass.ds(it * 2 + (r + 1), 1), 1 - r)
                        col = it * (2 * NC) + (r * NC + b)
                        dve.wait_ge(row_ready[b % 2], it * NC + (r * NC // 2 + b // 2 + 1))
                        ts(junk_v[b % 2][:, 0:LOW], rows[b % 2][:, 1:BANK], node_id[:, bass.ds(col, 1)], 0.0, ALU.is_le, ALU.add,
                           accum_out=upto[:, bass.ds(col + 1, 1)])
                        ts(row_base[:, bass.ds(col, 1)], rows[b % 2][:, 0:1], float(LANE), HIGH / 2, ALU.mult,
                           ALU.add).then_inc(row_free[b % 2], 1)
                    for i in range(2):
                        dve.wait_ge(row_free[i], it * (2 * NC) + (r * NC + NC + 2))
                    counts = upto[:, bass.ds(it * (2 * NC) + (r * NC + 1), NC)]
                    before = upto[:, bass.ds(it * (2 * NC) + r * NC, NC)]
                    chunk_cols = bass.ds(it * (2 * NC) + r * NC, NC)
                    step(stt(counts, sign_sum[:, chunk_cols], 0.5, counts, ALU.mult, ALU.add))
                    step(tt(counts, counts, row_base[:, chunk_cols], ALU.add))
                    t10 = tmp_nb[:, 0:NC]
                    step(tt(t10, counts, before, ALU.subtract))
                    step(ts(t10, t10, 1.0, None, ALU.min))
                    step(ts(t10, t10, -float(NOWHERE), float(NOWHERE), ALU.mult, ALU.add))
                    tt(start_idx[:, bass.ds(it * (2 * NC) + r * NC, NC)], t10, before, ALU.add).then_inc(starts_ready, 1)
                    assert n[0] == STEPSC

            dve.wait_ge(starts_ready, NK)
            link(ts(tmp_nb[:, :], upto[:, 1:NB + 1], 1.0, 0.0, ALU.subtract, ALU.max))
            dve.tensor_copy(end_idx[:, 0:NB], tmp_nb[:, :]).then_inc(upto_ready, 1)
            dve.wait_ge(upto_ready, 1)
            dve.wait_ge(wraps_in, 16)
            link(tt(degree[:, :], upto[:, 1:NB + 1], upto[:, 0:NB], ALU.subtract))
            link(ts(has[:, :], degree[:, :], 1.0, None, ALU.min))
            link(ts(degree[:, :], degree[:, :], 1.0, None, ALU.max))
            link(dve.reciprocal(inv_deg[:, :], degree[:, :]))
            link(tt(inv_deg[:, :], inv_deg[:, :], has[:, :], ALU.mult))
            link(ts(tmp_nb[:, :], has[:, :], -float(NOWHERE), float(NOWHERE), ALU.mult, ALU.add))
            link(tt(tmp_nb[:, :], tmp_nb[:, :], upto[:, 0:NB], ALU.add))
            link(dve.tensor_copy(start_idx[:, 0:1], tmp_nb[:, 0:1]))
            dve.tensor_copy(end_ix[0][:, :], end_idx[:, 0:NC])
            link(dve.tensor_copy(end_ix[1][:, :], end_idx[:, NC:2 * NC]))
            dve.sem_inc(nodes_ready, 1)
            dve.sem_inc(end_ix_ready, 2)

            dve.wait_ge(onehot_ready, NK + 1)
            link(tt(same[:, 1:LANE], dst_i[:, 1:LANE], dst_i[:, 0:LANE - 1], ALU.is_equal))
            link(tt(same[:, 0:1], ends[:, 0:1], ends[:, 2:3], ALU.is_equal))
            ts(below[:, 0, :], ident[:, :], ends[:, 3:4], None, ALU.mult).then_inc(seg_mm, 1)
            dve.wait_ge(fused_mm, 2)
            stt(same_seg[:, :], ps[:, 7, 128:256], ends[:, 0:1], earlier[:, :], ALU.is_equal, ALU.mult).then_inc(seg_mm, 1)
            dve.wait_ge(fused_mm, 3)
            dve.tensor_copy(same_segT[:, :], ps[:, 7, 256:384]).then_inc(seg_mm, 1)

            dve.wait_ge(weights1_in, 16 * WEIGHT_DMAS_1)
            for j in range(2):
                own = w1n[D * j:D * j + D, j, 2 * HID:2 * HID + D]
                last = tt(own, own, ident[D * j:D * j + D, D * j:D * j + D], ALU.add)
            last.then_inc(own_term, 1)
            hi, mid = bias_part[:, 0, :], bias_part[:, 1, :]
            mine = [ident[0:3, i:i + 1] for i in range(3)]
            dve.memset(ones3[:, :], 1.0)
            link(dve.tensor_copy(hi, bias[:, :]))
            ts(bias_sum[:, :], hi, mine[0], None, ALU.mult)
            link(tt(bias_rest[:, :], bias[:, :], hi, ALU.subtract))
            link(dve.tensor_copy(mid, bias_rest[:, :]))
            link(stt(bias_sum[:, :], mid, mine[1], bias_sum[:, :], ALU.mult, ALU.add))
            link(tt(bias_rest[:, :], bias_rest[:, :], mid, ALU.subtract))
            stt(bias_parts[:, :], bias_rest[:, :], mine[2], bias_sum[:, :], ALU.mult, ALU.add).then_inc(own_term, 1)

            terms = node_wide[:, 0:LANE * H].rearrange("p (t h) -> p t h", h=H)
            dve.wait_ge(terms_in, 16)
            dve.wait_ge(lane_terms_in, 16)
            for h in range(H):
                last = scan(terms[:, :, h], same[:, :], terms[:, :, h], lane_rows[:, MCOL + h:MCOL + h + 1], ALU.mult, ALU.add)
            link(last)
            dve.wait_ge(rows0_ready, 1)

            def wide(ap, shape):
                return ap.to_broadcast(shape)

            def turn0(c, slot, it):
                par = slot % 2
                G, R, before = G0[slot], R0[par], R0[1 - par][:, C0 - 1, :]
                same_c = same[:, bass.ds(c * C0, C0)]
                M = R[:, :, MCOL:ROW]
                dve.wait_ge(gathered0[slot], it * (16 * C0) + 16 * C0)
                tt(score[:, :, :], G[:, :, D:D + H], terms[:, bass.ds(c * C0, C0), :], ALU.add).then_inc(dv0, 1)
                dve.wait_ge(dv0, c * 4 + 1)
                dve.wait_ge(edge_mm, c + 1)
                tt(score[:, :, :], score[:, :, :], ps[:, par, 0:C0 * H].rearrange("p (t h) -> p t h", h=H), ALU.add).then_inc(edge_mm_free, 1)
                dve.wait_ge(edge_mm_free, c + 3)
                stt(score[:, :, :], score[:, :, :], SLOPE, score[:, :, :], ALU.mult, ALU.max).then_inc(dv0, 1)
                dve.wait_ge(dv0, c * 4 + 2)
                dve.wait_ge(rows0_stored[par], it * 32 + (16 * (slot // 2) + 16))
                for h in range(H):
                    last = scan(R[:, :, MCOL + h], same_c, score[:, :, h], before[:, MCOL + h:MCOL + h + 1], ALU.mult, ALU.max)
                last.then_inc(dv0, 1)
                dve.wait_ge(dv0, c * 4 + 3)
                tt(expo[:, :, 0:H], score[:, :, :], M, ALU.subtract)
                tt(expo[:, 1:C0, H:2 * H], M[:, 0:C0 - 1, :], M[:, 1:C0, :], ALU.subtract)
                tt(expo[:, 0, H:2 * H], before[:, MCOL:ROW], M[:, 0, :], ALU.subtract).then_inc(expo_ready, 1)
                dve.wait_ge(wq_ready, c + 1)
                tt(wq[:, :, H:2 * H], wq[:, :, H:2 * H], wide(same_c.unsqueeze(2), [P, C0, H]), ALU.mult)
                feats = G[:, :, 0:D].rearrange("p t (h d) -> p t h d", d=HD)
                tt(feats, feats, wide(wq[:, :, 0:H].unsqueeze(3), [P, C0, H, HD]), ALU.mult).then_inc(dv0, 1)
                dve.wait_ge(dv0, c * 4 + 4)
                dve.wait_ge(rows0_ready, c + 1)
                for f in range(D):
                    scan(R[:, :, f], wq[:, :, H + f // HD], G[:, :, f], before[:, f:f + 1], ALU.mult, ALU.add)
                for h in range(H):
                    last = scan(R[:, :, ZCOL + h], wq[:, :, H + h], wq[:, :, h], before[:, ZCOL + h:ZCOL + h + 1], ALU.mult, ALU.add)
                last.then_inc(rows0_ready, 1)

            with dve.Fori(0, K0 // RING0) as it:
                for slot in range(RING0):
                    turn0(it * RING0 + slot, slot, it)
            turn0(K0 - 1, 0, K0 // RING0)

            dve.wait_ge(rows0_ready, K0 + 1)
            tail = R0[0][:, C0 - 1, :]
            for h in range(H):
                last = ts(big_a[:, h, :], ident[:, :], tail[:, MCOL + h:MCOL + h + 1], None, ALU.mult)
            last.then_inc(carry_ready, 1)
            dve.wait_ge(carry_mm, 1)
            seg4 = wide(same_seg[:, :].unsqueeze(1), [P, H, P])
            link(tt(big_a, ps[:, 2, :].rearrange("p (h l) -> p h l", l=P), seg4, ALU.mult))
            link(dve.tensor_reduce(mc, big_a, AX.X, ALU.max))
            tt(big_b, big_a, wide(mc.unsqueeze(2), [P, H, P]), ALU.subtract).then_inc(carry_exp, 1)
            dve.wait_ge(carry_exp, 2)
            tt(big_c, big_c, seg4, ALU.mult).then_inc(carry_ready, 1)
            dve.wait_ge(carry_mm, 2)
            dve.tensor_copy(big_b.rearrange("p h l -> p (h l)"), ps[:, 3, :]).then_inc(carry_ready, 1)
            dve.wait_ge(carry_mm, 3)
            dve.tensor_copy(carry0[:, 0:MCOL], ps[:, 4, 0:MCOL])
            dve.tensor_copy(carry0[:, MCOL:ROW], mc).then_inc(carry_ready, 1)

            def choose(k, ready):
                ts(carry_sel[:, :, :], iota_q[:, :, :], firsts[:, bass.ds(k, 1)], None, ALU.is_equal).then_inc(ready, 1)

            def norm(chain, turn, variance, std):
                chain(dve.tensor_reduce(mu, ya, AX.X, ALU.add))
                chain(ts(mu, mu, 1.0 / D, None, ALU.mult))
                chain(tt(ya, ya, wide(mu.unsqueeze(2), [P, NC, D]), ALU.subtract))
                chain(tt(sq, ya, ya, ALU.mult))
                dve.tensor_reduce(var, sq, AX.X, ALU.add).then_inc(variance, 1)
                dve.wait_ge(std, turn + 1)
                chain(dve.reciprocal(rstd, rstd))

            def chained(sem_, start, steps):
                n = [0]

                def chain(ins):
                    n[0] += 1
                    ins.then_inc(sem_, 1)
                    dve.wait_ge(sem_, start + n[0])

                def end():
                    assert n[0] == steps, n[0]
                return chain, end

            STEPS0 = 24

            def node0(k, r, it, first=False, more=True):
                chain, end = chained(dvn, k * STEPS0, STEPS0)
                RG, x1 = RG0[r], x1c[r]
                if more:
                    dve.wait_ge(carried, k + 1)
                    choose(k + 1, sel_ready)
                dve.wait_ge(rg0_in[r], it * (16 * NC) + 16 * NC)
                dve.wait_ge(cc_ready, k + 2)
                dve.wait_ge(xh_in[r], it * 32 + 32)
                chain(tt(z1, RG[:, :, MCOL:ROW], cc[:, :, MCOL:ROW], ALU.max))
                tt(e8[:, :, 0:H], RG[:, :, MCOL:ROW], z1, ALU.subtract)
                tt(e8[:, :, H:2 * H], cc[:, :, MCOL:ROW], z1, ALU.subtract).then_inc(e8_ready, 1)
                dve.wait_ge(f8_ready, k + 1)
                tt(z1, RG[:, :, ZCOL:MCOL], f8[:, :, 0:H], ALU.mult)
                chain(tt(z2, cc[:, :, ZCOL:MCOL], f8[:, :, H:2 * H], ALU.mult))
                chain(tt(z1, z1, z2, ALU.add))
                chain(ts(z1, z1, EPS_SOFTMAX, None, ALU.add))
                chain(dve.reciprocal(z1, z1))
                chain(tt(z1, z1, wide(has[:, bass.ds(k * NC, NC)].unsqueeze(2), [P, NC, H]), ALU.mult))
                for i in range(2):
                    last = tt(e8[:, :, H * i:H * i + H], f8[:, :, H * i:H * i + H], z1, ALU.mult)
                chain(last)
                heads = lambda a: a.rearrange("p b (h d) -> p b h d", d=HD)
                tt(heads(ya), heads(RG[:, :, 0:D]), wide(e8[:, :, 0:H].unsqueeze(3), [P, NC, H, HD]), ALU.mult)
                chain(tt(heads(sq), heads(cc[:, :, 0:D]), wide(e8[:, :, H:2 * H].unsqueeze(3), [P, NC, H, HD]), ALU.mult))
                dve.sem_inc(cc_free, 1)
                ts(end_ix[r][:, :], end_idx[:, bass.ds(k * NC + 2 * NC, NC)], 1.0, None, ALU.mult).then_inc(end_ix_ready, 1)
                chain(tt(ya, ya, sq, ALU.add))
                chain(tt(ya, ya, hc[r][:, :, 0:D], ALU.add))
                norm(chain, k * 2, var_ready, std_ready)
                chain(tt(ya, ya, wide(rstd.unsqueeze(2), [P, NC, D]), ALU.mult))
                chain(tt(ya, ya, wide(row_bc[:, 0:1, :], [P, NC, D]), ALU.mult))
                chain(tt(ya, ya, wide(row_bc[:, 1:2, :], [P, NC, D]), ALU.add))
                chain(tt(ya, ya, xc[r], ALU.add))
                dve.sem_inc(node0_used, 1)
                norm(chain, k * 2 + 1, var_ready, std_ready)
                if not first:
                    dve.wait_ge(x1T_mm, k * NPC)
                tt(x1, ya, wide(rstd.unsqueeze(2), [P, NC, D]), ALU.mult).then_inc(x1_ready, 1)
                end()

            choose(0, sel_ready)
            node0(0, 0, 0, first=True)
            with dve.Fori(0, NK // 2 - 1) as it:
                for r in range(2):
                    node0(it * 2 + (r + 1), 1 - r, it + r)
            node0(NK - 1, 1, NK // 2 - 1, more=False)

            dve.wait_ge(pds_out, NB // 2 + 2)
            for r in range(2):
                dve.wait_ge(pss_stored[r], 16 * (NK // 2 + 1))
            own = node_wide[:, :].rearrange("p (b d) -> p b d", d=D)
            link(tt(b2_part, wide(has[:, :].unsqueeze(2), [P, NB, D]), wide(row_bc[:, 2:3, :], [P, NB, D]), ALU.mult))
            link(tt(own, own, b2_part, ALU.add))

            link(dve.memset(H1[RING1 - 1][:, C1 - 1, :], 0.0))
            dve.sem_inc(rows1_ready, 1)
            dve.wait_ge(lane_recv_in, 16)

            HOLDS, STEPS1 = C1, 2 * C1 - 1

            def turn1(c, s, it, start, first=False, final=False):
                X, Xb = X1[s], X1[(s - 1) % RING1]
                Hc, Hb = H1[(s - 1) % RING1], H1[(s - 2) % RING1]
                if not final:
                    dve.wait_ge(recv_in[s], it * 16 + 16)
                if not first:
                    dve.wait_ge(relu_done, c)
                    dve.wait_ge(rows1_ready, c)
                n = 0
                for u in range(C1):
                    if not final:
                        if u:
                            dve.wait_ge(dv1, start + (n - (0 if first else 1)))
                        stt(X[:, u, :], X[:, u - 1, :] if u else Xb[:, C1 - 1, :], same[:, bass.ds(c * C1 + u, 1)],
                            X[:, u, :], ALU.mult, ALU.add).then_inc(dv1, 1)
                        n += 1
                    if not first:
                        if u:
                            dve.wait_ge(dv1, start + (n - (0 if final else 1)))
                        a = stt(Hc[:, u, :], Hc[:, u - 1, :] if u else Hb[:, C1 - 1, :], same[:, bass.ds(c * C1 - C1 + u, 1)],
                                Hc[:, u, :], ALU.mult, ALU.add)
                        if u < C1 - 1:
                            a.then_inc(dv1, 1)
                            n += 1
                        else:
                            a.then_inc(rows1_ready, 1)
                if final:
                    return
                assert n == (HOLDS if first else STEPS1)
                dve.wait_ge(dv1, start + n)
                dve.wait_ge(gathered1[s], it * (16 * C1) + 16 * C1)
                tt(G1[s], G1[s], X, ALU.add).then_inc(recv_used, 1)
                dve.wait_ge(recv_used, c + 1)
                dve.wait_ge(edge1_mm, c + 1)
                for g in range(2):
                    part_g = G1[s][:, G1E * g:G1E * g + G1E, :].rearrange("p t f -> p (t f)")
                    last = tt(part_g, part_g, ps[:, 2 * s + g, :], ALU.add)
                last.then_inc(pre_ready, 1)

            turn1(0, 0, 0, 0, first=True)
            with dve.Fori(0, K1 // RING1 - 1) as it:
                for i in range(RING1):
                    c = it * RING1 + (i + 1)
                    turn1(c, (i + 1) % RING1, it + (i + 1) // RING1, it * (RING1 * STEPS1) + (HOLDS + i * STEPS1))
            for c in range(K1 - RING1 + 1, K1):
                turn1(c, c % RING1, c // RING1, HOLDS + (c - 1) * STEPS1)
            turn1(K1, K1 % RING1, K1 // RING1, HOLDS + (K1 - 1) * STEPS1, final=True)

            dve.wait_ge(rg0_in[0], 16 * NB // 2)
            dve.wait_ge(rg0_in[1], 16 * NB // 2)
            dve.tensor_copy(end_ix[0][:, :], end_idx[:, 0:NC])
            link(dve.tensor_copy(end_ix[1][:, :], end_idx[:, NC:2 * NC]))
            dve.sem_inc(end1_ix_ready, 2)
            dve.wait_ge(carry1_mm, 1)
            dve.tensor_copy(rgT[0][:, 0:P], ps[:, 0, 0:P]).then_inc(carry1_cp, 1)
            dve.wait_ge(carry1_mm, 2)
            dve.tensor_copy(carry1[:, :], ps[:, 1, 0:D]).then_inc(carry1_cp, 1)

            STEPS2 = 7

            def node1(k, r, it, more=True):
                chain, end = chained(dvf, k * STEPS2, STEPS2)
                five = lambda a: a.rearrange("p (a b) d -> p a b d", b=5)
                dve.wait_ge(agg_mm, k + 1)
                if more:
                    choose(k + 1, sel1_ready)
                chain(tt(five(ya), ps[:, 2 * r:2 * r + 2, 0:5 * D].rearrange("p a (b d) -> p a b d", d=D),
                         wide(inv_deg[:, bass.ds(k * NC, NC)].rearrange("p (a b) -> p a b", b=5).unsqueeze(3), [P, 2, 5, D]), ALU.mult))
                dve.sem_inc(agg_used, 1)
                chain(tt(ya, ya, node_wide[:, bass.ds(k * (NC * D), NC * D)].rearrange("p (b d) -> p b d", d=D), ALU.add))
                norm(chain, k, var1_ready, std1_ready)
                dve.wait_ge(fin_stored[r], it * 16 + 16)
                tt(fin[r], ya, wide(rstd.unsqueeze(2), [P, NC, D]), ALU.mult).then_inc(fin_ready, 1)
                dve.wait_ge(fin_ready, k + 1)
                end()

            choose(0, sel1_ready)
            with dve.Fori(0, NK // 2 - 1) as it:
                for r in range(2):
                    node1(it * 2 + r, r, it)
            node1(NK - 2, 0, NK // 2 - 1)
            node1(NK - 1, 1, NK // 2 - 1, more=False)


def kernel(**inputs):
    import numpy as np
    import concourse.bacc as bacc
    from concourse.bass_utils import run_bass_kernel_spmd

    a = {k: np.ascontiguousarray(v) for k, v in inputs.items()}
    xp = np.concatenate([a["x"], np.zeros((NP - N, D), a["x"].dtype)])
    lanes = lambda v, fill: np.concatenate([v, np.full((NE - E,) + v.shape[1:], fill, v.dtype)])

    def grouped(v, per):
        f = v.shape[1]
        v = lanes(v, 0).reshape(P, LANE // per, per, f)
        return np.ascontiguousarray(v.transpose(2, 3, 1, 0).reshape(per * f, LANE // per, P))

    def placed(shape, blocks):
        m = np.zeros(shape, blocks[0][2].dtype)
        for row, col, v in blocks:
            m[row:row + v.shape[0], col:col + v.shape[1]] = v
        return m

    W1 = a["L1_gnn_W1"]
    arrays = {
        "x_d": xp,
        "xT2_d": np.ascontiguousarray(xp.reshape(P, NB // 2, 2, D).transpose(2, 3, 1, 0).reshape(2 * D, NB // 2 * P)),
        "src_d": lanes(a["src"], 0).reshape(P, LANE),
        "dst_d": lanes(a["dst"], N).reshape(P, LANE),
        "e16g_d": grouped(a["edge_attr_16"], G0E),
        "e32g_d": grouped(a["edge_attr_32"], G1E),
        "W_node2_d": placed((2 * D, 2 * ROW), [(j * D, j * ROW, a["L0_gnn_W_node"]) for j in range(2)]),
        "W_nodeT2_d": np.ascontiguousarray(np.tile(a["L0_gnn_W_node"].T, (1, 2))),
        "attn2_d": placed((D, 2 * H), [(h * HD, i * H + h, a[n][h][:, None]) for i, n in
                                       enumerate(("L0_gnn_attn_src", "L0_gnn_attn_dst")) for h in range(H)]),
        "W_edge_bd_d": placed((P, G0E * H), [(j * F16, j * H, a["L0_gnn_W_edge"]) for j in range(G0E)]),
        "W1e_bd_d": placed((P, G1E * HID), [(j * F32E, j * HID, W1[2 * D:]) for j in range(G1E)]),
        "W1n_d": placed((P, 2 * (HID + RECV)), [(j * D, j * (HID + RECV), np.concatenate(
            [W1[0:D], W1[D:2 * D], a["L1_gnn_Wn"]], axis=1)) for j in range(2)]).reshape(P, 2, HID + RECV),
    }
    for name in ("L0_gnn_ln_gamma", "L0_gnn_ln_beta", "L1_gnn_b1", "L1_gnn_W2", "L1_gnn_b2", "L1_gnn_bn"):
        arrays[name + "_d"] = a[name]
    nc = bacc.Bacc("TRN2", target_bir_lowering=False, num_devices=1)
    args = [nc.dram_tensor(n, v.shape, mybir.dt.from_np(v.dtype), kind="ExternalInput").ap() for n, v in arrays.items()]
    args.append(nc.dram_tensor("out_d", (N, D), F32, kind="ExternalOutput").ap())
    build(nc, *args)
    return run_bass_kernel_spmd(nc, [arrays], core_ids=[0]).results[0]["out_d"]
```
